# Optimizing a Trainium2 kernel written in Bass

```python
import numpy as np
import jax
import jax.numpy as jnp

def _softmax(x, axis=-1):
    return jax.nn.softmax(x, axis=axis)

def _gelu(x):
    return jax.nn.gelu(x, approximate=True)

def _silu(x):
    return jax.nn.silu(x)

def _sigmoid(x):
    return jax.nn.sigmoid(x)

def _layernorm(x, axis=-1, eps=1e-05):
    m = jnp.mean(x, axis=axis, keepdims=True)
    v = jnp.var(x, axis=axis, keepdims=True)
    return (x - m) / jnp.sqrt(v + eps)

def _scatter_add(tgt, idx, src, axis=0):
    return tgt.at[idx].add(src)

def _segment_sum(src, seg, n):
    return jax.ops.segment_sum(src, seg, n)
kernel_name = 'mk_flamingo_gated_d2_seqx_r4_fcfd9d'

def setup_inputs(seed: int=0):
    np.random.seed(seed)
    _w = jnp.asarray

    def _rec_inputs():
        import jax
        import jax.numpy as jnp
        _rk = jax.random.key(seed)
        x = -0.0002928 + 1 * jax.random.normal(jax.random.fold_in(_rk, 1), (32, 128, 256), jnp.float32)
        _lenS = 128 - jax.random.randint(jax.random.fold_in(_rk, 7), (32,), 0, max(1, 128 // 4) + 1, jnp.int32)
        _lenS2 = 128 - jax.random.randint(jax.random.fold_in(_rk, 8), (32,), 0, max(1, 128 // 4) + 1, jnp.int32)
        _ctx_1024P = jax.random.normal(jax.random.fold_in(_rk, 11), (32, 16, 256), jnp.float32)
        _ctx_1024c = jax.random.dirichlet(jax.random.fold_in(_rk, 511), 0.3 * jnp.ones((16,), jnp.float32), (32, 128))
        _ctx_1024t = jnp.einsum('bsk,bkd->bsd', _ctx_1024c, _ctx_1024P)
        _ctx_1024t = _ctx_1024t * jax.lax.rsqrt(jnp.mean(jnp.square(_ctx_1024t)) + 1e-12) * 0.953939
        ctx_1024 = -1.39393e-06 + 0.999914 * (_ctx_1024t + 0.3 * jax.random.normal(jax.random.fold_in(_rk, 611), (32, 128, 256), jnp.float32))
        fside_SxS2_0 = 0.000376506 + 0.999991 * jax.random.normal(jax.random.fold_in(_rk, 12), (128, 128), jnp.float32)
        _g = jax.random.normal(jax.random.fold_in(_rk, 9001), (2, 2), jnp.float32)
        _g = jnp.sign(_g) * jnp.maximum(jnp.abs(_g), 1.0) + (_g == 0) * 1.0
        g_xattn = _g[0]
        g_ffn = _g[1]
        return (x, ctx_1024, fside_SxS2_0, g_xattn, g_ffn)
    x, ctx_1024, fside_SxS2_0, g_xattn, g_ffn = _rec_inputs()

    def _L0_xattn_setup():
        import jax, jax.numpy as jnp
        import numpy as np
        D_MODEL, D_HEAD, N_HEAD = (256, 64, 16)
        B, T1, T2 = (2, 512, 512)
        key = jax.random.key(seed)
        ks = jax.random.split(key, 8)
        s = 1.0 / np.sqrt(D_MODEL)
        return {'x': jax.random.normal(ks[0], (B, T1, D_MODEL), dtype=jnp.float32), 'context': jax.random.normal(ks[1], (B, T2, D_MODEL), dtype=jnp.float32), 'bias': jax.random.normal(ks[2], (T1, T2), dtype=jnp.float32), 'W_q': jax.random.normal(ks[3], (D_MODEL, N_HEAD * D_HEAD), dtype=jnp.float32) * s, 'W_k': jax.random.normal(ks[4], (D_MODEL, N_HEAD * D_HEAD), dtype=jnp.float32) * s, 'W_v': jax.random.normal(ks[5], (D_MODEL, N_HEAD * D_HEAD), dtype=jnp.float32) * s, 'W_out': jax.random.normal(ks[6], (N_HEAD * D_HEAD, D_MODEL), dtype=jnp.float32) * s, 'b_out': jnp.zeros((D_MODEL,), dtype=jnp.float32)}
    _L0_xattn_all = _L0_xattn_setup()
    _L0_xattn_in = {k: v for k, v in _L0_xattn_all.items() if k in ('W_q', 'W_k', 'W_v', 'W_out', 'b_out')}
    del _L0_xattn_all

    def _L0_ffn_setup():
        import jax, jax.numpy as jnp
        import numpy as np
        S, B, H = (512, 4, 256)
        E = 64
        K = 4
        I = 128
        CAP = 256
        key = jax.random.key(seed)
        k1, k2, k3, k4 = jax.random.split(key, 4)
        return {'hidden_states': jax.random.normal(k1, (S, B, H), dtype=jnp.float32), 'router_w': jax.random.normal(k2, (H, E), dtype=jnp.float32) * 0.02, 'w1': jax.random.normal(k3, (E, H, 2 * I), dtype=jnp.float32) * 0.02, 'w2': jax.random.normal(k4, (E, I, H), dtype=jnp.float32) * 0.02}
    _L0_ffn_all = _L0_ffn_setup()
    _L0_ffn_in = {k: v for k, v in _L0_ffn_all.items() if k in ('router_w', 'w1', 'w2')}
    del _L0_ffn_all

    def _L1_xattn_setup():
        import jax, jax.numpy as jnp
        import numpy as np
        DIM = 256
        H = 16
        D = 64
        INNER = H * D
        EPS = 1e-05

        def layernorm(x, w, b):
            mu = jnp.mean(x, axis=-1, keepdims=True)
            var = jnp.var(x, axis=-1, keepdims=True)
            return (x - mu) * jax.lax.rsqrt(var + EPS) * w + b
        key = jax.random.key(seed)
        ks = jax.random.split(key, 8)
        B, N, S = (4, 64, 2048)
        s = 1.0 / np.sqrt(DIM)
        return {'latents': jax.random.normal(ks[0], (B, N, DIM), jnp.float32), 'context': jax.random.normal(ks[1], (B, S, DIM), jnp.float32), 'ln_l_w': jnp.ones((DIM,), jnp.float32), 'ln_l_b': jnp.zeros((DIM,), jnp.float32), 'ln_c_w': jnp.ones((DIM,), jnp.float32), 'ln_c_b': jnp.zeros((DIM,), jnp.float32), 'Wq': jax.random.normal(ks[2], (DIM, INNER), jnp.float32) * s, 'Wkv': jax.random.normal(ks[3], (DIM, 2 * INNER), jnp.float32) * s, 'Wo': jax.random.normal(ks[4], (INNER, DIM), jnp.float32) * (1.0 / np.sqrt(INNER)), 'bo': jnp.zeros((DIM,), jnp.float32)}
    _L1_xattn_all = _L1_xattn_setup()
    _L1_xattn_in = {k: v for k, v in _L1_xattn_all.items() if k in ('ln_l_w', 'ln_l_b', 'ln_c_w', 'ln_c_b', 'Wq', 'Wkv', 'Wo', 'bo')}
    del _L1_xattn_all

    def _L1_ffn_setup():
        import math
        import jax, jax.numpy as jnp
        import numpy as np
        B, T, H = (4, 512, 256)
        E, K, F = (8, 2, 512)
        CAP_FACTOR = 1.25

        def _moe_forward(x, Wg, W_in, W_out):
            b, t, h = x.shape
            xf = x.reshape(-1, h)
            S = xf.shape[0]
            C = int(math.ceil(K * S / E * CAP_FACTOR))
            logits = xf @ Wg
            probs = jax.nn.softmax(logits, axis=-1)
            top_vals, top_idx = jax.lax.top_k(probs, K)
            flat_idx = top_idx.T.reshape(-1)
            onehot = jax.nn.one_hot(flat_idx, E, dtype=jnp.int32)
            cum = jnp.cumsum(onehot, axis=0) - 1
            loc = jnp.take_along_axis(cum, flat_idx[:, None], axis=1)[:, 0]
            loc = loc.reshape(K, S).T
            keep = loc < C
            gates = top_vals * keep.astype(top_vals.dtype)
            denom = jnp.maximum(gates.sum(-1, keepdims=True), 1e-09)
            gates = gates / denom
            loc_c = jnp.where(keep, loc, C)
            e_flat = top_idx.reshape(-1)
            l_flat = loc_c.reshape(-1)
            xk = jnp.broadcast_to(xf[:, None, :], (S, K, h)).reshape(-1, h)
            xk = jnp.where(keep.reshape(-1, 1), xk, 0.0)
            buf = jnp.zeros((E, C + 1, h), x.dtype).at[e_flat, l_flat].set(xk)
            inp = buf[:, :C]
            hid = jnp.einsum('ech,ehf->ecf', inp, W_in)
            a, g = jnp.split(hid, 2, axis=-1)
            hid = jax.nn.gelu(a, approximate=False) * g
            out_e = jnp.einsum('ecf,efh->ech', hid, W_out)
            out_pad = jnp.concatenate([out_e, jnp.zeros((E, 1, h), out_e.dtype)], axis=1)
            gathered = out_pad[e_flat, l_flat].reshape(S, K, h)
            y = (gathered * gates[..., None]).sum(axis=1)
            return y.reshape(b, t, h)
        key = jax.random.key(seed)
        k1, k2, k3, k4 = jax.random.split(key, 4)
        x = jax.random.normal(k1, (B, T, H), dtype=jnp.float32)
        Wg = jax.random.normal(k2, (H, E), dtype=jnp.float32) * 0.02
        W_in = jax.random.normal(k3, (E, H, 2 * F), dtype=jnp.float32) * (1.0 / math.sqrt(H))
        W_out = jax.random.normal(k4, (E, F, H), dtype=jnp.float32) * (1.0 / math.sqrt(F))
        return {'x': x, 'Wg': Wg, 'W_in': W_in, 'W_out': W_out}
    _L1_ffn_all = _L1_ffn_setup()
    _L1_ffn_in = {k: v for k, v in _L1_ffn_all.items() if k in ('Wg', 'W_in', 'W_out')}
    del _L1_ffn_all
    return {'x': x, 'ctx_1024': ctx_1024, 'fside_SxS2_0': fside_SxS2_0, 'g_xattn': g_xattn, 'g_ffn': g_ffn, 'L0_xattn_W_q': _L0_xattn_in['W_q'], 'L0_xattn_W_k': _L0_xattn_in['W_k'], 'L0_xattn_W_v': _L0_xattn_in['W_v'], 'L0_xattn_W_out': _L0_xattn_in['W_out'], 'L0_xattn_b_out': _L0_xattn_in['b_out'], 'L0_ffn_router_w': _L0_ffn_in['router_w'], 'L0_ffn_w1': _L0_ffn_in['w1'], 'L0_ffn_w2': _L0_ffn_in['w2'], 'L1_xattn_ln_l_w': _L1_xattn_in['ln_l_w'], 'L1_xattn_ln_l_b': _L1_xattn_in['ln_l_b'], 'L1_xattn_ln_c_w': _L1_xattn_in['ln_c_w'], 'L1_xattn_ln_c_b': _L1_xattn_in['ln_c_b'], 'L1_xattn_Wq': _L1_xattn_in['Wq'], 'L1_xattn_Wkv': _L1_xattn_in['Wkv'], 'L1_xattn_Wo': _L1_xattn_in['Wo'], 'L1_xattn_bo': _L1_xattn_in['bo'], 'L1_ffn_Wg': _L1_ffn_in['Wg'], 'L1_ffn_W_in': _L1_ffn_in['W_in'], 'L1_ffn_W_out': _L1_ffn_in['W_out']}

def reference(x, ctx_1024, fside_SxS2_0, g_xattn, g_ffn, L0_xattn_W_q, L0_xattn_W_k, L0_xattn_W_v, L0_xattn_W_out, L0_xattn_b_out, L0_ffn_router_w, L0_ffn_w1, L0_ffn_w2, L1_xattn_ln_l_w, L1_xattn_ln_l_b, L1_xattn_ln_c_w, L1_xattn_ln_c_b, L1_xattn_Wq, L1_xattn_Wkv, L1_xattn_Wo, L1_xattn_bo, L1_ffn_Wg, L1_ffn_W_in, L1_ffn_W_out):
    import jax
    import jax.numpy as jnp

    def _L0_xattn_ref(x, context, bias, W_q, W_k, W_v, W_out, b_out):
        import jax, jax.numpy as jnp
        import numpy as np
        D_MODEL, D_HEAD, N_HEAD = (256, 64, 16)
        B, T1, T2 = (2, 512, 512)
        Bq, T1_, _ = x.shape
        T2_ = context.shape[1]
        atten_scale = 1.0 / np.sqrt(D_HEAD)
        head_scale = jnp.exp2(-jnp.arange(1, N_HEAD + 1, dtype=jnp.float32))
        q = (x @ W_q).reshape(Bq, T1_, N_HEAD, D_HEAD).transpose(0, 2, 1, 3)
        k = (context @ W_k).reshape(Bq, T2_, N_HEAD, D_HEAD).transpose(0, 2, 1, 3)
        v = (context @ W_v).reshape(Bq, T2_, N_HEAD, D_HEAD).transpose(0, 2, 1, 3)
        scores = jnp.einsum('bhqd,bhkd->bhqk', q, k) * atten_scale
        scores = scores + bias[None, None, :, :] * head_scale[None, :, None, None]
        attn = jax.nn.softmax(scores, axis=-1)
        out = jnp.einsum('bhqk,bhkd->bqhd', attn, v).reshape(Bq, T1_, N_HEAD * D_HEAD)
        return out @ W_out + b_out

    def _L0_ffn_ref(hidden_states, router_w, w1, w2):
        import jax, jax.numpy as jnp
        import numpy as np
        S, B, H = (512, 4, 256)
        E = 64
        K = 4
        I = 128
        CAP = 256
        s, b, h = hidden_states.shape
        x = hidden_states.reshape(-1, h)
        T = x.shape[0]
        P = T * K
        logits = x @ router_w
        probs_all = jax.nn.softmax(logits, axis=-1)
        top_p, top_i = jax.lax.top_k(probs_all, K)
        rows = jnp.arange(T)[:, None]
        routing_map = jnp.zeros((T, E), dtype=bool).at[rows, top_i].set(True)
        probs = jnp.zeros((T, E), dtype=x.dtype).at[rows, top_i].set(top_p)
        flat = routing_map.T.reshape(-1)
        order = jnp.argsort((~flat).astype(jnp.int32), stable=True)[:P]
        expert_id = order // T
        token_idx = order % T
        group_sizes = routing_map.sum(axis=0)
        starts = jnp.cumsum(group_sizes) - group_sizes
        pos = jnp.arange(P) - starts[expert_id]
        perm_x = x[token_idx]
        buf = jnp.zeros((E, CAP, h), dtype=x.dtype).at[expert_id, pos].set(perm_x)
        h1 = jnp.einsum('ech,ehf->ecf', buf, w1)
        g = jax.nn.silu(h1[..., :I]) * h1[..., I:]
        y = jnp.einsum('eci,eih->ech', g, w2)
        perm_y = y[expert_id, pos]
        perm_probs = probs.T.reshape(-1)[order]
        out = jnp.zeros((T, h), dtype=x.dtype).at[token_idx].add(perm_y * perm_probs[:, None])
        return out.reshape(s, b, h)

    def _L1_xattn_ref(latents, context, ln_l_w, ln_l_b, ln_c_w, ln_c_b, Wq, Wkv, Wo, bo):
        import jax, jax.numpy as jnp
        import numpy as np
        DIM = 256
        H = 16
        D = 64
        INNER = H * D
        EPS = 1e-05

        def layernorm(x, w, b):
            mu = jnp.mean(x, axis=-1, keepdims=True)
            var = jnp.var(x, axis=-1, keepdims=True)
            return (x - mu) * jax.lax.rsqrt(var + EPS) * w + b
        b, n, _ = latents.shape
        s = context.shape[1]
        lat = layernorm(latents, ln_l_w, ln_l_b)
        ctx = layernorm(context, ln_c_w, ln_c_b)
        q = (lat @ Wq).reshape(b, n, H, D).transpose(0, 2, 1, 3)
        kv = ctx @ Wkv
        k, v = jnp.split(kv, 2, axis=-1)
        k = k.reshape(b, s, H, D).transpose(0, 2, 1, 3)
        v = v.reshape(b, s, H, D).transpose(0, 2, 1, 3)
        scale = D ** (-0.5)
        attn = jnp.einsum('bhnd,bhsd->bhns', q, k) * scale
        attn = jnp.clip(attn, -11.0, 11.0)
        attn = jax.nn.softmax(attn, axis=-1)
        out = jnp.einsum('bhns,bhsd->bhnd', attn, v)
        out = out.transpose(0, 2, 1, 3).reshape(b, n, INNER)
        return out @ Wo + bo

    def _L1_ffn_ref(x, Wg, W_in, W_out):
        import math
        import jax, jax.numpy as jnp
        import numpy as np
        B, T, H = (4, 512, 256)
        E, K, F = (8, 2, 512)
        CAP_FACTOR = 1.25

        def _moe_forward(x, Wg, W_in, W_out):
            b, t, h = x.shape
            xf = x.reshape(-1, h)
            S = xf.shape[0]
            C = int(math.ceil(K * S / E * CAP_FACTOR))
            logits = xf @ Wg
            probs = jax.nn.softmax(logits, axis=-1)
            top_vals, top_idx = jax.lax.top_k(probs, K)
            flat_idx = top_idx.T.reshape(-1)
            onehot = jax.nn.one_hot(flat_idx, E, dtype=jnp.int32)
            cum = jnp.cumsum(onehot, axis=0) - 1
            loc = jnp.take_along_axis(cum, flat_idx[:, None], axis=1)[:, 0]
            loc = loc.reshape(K, S).T
            keep = loc < C
            gates = top_vals * keep.astype(top_vals.dtype)
            denom = jnp.maximum(gates.sum(-1, keepdims=True), 1e-09)
            gates = gates / denom
            loc_c = jnp.where(keep, loc, C)
            e_flat = top_idx.reshape(-1)
            l_flat = loc_c.reshape(-1)
            xk = jnp.broadcast_to(xf[:, None, :], (S, K, h)).reshape(-1, h)
            xk = jnp.where(keep.reshape(-1, 1), xk, 0.0)
            buf = jnp.zeros((E, C + 1, h), x.dtype).at[e_flat, l_flat].set(xk)
            inp = buf[:, :C]
            hid = jnp.einsum('ech,ehf->ecf', inp, W_in)
            a, g = jnp.split(hid, 2, axis=-1)
            hid = jax.nn.gelu(a, approximate=False) * g
            out_e = jnp.einsum('ecf,efh->ech', hid, W_out)
            out_pad = jnp.concatenate([out_e, jnp.zeros((E, 1, h), out_e.dtype)], axis=1)
            gathered = out_pad[e_flat, l_flat].reshape(S, K, h)
            y = (gathered * gates[..., None]).sum(axis=1)
            return y.reshape(b, t, h)
        return _moe_forward(x, Wg, W_in, W_out)
    x = x + jnp.tanh(g_xattn[0]) * _L0_xattn_ref(_layernorm(x, axis=-1), ctx_1024, fside_SxS2_0, L0_xattn_W_q, L0_xattn_W_k, L0_xattn_W_v, L0_xattn_W_out, L0_xattn_b_out)
    x = x + jnp.tanh(g_ffn[0]) * _L0_ffn_ref(_layernorm(x, axis=-1), L0_ffn_router_w, L0_ffn_w1, L0_ffn_w2)
    x = x + jnp.tanh(g_xattn[1]) * _L1_xattn_ref(_layernorm(x, axis=-1), ctx_1024, L1_xattn_ln_l_w, L1_xattn_ln_l_b, L1_xattn_ln_c_w, L1_xattn_ln_c_b, L1_xattn_Wq, L1_xattn_Wkv, L1_xattn_Wo, L1_xattn_bo)
    x = x + jnp.tanh(g_ffn[1]) * _L1_ffn_ref(_layernorm(x, axis=-1), L1_ffn_Wg, L1_ffn_W_in, L1_ffn_W_out)
    return x

_drawn_inputs = setup_inputs


def setup_inputs(seed=0):
    import zlib

    import numpy as np

    out = dict(_drawn_inputs(seed))
    spreads = {'g_ffn': (-1.0, 0.6),
     'L0_xattn_b_out': (0.0, 0.1),
     'L1_xattn_ln_l_w': (1.0, 0.6),
     'L1_xattn_ln_l_b': (0.0, 0.767),
     'L1_xattn_ln_c_w': (1.0, 0.2),
     'L1_xattn_ln_c_b': (0.0, 0.1),
     'L1_xattn_bo': (0.0, 0.1)}
    factors = {'L0_ffn_router_w': 8.0, 'L0_ffn_w1': 8.0, 'L0_ffn_w2': 8.0}
    for name, (base, spread) in spreads.items():
        noise = np.random.default_rng([zlib.crc32(name.encode()), seed]).standard_normal(out[name].shape)
        drawn = base * np.exp(spread * noise) if base else spread * noise
        out[name] = jnp.asarray(drawn.astype(out[name].dtype))
    for name, factor in factors.items():
        out[name] = (out[name] * factor).astype(out[name].dtype)
    return out
```

```python
from contextlib import ExitStack

import concourse.bass as bass
from concourse import mybir

F32 = mybir.dt.float32
BF16 = mybir.dt.bfloat16
I32 = mybir.dt.int32
U32 = mybir.dt.uint32
ACT = mybir.ActivationFunctionType
ALU = mybir.AluOpType
AX = mybir.AxisListType.X

P = 128
NB = 32
D = 256
DC = D // P
H = 16
DH = 64
INNER = H * DH
HP = H // 2
GT = 2
NG = NB // GT
TOK = GT * P
HU = 4
UT = H // HU
UG = GT * UT
NU = NG * UG
EPS = 1e-5
SCALE = DH ** -0.5
CLIP = 11.0
BIG = 65536.0

E0, K0, F0, CAP0 = 64, 4, 128, 256
E1, K1, F1, CAP1 = 8, 2, 512, 1280
SLOT_TILES1 = CAP1 // TOK


def plus(g, n):
    return g + n if isinstance(g, int) else (g[0], g[1] + n)


def begun(g, n):
    return not isinstance(g, int) or g >= n


def at(g, per, k):
    if isinstance(g, int):
        return g * per + k
    reg, half = g
    return reg * (2 * per) + (half * per + k)


class Memory:

    def __init__(self, nc, stack):
        self.nc, self.stack = nc, stack

    def sb(self, name, shape, dt=F32):
        return self.stack.enter_context(self.nc.sbuf_tensor(name, shape, dt))

    def ps(self, name, shape, dt=F32):
        return self.stack.enter_context(self.nc.psum_tensor(name, shape, dt))

    def sem(self, name):
        return self.stack.enter_context(self.nc.semaphore(name))


def row_vector(ap, n):
    return ap.rearrange("(o n) -> o n", o=1).broadcast_to([P, n])


def setup(nc, t, d):
    with ExitStack() as stack:
        m = Memory(nc, stack)
        raw = m.sb("raw_gates", [P, 4])
        bo = m.sb("bo_raw", [P, 2, D])
        side = m.sb("side", [P, P])
        s_load = m.sem("setup_loaded")
        s_zero = m.sem("setup_cleared")
        s_const = m.sem("setup_made")
        s_tanh = m.sem("setup_tanh")
        s_v = m.sem("setup_vector")
        block = stack.enter_context(nc.Block())
        loads = 10

        @block.sync
        def _(sp):
            sp.dma_start(raw[:, 0:2], row_vector(d["g_xattn"], 2)).then_inc(s_load, 16)
            sp.dma_start(raw[:, 2:4], row_vector(d["g_ffn"], 2)).then_inc(s_load, 16)
            sp.dma_start(bo[:, 0, :], row_vector(d["L0_xattn_b_out"], D)).then_inc(s_load, 16)
            sp.dma_start(bo[:, 1, :], row_vector(d["L1_xattn_bo"], D)).then_inc(s_load, 16)
            sp.dma_start(side[:], d["fside_SxS2_0"]).then_inc(s_load, 16)
            for i, name in enumerate(("L1_xattn_ln_l_w", "L1_xattn_ln_l_b", "L1_xattn_ln_c_w", "L1_xattn_ln_c_b")):
                with nc.allow_non_contiguous_dma("256 numbers, one column each"):
                    sp.dma_start(t.affine[:, i, :], d[name].rearrange("(c p) -> p c", p=P)).then_inc(s_load, 16)
            sp.dma_start(t.x[:], d["x"].rearrange("b p d -> p b d")).then_inc(s_load, 16)
            sp.wait_ge(s_load, 16 * loads)

        @block.gpsimd
        def _(pool):
            g = nc.gpsimd
            g.memset(t.ident[:], 0.0).then_inc(s_zero, 1)
            g.memset(t.tri[:], 1.0).then_inc(s_zero, 1)
            g.memset(t.ones_bf[:], 1.0).then_inc(s_zero, 1)
            g.memset(t.minus_half[:], -0.5).then_inc(s_zero, 1)
            g.memset(t.zeros[:], 0.0).then_inc(s_zero, 1)
            pool.wait_ge(s_zero, 5)
            g.affine_select(out=t.ident[:], in_=t.ident[:], compare_op=ALU.not_equal, fill=1.0, base=0,
                            pattern=[[-1, P]], channel_multiplier=1).then_inc(s_const, 1)
            g.affine_select(out=t.tri[:], in_=t.tri[:], compare_op=ALU.is_gt, fill=0.0, base=0,
                            pattern=[[1, P]], channel_multiplier=-1).then_inc(s_const, 1)
            g.iota(t.iota[:], pattern=[[1, E0]], base=0, channel_multiplier=0,
                   allow_small_or_imprecise_dtypes=True).then_inc(s_const, 1)
            pool.wait_ge(s_const, 3)

        @block.scalar
        def _(act):
            act.wait_ge(s_load, 16 * loads)
            nc.scalar.activation(t.gate[:], raw[:], ACT.Tanh).then_inc(s_tanh, 1)
            act.wait_ge(s_tanh, 1)

        @block.vector
        def _(v):
            v.wait_ge(s_load, 16 * loads)
            for h in range(H):
                nc.vector.tensor_scalar(t.bias[:, h, :], side[:], 2.0 ** -(h + 1), None, ALU.mult)
            v.wait_ge(s_tanh, 1)
            for i in range(2):
                nc.vector.tensor_scalar(t.bo[:, i, :], bo[:, i, :], t.gate[:, i:i + 1], None, ALU.mult).then_inc(s_v, 1)
            v.wait_ge(s_v, 2)


def attention(nc, t, d, layer):
    L = f"a{layer}_"
    first = layer == 0
    with ExitStack() as stack:
        m = Memory(nc, stack)
        wq = m.sb(L + "wq", [P, DC, INNER])
        wk = m.sb(L + "wk", [P, DC, INNER])
        wv = m.sb(L + "wv", [P, DC, INNER])
        wo = m.sb(L + "wo", [P, HP, D])
        ctx = m.sb(L + "ctx", [P, 2, GT, D])
        xn = m.sb(L + "xn", [P, 2, GT, D])
        aT = m.sb(L + "aT", [P, 2, 2, DC, TOK])
        qT = m.sb(L + "qT", [P, 2, HP, TOK])
        kz = m.sb(L + "kz", [P, 2, HP, 2, TOK])
        v = m.sb(L + "v", [P, 2, GT, INNER])
        S = m.sb(L + "S", [P, 4, HU, P])
        PT = m.sb(L + "PT", [P, 2, HU, P])
        oT = m.sb(L + "oT", [P, 2, HP, P])
        stats = m.sb(L + "stats", [P, 2 * GT, 6])
        mv = m.sb(L + "mv", [P, 2 * GT, 2])
        var_eps = m.sb(L + "var_eps", [P, 2 * GT])
        rstd = m.sb(L + "rstd", [P, 2 * GT])
        mx = m.sb(L + "mx", [P, 2, HU])
        z = m.sb(L + "z", [P, 2, HU])
        rz = m.sb(L + "rz", [P, 2, HU])
        psP = [m.ps(L + f"psP{i}", [P, 512]) for i in range(2)]
        psS = [m.ps(L + f"psS{i}", [P, HU, P]) for i in range(2)]
        psT = [m.ps(L + f"psT{i}", [P, HU, P]) for i in range(2)]
        psV = m.ps(L + "psV", [P, 4, P])
        psM = m.ps(L + "psM", [P, 2, TOK])

        s_w = m.sem(L + "weights_loaded")
        s_kz = m.sem(L + "k_cleared")
        s_ctx = [m.sem(L + f"context_loaded{i}") for i in range(2)]
        s_zero = m.sem(L + "zeros_sent")
        s_st = m.sem(L + "stats_ready")
        s_mv = m.sem(L + "moments_ready")
        s_ve = m.sem(L + "variance_shifted")
        s_rstd = m.sem(L + "rstd_ready")
        s_xn = m.sem(L + "normed")
        s_tin = m.sem(L + "inputs_transposed")
        s_aT = m.sem(L + "inputs_evacuated")
        s_pj = m.sem(L + "projected")
        s_ev = [m.sem(L + f"projection_evacuated{i}") for i in range(2)]
        s_sc = m.sem(L + "scores_ready")
        s_read = m.sem(L + "scores_read")
        s_max = m.sem(L + "max_ready")
        s_sub = m.sem(L + "max_subtracted")
        s_exp = m.sem(L + "exp_ready")
        s_sum = m.sem(L + "sum_ready")
        s_rz = m.sem(L + "sum_inverted")
        s_norm = m.sem(L + "probs_normed")
        s_tr = m.sem(L + "probs_transposed")
        s_PT = m.sem(L + "probs_evacuated")
        s_pv = m.sem(L + "values_weighted")
        s_oT = m.sem(L + "heads_evacuated")
        s_wo = m.sem(L + "output_projected")
        s_bo = m.sem(L + "output_bias_added")
        s_x = m.sem(L + "x_updated")
        if not first:
            idx = m.sb(L + "idx", [P, GT * K0], I32)
            rows = m.sb(L + "rows", [P, GT * K0, D])
            cn = m.sb(L + "cn", [P, 2, GT, D])
            s_ix = m.sem(L + "indices_copied")
            s_row = m.sem(L + "rows_gathered")
            s_acc = m.sem(L + "row_added")
            s_xn1 = m.sem(L + "normed_once")
            s_cn = m.sem(L + "context_normed")
        block = stack.enter_context(nc.Block())

        JOBS = [("q", i) for i in range(4)] + [("k", i) for i in range(4)] + [("v", i) for i in range(4)]
        NJ = len(JOBS)
        OF_STEP = [[0, 1], [2], [3, 4], [5], [6, 7], [8], [9, 10], [11]]
        XT_STEP, CT_STEP = 5, 6

        def has(g, u, lag):
            return not isinstance(g, int) or 0 <= g * UG + u - lag < NU

        def settle(eng):
            eng.sem_inc(t.s_passed, 1)

        def run(eng, step, before):
            before()
            for u in range(UG):
                step(0, u, 0, True, True)
            for u in range(UG):
                step(1, u, 1, True, True)
            with eng.Fori(1, NG // 2 - 1) as j:
                for half in range(2):
                    for u in range(UG):
                        step((j, half), u, half, True, True)
            for u in range(UG):
                step(NG - 2, u, 0, True, False)
            for u in range(UG):
                step(NG - 1, u, 1, False, False)
            for u in range(4):
                step(NG, u, 0, False, False)

        def x_tile(g, i):
            if isinstance(g, int):
                return t.x[:, g * GT + i, :]
            return t.x[:, bass.ds(at(g, GT, i), 1), :].rearrange("p a d -> p (a d)")

        def wait_ctx(eng, g, par):
            eng.wait_ge(s_ctx[par], (g // 2 + 1) * 16 if isinstance(g, int) else g[0] * 16 + (g[1] // 2 + 1) * 16)

        @block.sync
        def _(sp):
            names = (("L0_xattn_W_q", 0), ("L0_xattn_W_k", 0), ("L0_xattn_W_v", 0), "L0_xattn_W_out") if first else (
                ("L1_xattn_Wq", 0), ("L1_xattn_Wkv", 0), ("L1_xattn_Wkv", INNER), "L1_xattn_Wo")

            def load_ctx(g, par):
                if begun(g, 2):
                    if first:
                        sp.wait_ge(s_tin, at(g, 2, 2 - 4))
                    else:
                        sp.wait_ge(s_cn, at(g, GT, GT - 2 * GT))
                src = d["ctx_1024"][g * GT:(g + 1) * GT] if isinstance(g, int) else d["ctx_1024"][bass.ds(at(g, GT, 0), GT)]
                sp.dma_start(ctx[:, par], src.rearrange("b p d -> p b d")).then_inc(s_ctx[par], 16)

            load_ctx(0, 0)
            for w, (name, off) in zip((wq, wk, wv), names):
                sp.dma_start(w[:], d[name][:, off:off + INNER].rearrange("(c p) n -> p c n", p=P)).then_inc(s_w, 16)
            load_ctx(1, 1)
            sp.dma_start(wo[:], d[names[3]].rearrange("(c p) n -> p c n", p=P)).then_inc(s_w, 16)
            n_zero = 0
            if first:
                for buf in (d["buf0"], d["buf1"]):
                    view = buf.rearrange("(p r) d -> p (r d)", p=P)
                    zw = t.zeros.shape[1]
                    for i in range(view.shape[1] // zw):
                        sp.dma_start(view[:, i * zw:(i + 1) * zw], t.zeros[:]).then_inc(s_zero, 16)
                        n_zero += 16
            with sp.Fori(1, NG // 2) as j:
                for half in range(2):
                    load_ctx((j, half), half)
            if n_zero:
                sp.wait_ge(s_zero, n_zero)

        @block.gpsimd
        def _(pool):
            g_ = nc.gpsimd
            NR = 1 if first else 2

            def rstd_of(g, r, n):
                pool.wait_ge(s_mv, at(g, NR, r + 1))
                if first and begun(g, 1):
                    pool.wait_ge(s_xn, at(g, 1, 0))
                settle(pool)
                g_.tensor_scalar(var_eps[:, 0:n], mv[:, 0:n, 1], EPS, None, ALU.add).then_inc(s_ve, 1)
                pool.wait_ge(s_ve, at(g, NR, r + 1))
                g_.tensor_tensor(rstd[:, 0:n], var_eps[:, 0:n], t.minus_half[:, 0:n], ALU.pow).then_inc(s_rstd, 1)

            def gather(g):
                pool.wait_ge(s_ix, at(g, 1, 1))
                if begun(g, 1):
                    pool.wait_ge(s_acc, at(g, GT * K0, 0))
                settle(pool)
                for i in range(GT * K0):
                    g_.indirect_dma_start(out=rows[:, i, :], out_offset=None, in_=d["y0"],
                                          in_offset=bass.IndirectOffsetOnAxis(ap=idx[:, i:i + 1], axis=0)
                                          ).then_inc(s_row, 16)

            def round1(g, par):
                rstd_of(g, 0, GT if first else 2 * GT)
                if not first:
                    pool.wait_ge(s_rstd, at(g, NR, 1))
                    if begun(g, 2):
                        pool.wait_ge(s_tin, at(g, 2, 2 - 4))
                    settle(pool)
                    for i in range(GT):
                        g_.tensor_scalar(cn[:, par, i], ctx[:, par, i], mv[:, GT + i, 0:1],
                                         rstd[:, GT + i:GT + i + 1], ALU.subtract, ALU.mult).then_inc(s_cn, 1)

            def round2(g, par):
                rstd_of(g, 1, GT)
                pool.wait_ge(s_rstd, at(g, NR, 2))
                settle(pool)
                for i in range(GT):
                    ins = g_.tensor_scalar(xn[:, par, i], xn[:, par, i], mv[:, i, 0:1], rstd[:, i:i + 1],
                                           ALU.subtract, ALU.mult)
                ins.then_inc(s_xn, 1)

            def step(g, u, par, proj, prep):
                if has(g, u, 1):
                    pool.wait_ge(s_rz, at(g, UG, u))
                    s = S[:, (u - 1) % 4]
                    g_.tensor_tensor(s, s, rz[:, (u - 1) % 2, :].unsqueeze(2).broadcast_to([P, HU, P]), ALU.mult
                                     ).then_inc(s_norm, 1)
                if first and has(g, u, 0):
                    pool.wait_ge(s_max, at(g, UG, u + 1))
                    s = S[:, u % 4]
                    g_.tensor_tensor(s, s, mx[:, u % 2, :].unsqueeze(2).broadcast_to([P, HU, P]), ALU.subtract
                                     ).then_inc(s_sub, 1)
                if prep:
                    if not first and u == 0:
                        gather(plus(g, 2))
                    if u == 2:
                        round1(plus(g, 2), par)
                    if not first and u == 4:
                        round2(plus(g, 2), par)

            def before():
                g_.memset(kz[:], 0.0).then_inc(s_kz, 1)
                for g in (0, 1):
                    if not first:
                        gather(g)
                    round1(g, g)
                    if not first:
                        round2(g, g)

            run(pool, step, before)

        @block.scalar
        def _(act):
            a = nc.scalar

            def evac_in(g, par, which):
                act.wait_ge(s_tin, at(g, 2, which + 1))
                if begun(g, 2):
                    act.wait_ge(s_pj, at(g, NJ, NJ - 2 * NJ))
                if first:
                    a.activation(aT[:, par, which], psM[:], ACT.Copy).then_inc(s_aT, 1)
                else:
                    for c in range(DC):
                        ins = a.activation(aT[:, par, which, c], psM[:, c], ACT.Identity,
                                           bias=t.affine[:, 2 * which + 1, c:c + 1], scale=t.affine[:, 2 * which, c:c + 1])
                    ins.then_inc(s_aT, 1)

            def evac_job(g, par, j):
                kind, i = JOBS[j]
                if kind == "k":
                    return
                act.wait_ge(s_pj, at(g, NJ, j + 1))
                if begun(g, 2) and j == 0:
                    act.wait_ge(s_sc, at(g, UG, -UG))
                if begun(g, 2) and j == 8:
                    act.wait_ge(s_pv, at(g, UG, -UG))
                if kind == "q":
                    ins = a.activation(qT[:, par, 2 * i:2 * i + 2], psP[j % 2][:].rearrange("p (c n) -> p c n", c=2),
                                       ACT.Copy, scale=SCALE)
                else:
                    ins = a.activation(v[:, par, i // 2, (i % 2) * 512:(i % 2) * 512 + 512], psP[j % 2][:], ACT.Copy)
                ins.then_inc(s_ev[j % 2], 1)

            def step(g, u, par, proj, prep):
                if proj:
                    for j in OF_STEP[u]:
                        evac_job(plus(g, 1), 1 - par, j)
                if has(g, u, 0):
                    act.wait_ge(s_sub if first else s_read, at(g, UG, u + 1))
                    s = S[:, u % 4]
                    a.activation(s, s, ACT.Exp).then_inc(s_exp, 1)
                if has(g, u, 2):
                    act.wait_ge(s_tr, at(g, UG, u - 1))
                    if has(g, u, 4):
                        act.wait_ge(s_pv, at(g, UG, u - 3))
                    a.activation(PT[:, u % 2], psT[u % 2][:], ACT.Copy).then_inc(s_PT, 1)
                if u % 2 == 0 and has(g, u, 3):
                    act.wait_ge(s_pv, at(g, UG, u - 2))
                    eight = ((u - 4) // 2) % 4
                    if not isinstance(g, int) or g * UG + u >= 12:
                        act.wait_ge(s_wo, at(g, GT, (u - 4) // 4 - 1))
                    a.activation(oT[:, eight // 2, (eight % 2) * 4:(eight % 2) * 4 + 4], psV[:], ACT.Copy).then_inc(s_oT, 1)
                if prep and u in (XT_STEP, CT_STEP):
                    evac_in(plus(g, 2), par, u - XT_STEP)

            def before():
                evac_in(0, 0, 0)
                evac_in(0, 0, 1)
                for j in range(NJ):
                    evac_job(0, 0, j)
                evac_in(1, 1, 0)
                evac_in(1, 1, 1)

            run(act, step, before)

        @block.vector
        def _(ve):
            v_ = nc.vector
            NR = 1 if first else 2

            def indices(g):
                if begun(g, 1):
                    ve.wait_ge(s_row, at(g, GT * K0 * 16, 0))
                src = t.comb0[:, g * GT:(g + 1) * GT] if isinstance(g, int) else t.comb0[:, bass.ds(at(g, GT, 0), GT)]
                v_.tensor_copy(idx[:].rearrange("p (t k) -> p t k", k=K0), src).then_inc(s_ix, 1)

            def add_rows(g):
                ve.wait_ge(s_row, at(g, GT * K0 * 16, GT * K0 * 16))
                n = 0
                for k in range(K0):
                    for i in range(GT):
                        pr = (t.prob0[:, g * GT + i, k:k + 1] if isinstance(g, int)
                              else t.prob0[:, bass.ds(at(g, GT, i), 1), k:k + 1].rearrange("p a b -> p (a b)"))
                        if k:
                            ve.wait_ge(s_acc, at(g, GT * K0, n - GT + 1))
                        v_.scalar_tensor_tensor(out=x_tile(g, i), in0=rows[:, i * K0 + k, :], scalar=pr, in1=x_tile(g, i),
                                                op0=ALU.mult, op1=ALU.add).then_inc(s_acc, 1)
                        n += 1
                ve.wait_ge(s_acc, at(g, GT * K0, n))

            def moments(g, par, r):
                n = 2 * GT if r == 0 and not first else GT
                if r == 0 and begun(g, 1):
                    ve.wait_ge(s_xn, at(g, 1, 0))
                    if not first:
                        ve.wait_ge(s_cn, at(g, GT, 0))
                if r:
                    ve.wait_ge(s_xn1, at(g, GT, GT))
                elif not first:
                    wait_ctx(ve, g, par)
                settle(ve)
                for i in range(n):
                    src = x_tile(g, i) if r == 0 and i < GT else xn[:, par, i] if r else ctx[:, par, i - GT]
                    v_.bn_stats(stats[:, i], src).then_inc(s_st, 1)
                per = GT if first else 3 * GT
                ve.wait_ge(s_st, at(g, per, n if r == 0 else per))
                if r:
                    ve.wait_ge(s_cn, at(g, GT, GT))
                settle(ve)
                for i in range(n):
                    ins = v_.bn_aggr(mv[:, i], stats[:, i])
                ins.then_inc(s_mv, 1)

            def norm(g, par):
                ve.wait_ge(s_rstd, at(g, NR, 1))
                ve.wait_ge(s_mv, at(g, NR, 1))
                if begun(g, 2):
                    ve.wait_ge(s_tin, at(g, 2, 2 - 4))
                for i in range(GT):
                    ins = v_.tensor_scalar(xn[:, par, i], x_tile(g, i), mv[:, i, 0:1], rstd[:, i:i + 1],
                                           ALU.subtract, ALU.mult)
                    if not first:
                        ins.then_inc(s_xn1, 1)
                if first:
                    ins.then_inc(s_xn, 1)

            def evac_k(g, par, j):
                kind, i = JOBS[j]
                if kind != "k":
                    return
                ve.wait_ge(s_pj, at(g, NJ, j + 1))
                if j == 4 and begun(g, 2):
                    ve.wait_ge(s_sc, at(g, UG, -UG))
                if j == 4 and isinstance(g, int) and g < 2:
                    ve.wait_ge(s_kz, 1)
                src = psP[j % 2][:].rearrange("p (c n) -> p c n", c=2)
                v_.tensor_copy(kz[0:DH, par, 2 * i:2 * i + 2, 0], src[0:DH])
                v_.tensor_copy(kz[DH:P, par, 2 * i:2 * i + 2, 1], src[DH:P]).then_inc(s_ev[j % 2], 1)

            def step(g, u, par, proj, prep):
                if has(g, u, 1):
                    s = S[:, (u - 1) % 4]
                    ve.wait_ge(s_exp, at(g, UG, u))
                    v_.tensor_reduce(z[:, (u - 1) % 2], s, AX, ALU.add).then_inc(s_sum, 1)
                    if has(g, u, 3):
                        ve.wait_ge(s_norm, at(g, UG, u - 2))
                    ve.wait_ge(s_sum, at(g, UG, u))
                    v_.reciprocal(rz[:, (u - 1) % 2], z[:, (u - 1) % 2]).then_inc(s_rz, 1)
                if has(g, u, 0):
                    s = S[:, u % 4]
                    if has(g, u, 4):
                        ve.wait_ge(s_tr, at(g, UG, u - 3))
                    ve.wait_ge(s_sc, at(g, UG, u + 1))
                    if first:
                        hu = (u % UT) * HU
                        v_.tensor_tensor(s, psS[u % 2][:], t.bias[:, hu:hu + HU], ALU.add).then_inc(s_read, 1)
                        if has(g, u, 2):
                            ve.wait_ge(s_sub, at(g, UG, u - 1))
                        ve.wait_ge(s_read, at(g, UG, u + 1))
                        v_.tensor_reduce(mx[:, u % 2], s, AX, ALU.max).then_inc(s_max, 1)
                    else:
                        v_.tensor_scalar(s, psS[u % 2][:], CLIP, -CLIP, ALU.min, ALU.max).then_inc(s_read, 1)
                if proj:
                    for j in OF_STEP[u]:
                        evac_k(plus(g, 1), 1 - par, j)
                if u % UT == 3 and has(g, u, 7):
                    i = u // UT - 1
                    x = x_tile(g, i)
                    v_.tensor_tensor(x, x, t.bo[:, layer], ALU.add).then_inc(s_bo, 1)
                    ve.wait_ge(s_bo, at(g, GT, i + 1))
                    ve.wait_ge(s_wo, at(g, GT, i + 1))
                    v_.scalar_tensor_tensor(out=x, in0=psM[:, 0], scalar=t.gate[:, layer:layer + 1], in1=x,
                                            op0=ALU.mult, op1=ALU.add).then_inc(s_x, 1)
                if prep:
                    g2 = plus(g, 2)
                    if u == 0 and not first:
                        indices(g2)
                    if u == 2:
                        if not first:
                            add_rows(g2)
                        moments(g2, par, 0)
                    if u == 3:
                        norm(g2, par)
                        if not first:
                            moments(g2, par, 1)

            def before():
                for g in (0, 1):
                    if not first:
                        indices(g)
                        add_rows(g)
                    moments(g, g, 0)
                    norm(g, g)
                    if not first:
                        moments(g, g, 1)
                for j in range(NJ):
                    evac_k(0, 0, j)

            run(ve, step, before)

        @block.tensor
        def _(pe):
            mm, tp = nc.tensor.matmul, nc.tensor.transpose

            def inputs(g, par, which):
                if which == 0 or not first:
                    pe.wait_ge(s_xn, at(g, 1, 1))
                if not first:
                    pe.wait_ge(s_cn, at(g, GT, GT))
                elif which:
                    wait_ctx(pe, g, par)
                if which or begun(g, 1):
                    pe.wait_ge(s_aT, at(g, 2, which))
                if which == 0 and begun(g, 3):
                    pe.wait_ge(s_x, at(g, GT, -2 * GT))
                src = xn if which == 0 else ctx if first else cn
                for c in range(DC):
                    for i in range(GT):
                        ins = tp(psM[:, c, i * P:(i + 1) * P], src[:, par, i, c * P:(c + 1) * P], t.ident[:])
                ins.then_inc(s_tin, 1)

            def project(g, par, j):
                kind, i = JOBS[j]
                if j == 0:
                    pe.wait_ge(s_aT, at(g, 2, 2))
                if begun(g, 1) or j >= 2:
                    pe.wait_ge(s_ev[j % 2], at(g, NJ // 2, j // 2))
                bank = psP[j % 2]
                if kind == "v":
                    tile, half = i // 2, i % 2
                    for c in range(DC):
                        ins = mm(bank[:], aT[:, par, 1, c, tile * P:(tile + 1) * P], wv[:, c, half * 512:half * 512 + 512],
                                 start=c == 0, stop=c == DC - 1)
                else:
                    w, src = (wq, 0) if kind == "q" else (wk, 1)
                    for b in range(2):
                        for c in range(DC):
                            ins = mm(bank[:, b * TOK:(b + 1) * TOK], w[:, c, (2 * i + b) * P:(2 * i + b + 1) * P],
                                     aT[:, par, src, c], start=c == 0, stop=c == DC - 1)
                ins.then_inc(s_pj, 1)

            def step(g, u, par, proj, prep):
                if has(g, u, 0):
                    if u == 0:
                        for i in range(2):
                            pe.wait_ge(s_ev[i], at(g, NJ // 2, NJ // 2))
                    if has(g, u, 2):
                        pe.wait_ge(s_read, at(g, UG, u - 1))
                    tile = u // UT
                    for i in range(2):
                        pair = (u % UT) * 2 + i
                        ins = mm(psS[u % 2][:, 2 * i:2 * i + 2], qT[:, par, pair, tile * P:(tile + 1) * P],
                                 kz[:, par, pair, :, tile * P:(tile + 1) * P], start=True, stop=True)
                    ins.then_inc(s_sc, 1)
                if proj:
                    for j in OF_STEP[u]:
                        project(plus(g, 1), 1 - par, j)
                if has(g, u, 2):
                    pe.wait_ge(s_norm, at(g, UG, u - 1))
                    if has(g, u, 4):
                        pe.wait_ge(s_PT, at(g, UG, u - 3))
                    for h in range(HU):
                        ins = tp(psT[u % 2][:, h], S[:, (u - 2) % 4, h], t.ident[:])
                    ins.then_inc(s_tr, 1)
                if has(g, u, 3):
                    pe.wait_ge(s_PT, at(g, UG, u - 2))
                    un = (u - 3) % UG
                    vpar = par if u >= 3 else 1 - par
                    if un % 2 == 0 and has(g, u, 5):
                        pe.wait_ge(s_oT, at(g, UG // 2, (u - 3) // 2))
                    tile = un // UT
                    for h in range(HU):
                        head = (un % UT) * HU + h
                        row = (h % 2) * DH
                        ins = mm(psV[row:row + DH, (un % 2) * 2 + h // 2], v[:, vpar, tile, head * DH:(head + 1) * DH],
                                 PT[:, (u - 3) % 2, h], start=True, stop=True)
                    ins.then_inc(s_pv, 1)
                if u % UT == 3 and has(g, u, 7):
                    i = u // UT - 1
                    pe.wait_ge(s_oT, at(g, UG // 2, 4 * i // 2 + 2))
                    if begun(g, 1) or i > 0:
                        pe.wait_ge(s_x, at(g, GT, i))
                    if prep:
                        if u == 7:
                            pe.wait_ge(s_aT, at(g, 2, 6))
                        else:
                            pe.wait_ge(s_aT, at(g, 2, 4))
                    for c in range(HP):
                        ins = mm(psM[:, 0], oT[:, i % 2, c], wo[:, c], start=c == 0, stop=c == HP - 1)
                    ins.then_inc(s_wo, 1)
                if prep and u in (XT_STEP, CT_STEP):
                    inputs(plus(g, 2), par, u - XT_STEP)

            def before():
                inputs(0, 0, 0)
                inputs(0, 0, 1)
                pe.wait_ge(s_w, 64)
                for j in range(NJ):
                    project(0, 0, j)
                inputs(1, 1, 0)
                inputs(1, 1, 1)

            run(pe, step, before)


def routing(nc, t, d, layer):
    L = f"r{layer}_"
    first = layer == 0
    E, K, CAP = (E0, K0, CAP0) if first else (E1, K1, CAP1)
    CW = E if first else K * E
    with ExitStack() as stack:
        m = Memory(nc, stack)
        rw = m.sb(L + "rw", [P, DC, E])
        xn = m.sb(L + "xn", [P, 2, GT, D]) if first else m.sb(L + "xn_all", [P, NB, D])
        xs = None if first else m.sb(L + "xs", [P, GT, D])
        xT = m.sb(L + "xT", [P, 2, DC, TOK])
        stats = m.sb(L + "stats", [P, GT, 6])
        mv = m.sb(L + "mv", [P, GT, 2])
        var_eps = m.sb(L + "var_eps", [P, GT])
        rstd = m.sb(L + "rstd", [P, GT])
        mx = m.sb(L + "mx", [P, GT])
        pr = m.sb(L + "pr", [P, GT, E])
        z = m.sb(L + "z", [P, GT])
        rz = m.sb(L + "rz", [P, GT])
        top = m.sb(L + "top", [P, GT, 8])
        ids = m.sb(L + "ids", [P, GT, 8], U32)
        idf = m.sb(L + "idf", [P, GT, K])
        oh = m.sb(L + "oh", [P, GT, K, E])
        cnt = m.sb(L + "cnt", [P, GT, CW], BF16)
        acc = m.sb(L + "acc", [P, CW], BF16)
        sel = m.sb(L + "sel", [P, GT, K, E])
        nt = GT if first else NB
        pos = m.sb(L + "pos", [P, nt, K])
        over = m.sb(L + "over", [P, nt, K])
        slot = m.sb(L + "slot", [P, nt, K])
        disp = m.sb(L + "disp", [P, 2 if first else 1, nt, K], I32)
        ps_x = m.ps(L + "ps_x", [P, DC, TOK])
        ps_l = m.ps(L + "ps_l", [P, GT, E])
        ps_c = m.ps(L + "ps_c", [P, GT, CW])
        s_w = m.sem(L + "router_loaded")
        s_v = m.sem(L + "vector_chain")
        s_st = m.sem(L + "stats_ready")
        s_mv = m.sem(L + "moments_ready")
        s_ve = m.sem(L + "variance_shifted")
        s_rstd = m.sem(L + "rstd_ready")
        s_xn = m.sem(L + "normed")
        s_tx = m.sem(L + "transposed")
        s_xT = m.sem(L + "evacuated")
        s_lg = m.sem(L + "logits_ready")
        s_sh = m.sem(L + "logits_shifted")
        s_exp = m.sem(L + "exp_ready")
        s_cnt = m.sem(L + "choices_ready")
        s_pos = m.sem(L + "positions_ready")
        s_sel = m.sem(L + "positions_read")
        s_slot = m.sem(L + "slots_ready")
        s_out = m.sem(L + "rows_scattered")
        if not first:
            oh2 = m.sb(L + "oh2", [P, NB, E])
            idf_all = m.sb(L + "idf_all", [P, NB, K])
            p_all = m.sb(L + "p_all", [P, NB, K])
            gates = m.sb(L + "gates", [P, NB, K])
            den = m.sb(L + "den", [P, NB])
            add1 = m.sb(L + "add1", [P, NB])
            total = m.sb(L + "total", [P, E])
            s_tot = m.sem(L + "totals_ready")
        block = stack.enter_context(nc.Block())
        NS = NG
        buf = d[f"buf{layer}"]

        def settle(eng):
            eng.sem_inc(t.s_passed, 1)

        def tiles(ap, g):
            return ap[:, g * GT:(g + 1) * GT] if isinstance(g, int) else ap[:, bass.ds(at(g, GT, 0), GT)]

        def x_tile(g, i):
            if isinstance(g, int):
                return t.x[:, g * GT + i, :]
            return t.x[:, bass.ds(at(g, GT, i), 1), :].rearrange("p a d -> p (a d)")

        def run(eng, step):
            step(0, 0)
            step(1, 1)
            with eng.Fori(1, NS // 2) as j:
                for half in range(2):
                    step((j, half), half)

        @block.sync
        def _(sp):
            name = "L0_ffn_router_w" if first else "L1_ffn_Wg"
            sp.dma_start(rw[:], d[name].rearrange("(c p) e -> p c e", p=P)).then_inc(s_w, 16)

        @block.gpsimd
        def _(pool):
            g_ = nc.gpsimd

            def norm(g, par):
                pool.wait_ge(s_mv, at(g, 1, 1))
                if begun(g, 1):
                    pool.wait_ge(s_xn, at(g, 1, 0))
                settle(pool)
                g_.tensor_scalar(var_eps[:], mv[:, :, 1], EPS, None, ALU.add).then_inc(s_ve, 1)
                pool.wait_ge(s_ve, at(g, 1, 1))
                g_.tensor_tensor(rstd[:], var_eps[:], t.minus_half[:, 0:GT], ALU.pow).then_inc(s_rstd, 1)

            def scatter(g, par):
                pool.wait_ge(s_slot, at(g, 1, 1))
                settle(pool)
                for i in range(GT):
                    for k in range(K):
                        g_.indirect_dma_start(out=buf, out_offset=bass.IndirectOffsetOnAxis(
                            ap=disp[:, par, i, k:k + 1], axis=0), in_=xn[:, par, i], in_offset=None,
                            bounds_check=E * CAP - 1, oob_is_err=False).then_inc(s_out, 16)

            if first:
                norm(0, 0)
                norm(1, 1)
                scatter(0, 0)
                with pool.Fori(1, NS // 2) as j:
                    for half in range(2):
                        norm((j, half), half)
                        scatter((j, half - 1), 1 - half)
                scatter(NS - 1, 1)
            else:
                run(pool, norm)
                pool.wait_ge(s_slot, 1)
                for tile in range(NB):
                    for k in range(K):
                        g_.indirect_dma_start(out=buf, out_offset=bass.IndirectOffsetOnAxis(
                            ap=disp[:, 0, tile, k:k + 1], axis=0), in_=xn[:, tile], in_offset=None,
                            bounds_check=E * CAP - 1, oob_is_err=False).then_inc(s_out, 16)
            pool.wait_ge(s_out, NB * K * 16)

        @block.scalar
        def _(act):
            def evac(g, par):
                act.wait_ge(s_tx, at(g, 1, 1))
                if begun(g, 2):
                    act.wait_ge(s_lg, at(g, 1, -1))
                nc.scalar.activation(xT[:, par], ps_x[:], ACT.Copy).then_inc(s_xT, 1)

            def exp(g, par):
                act.wait_ge(s_sh, at(g, 1, 1))
                nc.scalar.activation(pr[:], pr[:], ACT.Exp).then_inc(s_exp, 1)

            evac(0, 0)
            evac(1, 1)
            exp(0, 0)
            with act.Fori(1, NS // 2) as j:
                for half in range(2):
                    evac((j, half), half)
                    exp((j, half - 1), 1 - half)
            exp(NS - 1, 1)

        @block.tensor
        def _(pe):
            mm = nc.tensor.matmul

            def transposes(g, par):
                pe.wait_ge(s_xn, at(g, 1, 1))
                if begun(g, 1):
                    pe.wait_ge(s_xT, at(g, 1, 0))
                for c in range(DC):
                    for i in range(GT):
                        ins = nc.tensor.transpose(ps_x[:, c, i * P:(i + 1) * P],
                                                  (xn[:, par] if first else xs)[:, i, c * P:(c + 1) * P],
                                                  t.ident[:])
                ins.then_inc(s_tx, 1)

            def logits(g, par):
                pe.wait_ge(s_xT, at(g, 1, 1))
                if begun(g, 1):
                    pe.wait_ge(s_sh, at(g, 1, 0))
                for i in range(GT):
                    for c in range(DC):
                        ins = mm(ps_l[:, i], xT[:, par, c, i * P:(i + 1) * P], rw[:, c], start=c == 0, stop=c == DC - 1)
                ins.then_inc(s_lg, 1)

            def count(g, par):
                pe.wait_ge(s_cnt, at(g, 1, 1))
                if begun(g, 1):
                    pe.wait_ge(s_sel, at(g, 1, 0))
                for i in range(GT):
                    mm(ps_c[:, i], t.tri[:], cnt[:, i], start=True, stop=False)
                    if i:
                        mm(ps_c[:, i], t.ones_bf[:], cnt[:, 0], start=False, stop=False)
                    ins = mm(ps_c[:, i], t.ones_bf[:], acc[:], start=False, stop=True)
                ins.then_inc(s_pos, 1)

            pe.wait_ge(s_w, 16)
            transposes(0, 0)
            transposes(1, 1)
            logits(0, 0)
            count(0, 0)
            with pe.Fori(1, NS // 2) as j:
                for half in range(2):
                    transposes((j, half), half)
                    logits((j, half - 1), 1 - half)
                    count((j, half - 1), 1 - half)
            logits(NS - 1, 1)
            count(NS - 1, 1)
            if not first:
                pe.wait_ge(s_sel, NS)
                pe.wait_ge(s_cnt, NS + 1)
                mm(ps_c[:, 0, 0:E], t.ones_bf[:], acc[:, 0:E], start=True, stop=True).then_inc(s_tot, 1)

        @block.vector
        def _(ve):
            v_ = nc.vector
            links = {"n": 0, "g": 0, "per": 0}

            def link(ins):
                links["n"] += 1
                ins.then_inc(s_v, 1)
                ve.wait_ge(s_v, at(links["g"], links["per"], links["n"]))
                settle(ve)

            def norm(g, par):
                settle(ve)
                for i in range(GT):
                    ins = v_.bn_stats(stats[:, i], x_tile(g, i))
                ins.then_inc(s_st, 1)
                ve.wait_ge(s_st, at(g, 1, 1))
                settle(ve)
                for i in range(GT):
                    ins = v_.bn_aggr(mv[:, i], stats[:, i])
                ins.then_inc(s_mv, 1)
                ve.wait_ge(s_mv, at(g, 1, 1))
                if first and begun(g, 2):
                    ve.wait_ge(s_out, at(g, GT * K * 16, -GT * K * 16))
                if not first and begun(g, 1):
                    ve.wait_ge(s_tx, at(g, 1, 0))
                ve.wait_ge(s_rstd, at(g, 1, 1))
                for i in range(GT):
                    dst = xn[:, par, i] if first else xs[:, i]
                    ins = v_.tensor_scalar(dst, x_tile(g, i), mv[:, i, 0:1], rstd[:, i:i + 1], ALU.subtract, ALU.mult)
                ins.then_inc(s_xn, 1)
                if not first:
                    ve.wait_ge(s_xn, at(g, 1, 1))
                    v_.tensor_copy(tiles(xn, g), xs[:])

            def slots(pos_, idf_, over_, slot_, disp_, comb_, last):
                link(v_.tensor_scalar(over_, pos_, float(CAP), BIG, ALU.is_ge, ALU.mult))
                link(v_.scalar_tensor_tensor(out=slot_, in0=idf_, scalar=float(CAP), in1=pos_, op0=ALU.mult, op1=ALU.add))
                link(v_.tensor_tensor(over_, over_, slot_, ALU.add))
                v_.tensor_copy(disp_, over_)
                link(v_.tensor_scalar(pos_, pos_, float(CAP - 1), None, ALU.min))
                link(v_.scalar_tensor_tensor(out=slot_, in0=idf_, scalar=float(CAP), in1=pos_, op0=ALU.mult, op1=ALU.add))
                v_.tensor_copy(comb_, slot_).then_inc(last, 1)

            def choose(g, par):
                links.update(n=0, g=g, per=PER)
                ve.wait_ge(s_lg, at(g, 1, 1))
                link(v_.tensor_reduce(mx[:], ps_l[:], AX, ALU.max))
                v_.tensor_tensor(pr[:], ps_l[:], mx[:].unsqueeze(2).broadcast_to([P, GT, E]), ALU.subtract).then_inc(s_sh, 1)
                ve.wait_ge(s_exp, at(g, 1, 1))
                link(v_.tensor_reduce(z[:], pr[:], AX, ALU.add))
                link(v_.reciprocal(rz[:], z[:]))
                link(v_.tensor_tensor(pr[:], pr[:], rz[:].unsqueeze(2).broadcast_to([P, GT, E]), ALU.mult))
                for i in range(GT):
                    ins = v_.max(top[:, i], pr[:, i])
                link(ins)
                for i in range(GT):
                    ins = v_.max_index(ids[:, i], top[:, i], pr[:, i])
                link(ins)
                if first:
                    v_.tensor_scalar(tiles(t.prob0, g), top[:, :, 0:K], t.gate[:, 2:3], None, ALU.mult)
                else:
                    v_.tensor_copy(tiles(p_all, g), top[:, :, 0:K])
                link(v_.tensor_copy(idf[:], ids[:, :, 0:K]))
                ohf = oh[:].rearrange("p t k e -> p (t k) e")
                link(v_.tensor_tensor(ohf, t.iota[:, 0:E].unsqueeze(1).broadcast_to([P, GT * K, E]),
                                      idf[:].rearrange("p t k -> p (t k)").unsqueeze(2).broadcast_to([P, GT * K, E]), ALU.is_equal))
                if begun(g, 1):
                    ve.wait_ge(s_pos, at(g, 1, 0))
                    for i in range(GT):
                        link(v_.tensor_tensor(acc[:], acc[:], cnt[:, i], ALU.add))
                else:
                    for i in range(GT):
                        link(v_.memset(acc[:], 0.0))
                if first:
                    with nc.allow_low_precision("sums of at most K zeros and ones"):
                        v_.tensor_reduce(cnt[:], oh[:].rearrange("p t k e -> p t e k"), AX, ALU.add).then_inc(s_cnt, 1)
                else:
                    v_.tensor_copy(cnt[:], oh[:].rearrange("p t k e -> p t (k e)")).then_inc(s_cnt, 1)
                    v_.tensor_copy(tiles(oh2, g), oh[:, :, 1])
                    v_.tensor_copy(tiles(idf_all, g), idf[:])
                ve.wait_ge(s_pos, at(g, 1, 1))
                if first:
                    for i in range(GT):
                        ins = v_.tensor_tensor(sel[:, i], oh[:, i], ps_c[:, i].unsqueeze(1).broadcast_to([P, K, E]), ALU.mult)
                else:
                    ins = v_.tensor_tensor(sel[:].rearrange("p t k e -> p t (k e)"), oh[:].rearrange("p t k e -> p t (k e)"),
                                           ps_c[:], ALU.mult)
                ins.then_inc(s_sel, 1)
                ve.wait_ge(s_sel, at(g, 1, 1))
                dst = pos[:] if first else tiles(pos, g)
                link(v_.tensor_reduce(dst, sel[:], AX, ALU.add))
                if first:
                    if begun(g, 2):
                        ve.wait_ge(s_out, at(g, GT * K * 16, -GT * K * 16))
                    slots(pos[:], idf[:], over[:], slot[:], disp[:, par], tiles(t.comb0, g), s_slot)
                assert links["n"] == PER, links

            PER = (7 + GT + 1 + 5) + 1 if first else (7 + GT + 1) + 1

            norm(0, 0)
            norm(1, 1)
            choose(0, 0)
            with ve.Fori(1, NS // 2) as j:
                for half in range(2):
                    norm((j, half), half)
                    choose((j, half - 1), 1 - half)
            choose(NS - 1, 1)
            if not first:
                links.update(n=NS * PER, g=0, per=0)
                ve.wait_ge(s_pos, NS)
                for i in range(GT):
                    ins = v_.tensor_tensor(acc[:], acc[:], cnt[:, i], ALU.add)
                    if i < GT - 1:
                        link(ins)
                ins.then_inc(s_cnt, 1)
                ve.wait_ge(s_tot, 1)
                link(v_.tensor_copy(total[:], ps_c[:, 0, 0:E]))
                link(v_.tensor_tensor(oh2[:], oh2[:], total[:].unsqueeze(1).broadcast_to([P, NB, E]), ALU.mult))
                link(v_.tensor_reduce(add1[:], oh2[:], AX, ALU.add))
                link(v_.tensor_tensor(pos[:, :, 1], pos[:, :, 1], add1[:], ALU.add))
                link(v_.tensor_scalar(gates[:], pos[:], float(CAP), None, ALU.is_lt))
                link(v_.tensor_tensor(gates[:], gates[:], p_all[:], ALU.mult))
                link(v_.tensor_tensor(den[:], gates[:, :, 0], gates[:, :, 1], ALU.add))
                link(v_.tensor_scalar(den[:], den[:], 1e-9, None, ALU.max))
                link(v_.reciprocal(den[:], den[:]))
                link(v_.tensor_tensor(gates[:], gates[:], den[:].unsqueeze(2).broadcast_to([P, NB, K]), ALU.mult))
                v_.tensor_scalar(t.prob1[:], gates[:], t.gate[:, 3:4], None, ALU.mult)
                slots(pos[:], idf_all[:], over[:], slot[:], disp[:, 0], t.comb1[:], s_slot)


def experts(nc, t, d, layer):
    L = f"e{layer}_"
    first = layer == 0
    E, F, CAP = (E0, F0, CAP0) if first else (E1, F1, CAP1)
    FC = F // P
    NC = CAP // TOK
    EB = 4 if first else 2
    CB = EB * NC
    RB = 4 if first else 5
    UB = 2
    with ExitStack() as stack:
        m = Memory(nc, stack)
        w_in = m.sb(L + "w_in", [P, EB, DC, 2 * F])
        w_out = m.sb(L + "w_out", [P, EB, FC, D])
        rows = m.sb(L + "rows", [P, RB, GT, D])
        xT = m.sb(L + "xT", [P, UB, DC, TOK])
        act_ = m.sb(L + "act", [P, UB, FC, TOK])
        hT = m.sb(L + "hT", [P, UB, FC, TOK])
        y = m.sb(L + "y", [P, UB, GT, D])
        NHB = 1 if first else 2
        psX = [m.ps(L + f"psX{i}", [P, DC, TOK]) for i in range(2)]
        psH = [m.ps(L + f"psH{i}", [P, 2, TOK]) for i in range(UB if first else 4)]
        psY = [m.ps(L + f"psY{i}", [P, GT, D]) for i in range(2)]
        s_w = [m.sem(L + f"weights_loaded{i}") for i in range(EB)]
        s_r = [m.sem(L + f"rows_loaded{i}") for i in range(RB)]
        s_tx = m.sem(L + "transposed")
        s_xT = m.sem(L + "evacuated")
        s_h = m.sem(L + "hidden_ready")
        s_act = m.sem(L + "activated")
        s_hT = m.sem(L + "gated")
        s_y = m.sem(L + "output_ready")
        s_ye = m.sem(L + "output_evacuated")
        s_st = [m.sem(L + f"rows_stored{i}") for i in range(2)]
        block = stack.enter_context(nc.Block())
        buf, yd = d[f"buf{layer}"], d[f"y{layer}"]
        win, wout = (d["L0_ffn_w1"], d["L0_ffn_w2"]) if first else (d["L1_ffn_W_in"], d["L1_ffn_W_out"])
        NCH = E * NC
        NIT = E // EB

        def n_at(it, per, k):
            return it * per + k

        def each(eng, body):
            body(0, True)
            with eng.Fori(1, NIT) as it:
                body(it, False)

        @block.sync
        def _(sp):
            def body(it, fresh):
                for c in range(CB):
                    e, s = c // NC, c % NC
                    if s == 0:
                        if not fresh:
                            sp.wait_ge(s_y, it * CB + (c + NC - CB))
                        ex = e if fresh else it * EB + e
                        w1 = win[ex] if fresh else win[bass.ds(ex, 1)].rearrange("o k n -> (o k) n")
                        w2 = wout[ex] if fresh else wout[bass.ds(ex, 1)].rearrange("o k n -> (o k) n")
                        sp.dma_start(w_in[:, e], w1.rearrange("(c p) n -> p c n", p=P)).then_inc(s_w[e], 16)
                        sp.dma_start(w_out[:, e], w2.rearrange("(c p) n -> p c n", p=P)).then_inc(s_w[e], 16)
                    if not (fresh and c < RB):
                        sp.wait_ge(s_tx, (c if fresh else it * CB + c) - RB + 1)
                    r0 = c * TOK if fresh else it * (CB * TOK) + c * TOK
                    sp.dma_start(rows[:, c % RB], buf[bass.ds(r0, TOK) if not fresh else slice(r0, r0 + TOK)]
                                 .rearrange("(i p) n -> p i n", p=P)).then_inc(s_r[c % RB], 16)
            each(sp, body)

        RPI = CB // RB

        @block.tensor
        def _(pe):
            mm = nc.tensor.matmul

            def val(it, n):
                return it * CB + n

            def transposes(it, c, skip):
                pe.wait_ge(s_r[c % RB], (it * RPI + c // RB + 1) * 16)
                if not skip(2):
                    pe.wait_ge(s_xT, val(it, c - 1))
                for k in range(DC):
                    for i in range(GT):
                        ins = nc.tensor.transpose(psX[c % 2][:, k, i * P:(i + 1) * P], rows[:, c % RB, i, k * P:(k + 1) * P],
                                                  t.ident[:])
                ins.then_inc(s_tx, 1)

            def hidden(it, c, skip):
                e = c // NC
                if c % NC == 0:
                    pe.wait_ge(s_w[e], (it + 1) * 32)
                pe.wait_ge(s_xT, val(it, c + 1))
                for f in range(2 * FC):
                    if first:
                        if f == 0 and not skip(2):
                            pe.wait_ge(s_hT, val(it, c - 1))
                        dst = psH[c % 2][:, f]
                    else:
                        if f == 0 and not skip(1):
                            pe.wait_ge(s_act, val(it, c))
                        if f == FC and not skip(1):
                            pe.wait_ge(s_hT, val(it, c))
                        dst = psH[f // 2][:, f % 2]
                    for k in range(DC):
                        ins = mm(dst, w_in[:, e, k, f * P:(f + 1) * P], xT[:, c % 2, k], start=k == 0, stop=k == DC - 1)
                    if f in (FC - 1, 2 * FC - 1):
                        ins.then_inc(s_h, 1)

            def output(it, c, skip):
                e = c // NC
                pe.wait_ge(s_hT, val(it, c + 1))
                if not skip(2):
                    pe.wait_ge(s_ye, val(it, c - 1))
                for i in range(GT):
                    for f in range(FC):
                        ins = mm(psY[c % 2][:, i], hT[:, c % 2, f, i * P:(i + 1) * P], w_out[:, e, f], start=f == 0, stop=f == FC - 1)
                ins.then_inc(s_y, 1)

            def body(it, fresh):
                for c in range(CB):
                    n = lambda lag, c=c: (lambda back: fresh and c - lag < back)
                    transposes(it, c, n(0))
                    if not fresh or c >= 1:
                        hidden(*((it, c - 1) if c else (it - 1, CB - 1)), n(1))
                    if not fresh or c >= 2:
                        output(*((it, c - 2) if c >= 2 else (it - 1, CB + c - 2)), n(2))
            each(pe, body)
            no = lambda back: False
            output(NIT - 1, CB - 2, no)
            hidden(NIT - 1, CB - 1, no)
            output(NIT - 1, CB - 1, no)

        @block.scalar
        def _(act):
            a = nc.scalar

            def body(it, fresh):
                for c in range(CB):
                    act.wait_ge(s_tx, it * CB + c + 1)
                    if not (fresh and c < 2):
                        act.wait_ge(s_h, it * (2 * CB) + 2 * (c - 1))
                    a.activation(xT[:, c % 2], psX[c % 2][:], ACT.Copy).then_inc(s_xT, 1)
                    if not fresh or c >= 1:
                        activate(it, c - 1, fresh and c <= 2)
            def activate(it, c, fresh2):
                p = c % 2
                act.wait_ge(s_h, it * (2 * CB) + 2 * c + (2 if first else 1))
                if not fresh2:
                    act.wait_ge(s_hT, it * CB + c - 1)
                if first:
                    a.activation(act_[:, p, 0], psH[p][:, 0], ACT.Silu).then_inc(s_act, 1)
                else:
                    for b in range(2):
                        ins = a.activation(act_[:, p, 2 * b:2 * b + 2], psH[b][:], ACT.Gelu)
                    ins.then_inc(s_act, 1)
            each(act, body)
            activate(NIT, -1, False)

        @block.vector
        def _(ve):
            v_ = nc.vector

            def gate(it, c, fresh2):
                p = c % 2
                ve.wait_ge(s_act, it * CB + c + 1)
                ve.wait_ge(s_h, it * (2 * CB) + 2 * c + 2)
                if not fresh2:
                    ve.wait_ge(s_y, it * CB + c - 1)
                if first:
                    v_.tensor_tensor(hT[:, p, 0], act_[:, p, 0], psH[p][:, 1], ALU.mult).then_inc(s_hT, 1)
                else:
                    for b in range(2):
                        ins = v_.tensor_tensor(hT[:, p, 2 * b:2 * b + 2], act_[:, p, 2 * b:2 * b + 2], psH[2 + b][:], ALU.mult)
                    ins.then_inc(s_hT, 1)

            def out(it, c, fresh2):
                ve.wait_ge(s_y, it * CB + c + 1)
                if not fresh2:
                    ve.wait_ge(s_st[c % 2], it * (CB * 8) + (c // 2) * 16)
                v_.tensor_copy(y[:, c % 2], psY[c % 2][:]).then_inc(s_ye, 1)

            def body(it, fresh):
                for c in range(CB):
                    gate(it, c, fresh and c < 2)
                    if not fresh or c >= 1:
                        out(it, c - 1, fresh and c <= 2)
            each(ve, body)
            out(NIT, -1, False)

        @block.gpsimd
        def _(pool):
            def body(it, fresh):
                for c in range(CB):
                    r0 = c * TOK if fresh else it * (CB * TOK) + c * TOK
                    pool.wait_ge(s_ye, it * CB + c + 1)
                    settle_(pool)
                    pool.dma_start(yd[bass.ds(r0, TOK) if not fresh else slice(r0, r0 + TOK)]
                                   .rearrange("(i p) n -> p i n", p=P), y[:, c % 2]).then_inc(s_st[c % 2], 16)

            def settle_(eng):
                eng.sem_inc(t.s_passed, 1)
            each(pool, body)
            for i in range(2):
                pool.wait_ge(s_st[i], NCH // 2 * 16)


def combine(nc, t, d):
    with ExitStack() as stack:
        m = Memory(nc, stack)
        RB = 4
        rows = m.sb("c_rows", [P, RB, K1, D])
        s_row = [m.sem(f"c_rows_gathered{i}") for i in range(RB)]
        s_acc = m.sem("c_row_added")
        s_out = m.sem("c_stored")
        block = stack.enter_context(nc.Block())

        @block.gpsimd
        def _(pool):
            for tile in range(NB):
                if tile >= RB:
                    pool.wait_ge(s_acc, K1 * (tile - RB + 1))
                for k in range(K1):
                    nc.gpsimd.indirect_dma_start(out=rows[:, tile % RB, k], out_offset=None, in_=d["y1"],
                                                 in_offset=bass.IndirectOffsetOnAxis(ap=t.comb1[:, tile, k:k + 1], axis=0)
                                                 ).then_inc(s_row[tile % RB], 16)

        @block.vector
        def _(ve):
            for tile in range(NB):
                ve.wait_ge(s_row[tile % RB], 16 * K1 * (tile // RB + 1))
                for k in range(K1):
                    if k:
                        ve.wait_ge(s_acc, K1 * tile + k)
                    nc.vector.scalar_tensor_tensor(out=t.x[:, tile], in0=rows[:, tile % RB, k], scalar=t.prob1[:, tile, k:k + 1],
                                                   in1=t.x[:, tile], op0=ALU.mult, op1=ALU.add).then_inc(s_acc, 1)

        @block.sync
        def _(sp):
            for tile in range(NB):
                sp.wait_ge(s_acc, K1 * (tile + 1))
                sp.dma_start(d["out"][tile], t.x[:, tile]).then_inc(s_out, 16)
            sp.wait_ge(s_out, 16 * NB)


class Resident:
    pass


def program(nc, d):
    with ExitStack() as stack:
        m = Memory(nc, stack)
        t = Resident()
        t.x = m.sb("x_all", [P, NB, D])
        t.ident = m.sb("ident", [P, P])
        t.tri = m.sb("tri", [P, P], BF16)
        t.ones_bf = m.sb("ones_bf", [P, P], BF16)
        t.iota = m.sb("iota", [P, E0])
        t.minus_half = m.sb("minus_half", [P, 2 * GT])
        t.zeros = m.sb("zeros", [P, 2048])
        t.gate = m.sb("gate", [P, 4])
        t.affine = m.sb("affine", [P, 4, DC])
        t.bias = m.sb("bias", [P, H, P])
        t.bo = m.sb("bo", [P, 2, D])
        t.comb0 = m.sb("comb0", [P, NB, K0], I32)
        t.prob0 = m.sb("prob0", [P, NB, K0])
        t.comb1 = m.sb("comb1", [P, NB, K1], I32)
        t.prob1 = m.sb("prob1", [P, NB, K1])
        t.s_passed = m.sem("waits_passed")
        for layer, n in ((0, E0 * CAP0), (1, E1 * CAP1)):
            d[f"buf{layer}"] = nc.dram_tensor(f"buf{layer}", [n, D], F32).ap()
            d[f"y{layer}"] = nc.dram_tensor(f"y{layer}", [n, D], F32).ap()
        for phase in PHASES:
            if phase == "setup":
                setup(nc, t, d)
            elif phase == "combine":
                combine(nc, t, d)
            else:
                {"attention": attention, "routing": routing, "experts": experts}[phase[:-1]](nc, t, d, int(phase[-1]))


PHASES = ("setup", "attention0", "routing0", "experts0", "attention1", "routing1", "experts1", "combine")

_INS = ["x", "ctx_1024", "fside_SxS2_0", "g_xattn", "g_ffn", "L0_xattn_W_q", "L0_xattn_W_k", "L0_xattn_W_v",
        "L0_xattn_W_out", "L0_xattn_b_out", "L0_ffn_router_w", "L0_ffn_w1", "L0_ffn_w2", "L1_xattn_ln_l_w",
        "L1_xattn_ln_l_b", "L1_xattn_ln_c_w", "L1_xattn_ln_c_b", "L1_xattn_Wq", "L1_xattn_Wkv", "L1_xattn_Wo",
        "L1_xattn_bo", "L1_ffn_Wg", "L1_ffn_W_in", "L1_ffn_W_out"]


def kernel(**inputs):
    import numpy as np
    import concourse.bacc as bacc
    from concourse.bass_utils import run_bass_kernel_spmd

    nc = bacc.Bacc("TRN2", target_bir_lowering=False, num_devices=1)
    arrays, d = {}, {}
    for name in _INS:
        a = np.ascontiguousarray(inputs[name])
        arrays[f"in_{name}"] = a
        d[name] = nc.dram_tensor(f"in_{name}", a.shape, mybir.dt.from_np(a.dtype), kind="ExternalInput").ap()
    d["out"] = nc.dram_tensor("out_x", (NB, P, D), F32, kind="ExternalOutput").ap()
    program(nc, d)
    result = run_bass_kernel_spmd(nc, [arrays], core_ids=[0])
    return result.results[0]["out_x"]
```

```python
from contextlib import ExitStack

import concourse.bass as bass
from concourse import mybir

F32 = mybir.dt.float32
BF16 = mybir.dt.bfloat16
I32 = mybir.dt.int32
U32 = mybir.dt.uint32
ACT = mybir.ActivationFunctionType
ALU = mybir.AluOpType
AX = mybir.AxisListType.X

P = 128
NB = 32
D = 256
DC = D // P
H = 16
DH = 64
INNER = H * DH
HP = H // 2
GT = 2
NG = NB // GT
TOK = GT * P
HU = 4
UT = H // HU
UG = GT * UT
NU = NG * UG
EPS = 1e-5
SCALE = DH ** -0.5
CLIP = 11.0
BIG = 65536.0

E0, K0, F0, CAP0 = 64, 4, 128, 256
E1, K1, F1, CAP1 = 8, 2, 512, 1280
ROWS0, ROWS1 = E0 * CAP0, 2 * E1 * CAP1


def plus(g, n):
    return g + n if isinstance(g, int) else (g[0], g[1] + n)


def begun(g, n):
    return not isinstance(g, int) or g >= n


def at(g, per, k):
    if isinstance(g, int):
        return g * per + k
    reg, half = g
    return reg * (2 * per) + (half * per + k)


class Memory:

    def __init__(self, nc, stack):
        self.nc, self.stack = nc, stack

    def sb(self, name, shape, dt=F32):
        return self.stack.enter_context(self.nc.sbuf_tensor(name, shape, dt))

    def ps(self, name, shape, dt=F32):
        return self.stack.enter_context(self.nc.psum_tensor(name, shape, dt))

    def sem(self, name):
        return self.stack.enter_context(self.nc.semaphore(name))


def row_vector(ap, n):
    return ap.rearrange("(o n) -> o n", o=1).broadcast_to([P, n])


def setup(nc, t, d):
    with ExitStack() as stack:
        m = Memory(nc, stack)
        raw = m.sb("raw_gates", [P, 4])
        bo = m.sb("bo_raw", [P, 2, D])
        s_load = m.sem("setup_loaded")
        s_const = m.sem("setup_constants")
        s_tanh = m.sem("setup_tanh")
        s_v = m.sem("setup_vector")
        block = stack.enter_context(nc.Block())
        loads = 4

        @block.sync
        def _(sp):
            sp.dma_start(t.x[:, 0:2 * GT], d["x"][0:2 * GT].rearrange("b p d -> p b d")).then_inc(t.s_xl[0], 16)
            sp.dma_start(raw[:, 0:2], row_vector(d["g_xattn"], 2)).then_inc(s_load, 16)
            sp.dma_start(raw[:, 2:4], row_vector(d["g_ffn"], 2)).then_inc(s_load, 16)
            sp.dma_start(bo[:, 0, :], row_vector(d["L0_xattn_b_out"], D)).then_inc(s_load, 16)
            sp.dma_start(bo[:, 1, :], row_vector(d["L1_xattn_bo"], D)).then_inc(s_load, 16)
            sp.wait_ge(s_load, 16 * loads)

        @block.gpsimd
        def _(pool):
            g = nc.gpsimd
            g.memset(t.ident[:], 0.0).then_inc(s_const, 1)
            g.memset(t.tri[:], 1.0).then_inc(s_const, 1)
            g.memset(t.ones_bf[:], 1.0).then_inc(s_const, 1)
            g.memset(t.minus_half[:], -0.5).then_inc(s_const, 1)
            pool.wait_ge(s_const, 4)
            g.affine_select(out=t.ident[:], in_=t.ident[:], compare_op=ALU.not_equal, fill=1.0, base=0,
                            pattern=[[-1, P]], channel_multiplier=1).then_inc(s_const, 1)
            g.affine_select(out=t.tri[:], in_=t.tri[:], compare_op=ALU.is_gt, fill=0.0, base=0,
                            pattern=[[1, P]], channel_multiplier=-1).then_inc(s_const, 1)
            g.iota(t.iota[:], pattern=[[1, E0]], base=0, channel_multiplier=0,
                   allow_small_or_imprecise_dtypes=True).then_inc(s_const, 1)
            pool.wait_ge(s_const, 7)
            g.memset(t.kz[DH:P, :, :, 0], 0.0).then_inc(s_const, 1)
            pool.wait_ge(s_const, 8)

        @block.scalar
        def _(act):
            act.wait_ge(s_load, 16 * loads)
            nc.scalar.activation(t.gate[:], raw[:], ACT.Tanh).then_inc(s_tanh, 1)
            act.wait_ge(s_tanh, 1)

        @block.vector
        def _(v):
            nc.vector.memset(t.kz[0:DH, :, :, 1], 0.0).then_inc(s_v, 1)
            v.wait_ge(s_load, 16 * loads)
            v.wait_ge(s_tanh, 1)
            for i in range(2):
                nc.vector.tensor_scalar(t.bo[:, i, :], bo[:, i, :], t.gate[:, i:i + 1], None, ALU.mult).then_inc(s_v, 1)
            v.wait_ge(s_v, 3)


def attention(nc, t, d, layer):
    L = f"a{layer}_"
    first = layer == 0
    with ExitStack() as stack:
        m = Memory(nc, stack)
        wq = m.sb(L + "wq", [P, DC, INNER])
        wk = m.sb(L + "wk", [P, DC, INNER])
        wv = m.sb(L + "wv", [P, DC, INNER])
        wo = m.sb(L + "wo", [P, HP, D])
        ctx = m.sb(L + "ctx", [P, GT, D])
        xn = m.sb(L + "xn", [P, GT, D])
        xT = m.sb(L + "xT", [P, DC, TOK])
        cT = m.sb(L + "cT", [P, 2, DC, TOK])
        qT = m.sb(L + "qT", [P, 2, HP, TOK])
        kz = t.kz
        v = m.sb(L + "v", [P, 2, GT, INNER])
        S = m.sb(L + "S", [P, 4, HU, P])
        PT = m.sb(L + "PT", [P, 2, HU, P])
        oT = m.sb(L + "oT", [P, HP, P])
        stats = m.sb(L + "stats", [P, GT, 6])
        mv = m.sb(L + "mv", [P, GT, 2])
        var_eps = m.sb(L + "var_eps", [P, GT])
        rstd = m.sb(L + "rstd", [P, GT])
        mx = m.sb(L + "mx", [P, 2, HU])
        z = m.sb(L + "z", [P, 2, HU])
        rz = m.sb(L + "rz", [P, 2, HU])
        psP = [m.ps(L + f"psP{i}", [P, 512]) for i in range(2)]
        psS = [m.ps(L + f"psS{i}", [P, HU, P]) for i in range(2)]
        psT = [m.ps(L + f"psT{i}", [P, HU, P]) for i in range(2)]
        psV = m.ps(L + "psV", [P, 4, P])
        psM = m.ps(L + "psM", [P, 2, TOK])

        s_w = {w: m.sem(L + f"w_{w}_loaded") for w in ("k", "v", "q")}
        s_ctx = m.sem(L + "context_loaded")
        s_mv = m.sem(L + "stats_then_moments_ready")
        s_ve = m.sem(L + "variance_shifted")
        s_rstd = m.sem(L + "rstd_ready")
        s_xn = m.sem(L + "normed")
        s_tx = m.sem(L + "x_transposed")
        s_tc = m.sem(L + "context_transposed")
        s_xT = m.sem(L + "x_transposes_evacuated")
        s_cT = m.sem(L + "context_transposes_evacuated")
        s_pj = m.sem(L + "projected")
        s_ev = [m.sem(L + f"projection_evacuated{i}") for i in range(2)]
        s_sc = m.sem(L + "scores_ready")
        s_read = m.sem(L + "scores_read")
        s_exp = m.sem(L + "exp_ready")
        s_rz = m.sem(L + "sum_then_inverse_ready")
        s_norm = m.sem(L + "probs_normed")
        s_tr = m.sem(L + "probs_transposed")
        s_PT = m.sem(L + "probs_evacuated")
        s_pv = m.sem(L + "values_weighted")
        s_oT = m.sem(L + "heads_evacuated")
        s_wo = m.sem(L + "output_projected")
        s_bo = m.sem(L + "output_bias_added")
        s_x = m.sem(L + "x_updated")
        if not first:
            idx = m.sb(L + "idx", [P, GT * K0], I32)
            rows = m.sb(L + "rows", [P, GT * K0, D])
            cn = m.sb(L + "cn", [P, GT, D])
            s_ix = m.sem(L + "indices_copied")
            s_row = [m.sem(L + f"rows_gathered{i}") for i in range(2)]
            s_acc = m.sem(L + "row_added")
            s_xn1 = m.sem(L + "normed_once")
            s_cn = m.sem(L + "context_normed")
            cstats = m.sb(L + "cstats", [P, GT, 6])
            cmv = m.sb(L + "cmv", [P, GT, 2])
            cve = m.sb(L + "cve", [P, GT])
            crs = m.sb(L + "crs", [P, GT])
            s_cmv = m.sem(L + "context_stats_then_moments_ready")
            s_cve = m.sem(L + "context_variance_shifted")
            s_crs = m.sem(L + "context_rstd_ready")
        else:
            zeros = m.sb(L + "zeros", [P, 512])
            s_zs = m.sem(L + "zeros_made")
            s_max = m.sem(L + "max_ready")
            s_sub = m.sem(L + "max_subtracted")
            s_zero = [m.sem(L + f"buffer_{i}_cleared") for i in range(2)]
        E, K, CAP = (E0, K0, CAP0) if first else (E1, K1, CAP1)
        CW = E if first else K * E
        EW = P
        rw = m.sb(L + "rw", [P, DC, EW])
        rxn = m.sb(L + "rxn", [P, 2, GT, D])
        rxT = m.sb(L + "rxT", [P, DC, TOK])
        rstats = m.sb(L + "rstats", [P, GT, 6])
        rmv = m.sb(L + "rmv", [P, GT, 2])
        rve = m.sb(L + "rve", [P, GT])
        rrs = m.sb(L + "rrs", [P, GT])
        rmx = m.sb(L + "rmx", [P, GT])
        pr = m.sb(L + "pr", [P, GT, E])
        rzs = m.sb(L + "rzs", [P, GT])
        rrz = m.sb(L + "rrz", [P, GT])
        top = m.sb(L + "top", [P, GT, 8])
        ids = m.sb(L + "ids", [P, GT, 8], U32)
        idf = m.sb(L + "idf", [P, GT, K])
        oh = m.sb(L + "oh", [P, GT, K, E])
        sel = m.sb(L + "sel", [P, GT, K, E])
        pos = m.sb(L + "pos", [P, GT, K])
        over = m.sb(L + "over", [P, GT, K])
        slot = m.sb(L + "slot", [P, GT, K])
        disp = m.sb(L + "disp", [P, 2, GT, K], I32)
        s_late = m.sem(L + "w_out_and_router_loaded")
        s_rwz = m.sem(L + "router_padded")
        s_v = m.sem(L + "routing_chain")
        s_rmv = m.sem(L + "routing_stats_then_moments_ready")
        s_rve = m.sem(L + "routing_variance_shifted")
        s_rrs = m.sem(L + "routing_rstd_ready")
        s_rxn = m.sem(L + "routing_normed")
        s_rtx = m.sem(L + "routing_transposed")
        s_rxT = m.sem(L + "routing_evacuated")
        s_lg = m.sem(L + "logits_ready")
        s_sh = m.sem(L + "logits_shifted")
        s_re = m.sem(L + "routing_exp_ready")
        s_cnt = m.sem(L + "choices_ready")
        s_pos = m.sem(L + "positions_ready")
        s_sel = m.sem(L + "positions_read")
        s_slot = m.sem(L + "slots_ready")
        s_out = [m.sem(L + f"rows_scattered{i}") for i in range(2)]
        buf = d[f"buf{layer}"]
        block = stack.enter_context(nc.Block())

        JOBS = [("k", i) for i in range(4)] + [("v", i) for i in range(4)] + [("q", i) for i in range(4)]
        NJ = len(JOBS)
        OF_STEP = [[0, 1], [2], [3, 4], [5], [6, 7], [8], [9, 10], [11]]
        XT_STEP, CT_STEP = 1, 5
        PEEL = 4

        OUT = GT * K * 16

        def outs(g):
            return g // 2 * OUT if isinstance(g, int) else g[0] * OUT + g[1] // 2 * OUT

        def tiles(ap, g):
            return ap[:, g * GT:(g + 1) * GT] if isinstance(g, int) else ap[:, bass.ds(at(g, GT, 0), GT)]

        def has(g, u, lag):
            return not isinstance(g, int) or 0 <= g * UG + u - lag < NU

        def routed(g, lag):
            return not isinstance(g, int) or 0 <= g - lag < NG

        def has_group(g, n):
            return not isinstance(g, int) or g + n < NG

        def settle(eng):
            eng.sem_inc(t.s_passed, 1)

        def run(eng, step, before):
            before()
            for g in range(PEEL):
                for u in range(UG):
                    step(g, u, g % 2, True, True)
            with eng.Fori(PEEL // 2, NG // 2 - 2) as j:
                for half in range(2):
                    for u in range(UG):
                        step((j, half), u, half, True, True)
            for g in (NG - 4, NG - 3):
                for u in range(UG):
                    step(g, u, g % 2, True, True)
            for u in range(UG):
                step(NG - 2, u, 0, True, False)
            for u in range(UG):
                step(NG - 1, u, 1, False, False)
            for g in (NG, NG + 1):
                for u in range(UG):
                    step(g, u, g % 2, False, False)

        def x_tile(g, i):
            if isinstance(g, int):
                return t.x[:, g * GT + i, :]
            return t.x[:, bass.ds(at(g, GT, i), 1), :].rearrange("p a d -> p (a d)")

        def wait_ctx(eng, g):
            eng.wait_ge(s_ctx, at(g, 16, 16))

        @block.sync
        def _(sp):
            W = {"q": (wq, "L0_xattn_W_q" if first else "L1_xattn_Wq", 0),
                 "k": (wk, "L0_xattn_W_k" if first else "L1_xattn_Wkv", 0),
                 "v": (wv, "L0_xattn_W_v" if first else "L1_xattn_Wkv", 0 if first else INNER)}

            def load_w(kind):
                w, name, off = W[kind]
                sp.dma_start(w[:], d[name][:, off:off + INNER].rearrange("(c p) n -> p c n", p=P)).then_inc(s_w[kind], 16)

            def load_ctx(g):
                if begun(g, 1):
                    if first:
                        sp.wait_ge(s_tc, at(g, 1, 0))
                    else:
                        sp.wait_ge(s_cn, at(g, GT, 0))
                src = d["ctx_1024"][g * GT:(g + 1) * GT] if isinstance(g, int) else d["ctx_1024"][bass.ds(at(g, GT, 0), GT)]
                sp.dma_start(ctx[:], src.rearrange("b p d -> p b d")).then_inc(s_ctx, 16)

            load_ctx(0)
            load_w("k")
            load_w("v")
            load_w("q")
            load_ctx(1)
            if first:
                sp.dma_start(t.side[:], d["fside_SxS2_0"]).then_inc(t.s_vec, 16)
                for i, name in enumerate(("L1_xattn_ln_l_w", "L1_xattn_ln_l_b", "L1_xattn_ln_c_w", "L1_xattn_ln_c_b")):
                    with nc.allow_non_contiguous_dma("256 numbers, one column each"):
                        sp.dma_start(t.affine[:, i, :], d[name].rearrange("(c p) -> p c", p=P)).then_inc(t.s_vec, 16)
            sp.dma_start(wo[:], d["L0_xattn_W_out" if first else "L1_xattn_Wo"].rearrange("(c p) n -> p c n", p=P)
                         ).then_inc(s_late, 16)
            if first:
                sp.dma_start(t.x[:, 2 * GT:NB], d["x"][2 * GT:NB].rearrange("b p d -> p b d")).then_inc(t.s_xl[1], 16)
            sp.wait_ge(s_rwz, 1)
            sp.dma_start(rw[:, :, 0:E], d["L0_ffn_router_w" if first else "L1_ffn_Wg"].rearrange("(c p) e -> p c e", p=P)
                         ).then_inc(s_late, 16)
            def clear(n):
                layer, part = divmod(n, 2 * UG)
                dst = d[f"buf{layer}"].rearrange("(p r) d -> p (r d)", p=P).rearrange("p (n z) -> p n z", z=zeros.shape[1])
                per = dst.shape[1] // (2 * UG)
                sp.dma_start(dst[:, part * per:(part + 1) * per], zeros[:].unsqueeze(1).broadcast_to([P, per, zeros.shape[1]])
                             ).then_inc(s_zero[layer], 16)

            load_ctx(2)
            if first:
                sp.wait_ge(s_zs, 1)
                for g in range(PEEL):
                    for u in range(UG):
                        sp.wait_ge(s_sc, at(g, UG, u + 1))
                        clear(g * UG + u)
                    load_ctx(g + 3)
                for i in range(2):
                    sp.wait_ge(s_zero[i], 16 * 2 * UG)
            for g in range(PEEL + 3 if first else 3, 2 * PEEL):
                load_ctx(g)
            with sp.Fori(PEEL, NG // 2) as j:
                for half in range(2):
                    load_ctx((j, half))

        @block.gpsimd
        def _(pool):
            g_ = nc.gpsimd
            NR = 1 if first else 2

            def rstd_of(g, r):
                pool.wait_ge(s_mv, at(g, 2 * NR, 2 * r + 2))
                if r == 0 and begun(g, 1):
                    pool.wait_ge(s_xn, at(g, 1, 0))
                settle(pool)
                g_.tensor_scalar(var_eps[:], mv[:, :, 1], EPS, None, ALU.add).then_inc(s_ve, 1)
                pool.wait_ge(s_ve, at(g, NR, r + 1))
                g_.tensor_tensor(rstd[:], var_eps[:], t.minus_half[:], ALU.pow).then_inc(s_rstd, 1)

            def context_rstd(g):
                pool.wait_ge(s_cmv, at(g, 2, 2))
                if begun(g, 1):
                    pool.wait_ge(s_cn, at(g, GT, 0))
                settle(pool)
                g_.tensor_scalar(cve[:], cmv[:, :, 1], EPS, None, ALU.add).then_inc(s_cve, 1)
                pool.wait_ge(s_cve, at(g, 1, 1))
                g_.tensor_tensor(crs[:], cve[:], t.minus_half[:], ALU.pow).then_inc(s_crs, 1)

            def route_rstd(g):
                pool.wait_ge(s_rmv, at(g, 2, 2))
                if begun(g, 1):
                    pool.wait_ge(s_rxn, at(g, 1, 0))
                settle(pool)
                g_.tensor_scalar(rve[:], rmv[:, :, 1], EPS, None, ALU.add).then_inc(s_rve, 1)
                pool.wait_ge(s_rve, at(g, 1, 1))
                g_.tensor_tensor(rrs[:], rve[:], t.minus_half[:], ALU.pow).then_inc(s_rrs, 1)

            def scatter(g, par, part):
                if part == 0:
                    pool.wait_ge(s_slot, at(g, 1, 1))
                    if isinstance(g, int) and g == 0 and first:
                        pool.wait_ge(s_zero[0], 16 * 2 * UG)
                    settle(pool)
                for n in range(part * 2, part * 2 + 2):
                    i, k = n // K, n % K
                    g_.indirect_dma_start(out=buf, out_offset=bass.IndirectOffsetOnAxis(
                        ap=disp[:, par, i, k:k + 1], axis=0), in_=rxn[:, par, i], in_offset=None,
                        bounds_check=buf.shape[0] - 1, oob_is_err=False).then_inc(s_out[par], 16)

            def gather(g, part):
                if part == 0:
                    pool.wait_ge(s_ix, at(g, 1, 1))
                if begun(g, 1):
                    pool.wait_ge(s_acc, at(g, GT * K0, GT * (part + 1) - GT * K0))
                settle(pool)
                for i in range(GT):
                    n = part * GT + i
                    g_.indirect_dma_start(out=rows[:, n, :], out_offset=None, in_=d["y0"],
                                          in_offset=bass.IndirectOffsetOnAxis(ap=idx[:, n:n + 1], axis=0)
                                          ).then_inc(s_row[part // 2], 16)

            def step(g, u, par, proj, prep):
                if has(g, u, 1):
                    pool.wait_ge(s_rz, at(g, 2 * UG, 2 * u))
                    s = S[:, (u - 1) % 4]
                    g_.tensor_tensor(s, s, rz[:, (u - 1) % 2, :].unsqueeze(2).broadcast_to([P, HU, P]), ALU.mult
                                     ).then_inc(s_norm, 1)
                if first and has(g, u, 0):
                    pool.wait_ge(s_max, at(g, UG, u + 1))
                    s = S[:, u % 4]
                    g_.tensor_tensor(s, s, mx[:, u % 2, :].unsqueeze(2).broadcast_to([P, HU, P]), ALU.subtract
                                     ).then_inc(s_sub, 1)
                if u == 3 and routed(g, 1):
                    route_rstd(plus(g, -1))
                if 4 <= u < 4 + GT * K // 2 and routed(g, 2):
                    scatter(plus(g, -2), par, u - 4)
                if not first:
                    if u >= 6 and has_group(g, 3):
                        gather(plus(g, 3), u - 6)
                    if u < 2 and begun(g, 1) and has_group(g, 2):
                        gather(plus(g, 2), u + 2)
                    if u == 3 and prep:
                        context_rstd(plus(g, 2))
                    if u == 7 and prep:
                        rstd_of(plus(g, 2), 1)
                if u == 6 and prep:
                    rstd_of(plus(g, 2), 0)

            def before():
                g_.memset(rw[:], 0.0).then_inc(s_rwz, 1)
                if first:
                    g_.memset(zeros[:], 0.0).then_inc(s_zs, 1)
                    rstd_of(0, 0)
                    rstd_of(1, 0)
                    return
                gather(0, 0)
                context_rstd(0)
                for part in range(1, 4):
                    gather(0, part)
                context_rstd(1)
                rstd_of(0, 0)
                rstd_of(0, 1)
                for part in range(4):
                    gather(1, part)
                rstd_of(1, 0)
                rstd_of(1, 1)
                for part in range(4):
                    gather(2, part)

            run(pool, step, before)
            for i in range(2):
                pool.wait_ge(s_out[i], NG // 2 * OUT)

        @block.scalar
        def _(act):
            a = nc.scalar

            def evac_in(src, dst, row, done):
                if first:
                    a.activation(dst, src, ACT.Copy).then_inc(done, 1)
                else:
                    for c in range(DC):
                        ins = a.activation(dst[:, c], src[:, c], ACT.Identity,
                                           bias=t.affine[:, row + 1, c:c + 1], scale=t.affine[:, row, c:c + 1])
                    ins.then_inc(done, 1)

            def evac_x(g):
                act.wait_ge(s_tx, at(g, 1, 1))
                if begun(g, 1):
                    act.wait_ge(s_pj, at(g, NJ, 0))
                evac_in(psM[:], xT[:], 0, s_xT)

            def evac_ctx(g, par):
                act.wait_ge(s_tc, at(g, 1, 1))
                if begun(g, 2):
                    act.wait_ge(s_pj, at(g, NJ, 8 - 2 * NJ))
                evac_in(psM[:], cT[:, par], 2, s_cT)

            def evac_job(g, par, j):
                kind, i = JOBS[j]
                if kind == "k":
                    return
                act.wait_ge(s_pj, at(g, NJ, j + 1))
                if begun(g, 2) and j == 8:
                    act.wait_ge(s_sc, at(g, UG, -UG))
                if begun(g, 2) and j == 4:
                    act.wait_ge(s_pv, at(g, UG, -UG))
                if kind == "q":
                    ins = a.activation(qT[:, par, 2 * i:2 * i + 2], psP[j % 2][:].rearrange("p (c n) -> p c n", c=2),
                                       ACT.Copy, scale=SCALE)
                else:
                    ins = a.activation(v[:, par, i // 2, (i % 2) * 512:(i % 2) * 512 + 512], psP[j % 2][:], ACT.Copy)
                ins.then_inc(s_ev[j % 2], 1)

            def step(g, u, par, proj, prep):
                if proj:
                    for j in OF_STEP[u]:
                        evac_job(plus(g, 1), 1 - par, j)
                if has(g, u, 0):
                    act.wait_ge(s_sub if first else s_read, at(g, UG, u + 1))
                    s = S[:, u % 4]
                    a.activation(s, s, ACT.Exp).then_inc(s_exp, 1)
                if has(g, u, 2):
                    act.wait_ge(s_tr, at(g, UG, u - 1))
                    if has(g, u, 4):
                        act.wait_ge(s_pv, at(g, UG, u - 3))
                    a.activation(PT[:, u % 2], psT[u % 2][:], ACT.Copy).then_inc(s_PT, 1)
                if u % 2 == 0 and has(g, u, 3):
                    act.wait_ge(s_pv, at(g, UG, u - 2))
                    eight = ((u - 4) // 2) % 4
                    if not isinstance(g, int) or g * UG + u >= 8:
                        act.wait_ge(s_wo, at(g, GT, (u - 4) // 4))
                    a.activation(oT[:, (eight % 2) * 4:(eight % 2) * 4 + 4], psV[:], ACT.Copy).then_inc(s_oT, 1)
                if u == 0 and routed(g, 2):
                    act.wait_ge(s_sh, at(g, 1, -1))
                    a.activation(pr[:], pr[:], ACT.Exp).then_inc(s_re, 1)
                if u == 4 and routed(g, 1):
                    act.wait_ge(s_rtx, at(g, 1, 0))
                    if routed(g, 2):
                        act.wait_ge(s_lg, at(g, 1, -1))
                    a.activation(rxT[:], psM[:], ACT.Copy).then_inc(s_rxT, 1)
                if proj and u == XT_STEP:
                    evac_x(plus(g, 1))
                if prep and u == CT_STEP:
                    evac_ctx(plus(g, 2), par)

            def before():
                if not first:
                    act.wait_ge(t.s_vec, 16 * 5)
                evac_ctx(0, 0)
                for j in range(8):
                    evac_job(0, 0, j)
                evac_ctx(1, 1)
                evac_x(0)
                for j in range(8, NJ):
                    evac_job(0, 0, j)

            run(act, step, before)

        @block.vector
        def _(ve):
            v_ = nc.vector
            NR = 1 if first else 2

            def indices(g):
                if begun(g, 1):
                    for i in range(2):
                        ve.wait_ge(s_row[i], at(g, GT * K0 * 8, 0))
                src = t.comb0[:, g * GT:(g + 1) * GT] if isinstance(g, int) else t.comb0[:, bass.ds(at(g, GT, 0), GT)]
                v_.tensor_copy(idx[:].rearrange("p (k t) -> p t k", k=K0), src).then_inc(s_ix, 1)

            def add_rows(g, k):
                if k % 2 == 0:
                    ve.wait_ge(s_row[k // 2], at(g, GT * K0 * 8, GT * K0 * 8))
                for i in range(GT):
                    pr = (t.prob0[:, g * GT + i, k:k + 1] if isinstance(g, int)
                          else t.prob0[:, bass.ds(at(g, GT, i), 1), k:k + 1].rearrange("p a b -> p (a b)"))
                    if k:
                        ve.wait_ge(s_acc, at(g, GT * K0, (k - 1) * GT + i + 1))
                    v_.scalar_tensor_tensor(out=x_tile(g, i), in0=rows[:, k * GT + i, :], scalar=pr, in1=x_tile(g, i),
                                            op0=ALU.mult, op1=ALU.add).then_inc(s_acc, 1)

            def moments(g, r):
                if r == 0:
                    if begun(g, 1):
                        ve.wait_ge(s_xn, at(g, 1, 0))
                    if first and isinstance(g, int) and g in (0, 2):
                        ve.wait_ge(t.s_xl[g // 2], 16)
                    if not first:
                        ve.wait_ge(s_acc, at(g, GT * K0, GT * K0))
                else:
                    ve.wait_ge(s_xn1, at(g, 1, 1))
                settle(ve)
                for i in range(GT):
                    ins = v_.bn_stats(stats[:, i], xn[:, i] if r else x_tile(g, i))
                ins.then_inc(s_mv, 1)
                ve.wait_ge(s_mv, at(g, 2 * NR, 2 * r + 1))
                settle(ve)
                for i in range(GT):
                    ins = v_.bn_aggr(mv[:, i], stats[:, i])
                ins.then_inc(s_mv, 1)

            def norm(g, r):
                ve.wait_ge(s_rstd, at(g, NR, r + 1))
                ve.wait_ge(s_mv, at(g, 2 * NR, 2 * r + 2))
                if r == 0 and begun(g, 1):
                    ve.wait_ge(s_tx, at(g, 1, 0))
                for i in range(GT):
                    ins = v_.tensor_scalar(xn[:, i], xn[:, i] if r else x_tile(g, i), mv[:, i, 0:1], rstd[:, i:i + 1],
                                           ALU.subtract, ALU.mult)
                ins.then_inc(s_xn if r == NR - 1 else s_xn1, 1)

            def context_moments(g):
                wait_ctx(ve, g)
                if begun(g, 1):
                    ve.wait_ge(s_cn, at(g, GT, 0))
                settle(ve)
                for i in range(GT):
                    ins = v_.bn_stats(cstats[:, i], ctx[:, i])
                ins.then_inc(s_cmv, 1)
                ve.wait_ge(s_cmv, at(g, 2, 1))
                settle(ve)
                for i in range(GT):
                    ins = v_.bn_aggr(cmv[:, i], cstats[:, i])
                ins.then_inc(s_cmv, 1)

            def context_norm(g):
                ve.wait_ge(s_crs, at(g, 1, 1))
                ve.wait_ge(s_cmv, at(g, 2, 2))
                if begun(g, 1):
                    ve.wait_ge(s_tc, at(g, 1, 0))
                for i in range(GT):
                    v_.tensor_scalar(cn[:, i], ctx[:, i], cmv[:, i, 0:1], crs[:, i:i + 1],
                                     ALU.subtract, ALU.mult).then_inc(s_cn, 1)

            def evac_k(g, par, j):
                kind, i = JOBS[j]
                if kind != "k":
                    return
                ve.wait_ge(s_pj, at(g, NJ, j + 1))
                if j == 0 and begun(g, 2):
                    ve.wait_ge(s_sc, at(g, UG, -UG))
                src = psP[j % 2][:].rearrange("p (c n) -> p c n", c=2)
                v_.tensor_copy(kz[0:DH, par, 2 * i:2 * i + 2, 0], src[0:DH])
                v_.tensor_copy(kz[DH:P, par, 2 * i:2 * i + 2, 1], src[DH:P]).then_inc(s_ev[j % 2], 1)

            links = {"n": 0, "g": 0}
            PER = 13 if first else 12

            def link(ins):
                links["n"] += 1
                ins.then_inc(s_v, 1)
                ve.wait_ge(s_v, at(links["g"], PER, links["n"]))
                settle(ve)

            def route_moments(g):
                ve.wait_ge(s_x, at(g, GT, GT))
                settle(ve)
                for i in range(GT):
                    ins = v_.bn_stats(rstats[:, i], x_tile(g, i))
                ins.then_inc(s_rmv, 1)
                ve.wait_ge(s_rmv, at(g, 2, 1))
                settle(ve)
                for i in range(GT):
                    ins = v_.bn_aggr(rmv[:, i], rstats[:, i])
                ins.then_inc(s_rmv, 1)

            def route_norm(g, par):
                ve.wait_ge(s_rrs, at(g, 1, 1))
                if begun(g, 2):
                    ve.wait_ge(s_out[par], outs(g))
                for i in range(GT):
                    ins = v_.tensor_scalar(rxn[:, par, i], x_tile(g, i), rmv[:, i, 0:1], rrs[:, i:i + 1],
                                           ALU.subtract, ALU.mult)
                ins.then_inc(s_rxn, 1)

            def route_shift(g):
                links.update(n=0, g=g)
                ve.wait_ge(s_lg, at(g, 1, 1))
                link(v_.tensor_reduce(rmx[:], psM[:, :, 0:E], AX, ALU.max))
                v_.tensor_tensor(pr[:], psM[:, :, 0:E], rmx[:].unsqueeze(2).broadcast_to([P, GT, E]), ALU.subtract
                                 ).then_inc(s_sh, 1)

            def route_choose(g):
                ve.wait_ge(s_re, at(g, 1, 1))
                settle(ve)
                for i in range(GT):
                    v_.max(top[:, i], pr[:, i])
                link(v_.tensor_reduce(rzs[:], pr[:], AX, ALU.add))
                for i in range(GT):
                    v_.max_index(ids[:, i], top[:, i], pr[:, i])
                link(v_.reciprocal(rrz[:], rzs[:]))
                if first:
                    v_.tensor_scalar(rrz[:], rrz[:], t.gate[:, 2:3], None, ALU.mult)
                link(v_.tensor_copy(idf[:], ids[:, :, 0:K]))
                v_.tensor_tensor(tiles(t.prob0 if first else t.p1, g), top[:, :, 0:K],
                                 rrz[:].unsqueeze(2).broadcast_to([P, GT, K]), ALU.mult)
                link(v_.tensor_tensor(oh[:].rearrange("p t k e -> p (t k) e"),
                                      t.iota[:, 0:E].unsqueeze(1).broadcast_to([P, GT * K, E]),
                                      idf[:].rearrange("p t k -> p (t k)").unsqueeze(2).broadcast_to([P, GT * K, E]),
                                      ALU.is_equal))
                for i in range(GT):
                    if begun(g, 1):
                        if i == 0:
                            ve.wait_ge(s_pos, at(g, 1, 0))
                        link(v_.tensor_tensor(t.acc[:, 0:CW], t.acc[:, 0:CW], t.cnt[:, i, 0:CW], ALU.add))
                    else:
                        link(v_.memset(t.acc[:, 0:CW], 0.0))
                if first:
                    with nc.allow_low_precision("sums of at most K zeros and ones"):
                        v_.tensor_reduce(t.cnt[:], oh[:].rearrange("p t k e -> p t e k"), AX, ALU.add).then_inc(s_cnt, 1)
                else:
                    v_.tensor_copy(t.cnt[:, :, 0:CW], oh[:].rearrange("p t k e -> p t (k e)")).then_inc(s_cnt, 1)
                    v_.tensor_copy(tiles(t.oh1, g), oh[:, :, 1])
                    v_.tensor_copy(tiles(t.idf1, g), idf[:])

            def route_read(g):
                ve.wait_ge(s_pos, at(g, 1, 1))
                for i in range(GT):
                    if first:
                        ins = v_.tensor_tensor(sel[:, i], oh[:, i], psM[:, i, 0:E].unsqueeze(1).broadcast_to([P, K, E]), ALU.mult)
                    else:
                        ins = v_.tensor_tensor(sel[:, i].rearrange("p k e -> p (k e)"), oh[:, i].rearrange("p k e -> p (k e)"),
                                               psM[:, i, 0:CW], ALU.mult)
                ins.then_inc(s_sel, 1)

            def route_slots(g, par):
                ve.wait_ge(s_sel, at(g, 1, 1))
                link(v_.tensor_reduce(pos[:], sel[:], AX, ALU.add))
                if not first:
                    v_.tensor_copy(tiles(t.pos1, g), pos[:])
                link(v_.tensor_scalar(over[:], pos[:], float(CAP), BIG, ALU.is_ge, ALU.mult))
                link(v_.scalar_tensor_tensor(out=slot[:], in0=idf[:], scalar=float(CAP), in1=pos[:], op0=ALU.mult, op1=ALU.add))
                link(v_.tensor_tensor(over[:], over[:], slot[:], ALU.add))
                if first:
                    v_.tensor_copy(disp[:, par], over[:])
                    link(v_.tensor_scalar(pos[:], pos[:], float(CAP - 1), None, ALU.min))
                    link(v_.scalar_tensor_tensor(out=slot[:], in0=idf[:], scalar=float(CAP), in1=pos[:], op0=ALU.mult, op1=ALU.add))
                    v_.tensor_copy(tiles(t.comb0, g), slot[:]).then_inc(s_slot, 1)
                else:
                    link(v_.tensor_scalar(over[:, :, 1], over[:, :, 1], float(E * CAP), None, ALU.add))
                    v_.tensor_copy(disp[:, par], over[:]).then_inc(s_slot, 1)
                assert links["n"] == PER, links

            def step(g, u, par, proj, prep):
                if u == 0 and proj:
                    norm(plus(g, 1), NR - 1)
                if u == 4 and routed(g, 1):
                    route_norm(plus(g, -1), 1 - par)
                if u == 3 and routed(g, 2):
                    route_read(plus(g, -2))
                if has(g, u, 1):
                    s = S[:, (u - 1) % 4]
                    ve.wait_ge(s_exp, at(g, UG, u))
                    v_.tensor_reduce(z[:, (u - 1) % 2], s, AX, ALU.add).then_inc(s_rz, 1)
                    if has(g, u, 3):
                        ve.wait_ge(s_norm, at(g, UG, u - 2))
                    ve.wait_ge(s_rz, at(g, 2 * UG, 2 * u - 1))
                    v_.reciprocal(rz[:, (u - 1) % 2], z[:, (u - 1) % 2]).then_inc(s_rz, 1)
                if has(g, u, 0):
                    s = S[:, u % 4]
                    if has(g, u, 4):
                        ve.wait_ge(s_tr, at(g, UG, u - 3))
                    ve.wait_ge(s_sc, at(g, UG, u + 1))
                    if first:
                        for h in range(HU):
                            head = (u % UT) * HU + h
                            ins = v_.scalar_tensor_tensor(out=s[:, h], in0=t.side[:], scalar=2.0 ** -(head + 1),
                                                          in1=psS[u % 2][:, h], op0=ALU.mult, op1=ALU.add)
                        ins.then_inc(s_read, 1)
                        if has(g, u, 2):
                            ve.wait_ge(s_sub, at(g, UG, u - 1))
                        ve.wait_ge(s_read, at(g, UG, u + 1))
                        v_.tensor_reduce(mx[:, u % 2], s, AX, ALU.max).then_inc(s_max, 1)
                    else:
                        v_.tensor_scalar(s, psS[u % 2][:], CLIP, -CLIP, ALU.min, ALU.max).then_inc(s_read, 1)
                if proj:
                    for j in OF_STEP[u]:
                        evac_k(plus(g, 1), 1 - par, j)
                if u % UT == 3 and has(g, u, 7):
                    i = u // UT - 1
                    x = x_tile(g, i)
                    v_.tensor_tensor(x, x, t.bo[:, layer], ALU.add).then_inc(s_bo, 1)
                    ve.wait_ge(s_bo, at(g, GT, i + 1))
                    ve.wait_ge(s_wo, at(g, GT, i + 1))
                    v_.scalar_tensor_tensor(out=x, in0=psM[:, 0], scalar=t.gate[:, layer:layer + 1], in1=x,
                                            op0=ALU.mult, op1=ALU.add).then_inc(s_x, 1)
                if routed(g, 2):
                    r = plus(g, -2)
                    if u == 0:
                        route_shift(r)
                    if u == 1:
                        route_choose(r)
                    if u == 3:
                        route_slots(r, par)
                if u == 3 and routed(g, 1):
                    route_moments(plus(g, -1))
                if prep:
                    g2 = plus(g, 2)
                    if not first:
                        if u == 2:
                            add_rows(g2, 0)
                            context_moments(g2)
                        if u == 4:
                            add_rows(g2, 1)
                            context_norm(g2)
                        if u == 5:
                            add_rows(g2, 2)
                            add_rows(g2, 3)
                            if has_group(g, 3):
                                indices(plus(g, 3))
                        if u == 7:
                            norm(g2, 0)
                            moments(g2, 1)
                    if u == 6:
                        moments(g2, 0)

            def before():
                if first:
                    moments(0, 0)
                    norm(0, 0)
                    moments(1, 0)
                else:
                    indices(0)
                    context_moments(0)
                    context_norm(0)
                    context_moments(1)
                for j in range(NJ):
                    evac_k(0, 0, j)
                if first:
                    ve.wait_ge(t.s_vec, 16 * 5)
                    return
                context_norm(1)
                for g in (0, 1):
                    for k in range(K0):
                        add_rows(g, k)
                    indices(g + 1)
                    moments(g, 0)
                    norm(g, 0)
                    moments(g, 1)
                    if g == 0:
                        norm(g, 1)

            run(ve, step, before)

        @block.tensor
        def _(pe):
            mm, tp = nc.tensor.matmul, nc.tensor.transpose

            def transposes(src, done):
                for c in range(DC):
                    for i in range(GT):
                        ins = tp(psM[:, c, i * P:(i + 1) * P], src[:, i, c * P:(c + 1) * P], t.ident[:])
                ins.then_inc(done, 1)

            def transpose_x(g):
                pe.wait_ge(s_xn, at(g, 1, 1))
                if begun(g, 3):
                    pe.wait_ge(s_sh, at(g, 1, -2))
                elif g == 2:
                    pe.wait_ge(s_x, 1)
                else:
                    pe.wait_ge(s_cT, 2)
                if g == 1:
                    pe.wait_ge(s_xT, 1)
                transposes(xn, s_tx)

            def transpose_ctx(g):
                if first:
                    wait_ctx(pe, g)
                else:
                    pe.wait_ge(s_cn, at(g, GT, GT))
                if begun(g, 3):
                    pe.wait_ge(s_rxT, at(g, 1, -2))
                elif g == 2:
                    pe.wait_ge(s_xT, 2)
                elif g == 1:
                    pe.wait_ge(s_cT, 1)
                transposes(ctx if first else cn, s_tc)

            def project(g, par, j):
                kind, i = JOBS[j]
                if j == 0:
                    pe.wait_ge(s_cT, at(g, 1, 1))
                if j == 8:
                    pe.wait_ge(s_xT, at(g, 1, 1))
                if i == 0 and isinstance(g, int) and g == 0:
                    pe.wait_ge(s_w[kind], 16)
                if begun(g, 1) or j >= 2:
                    pe.wait_ge(s_ev[j % 2], at(g, NJ // 2, j // 2))
                bank = psP[j % 2]
                if kind == "v":
                    tile, half = i // 2, i % 2
                    for c in range(DC):
                        ins = mm(bank[:], cT[:, par, c, tile * P:(tile + 1) * P], wv[:, c, half * 512:half * 512 + 512],
                                 start=c == 0, stop=c == DC - 1)
                else:
                    w, src = (wq, xT) if kind == "q" else (wk, cT[:, par])
                    for b in range(2):
                        for c in range(DC):
                            ins = mm(bank[:, b * TOK:(b + 1) * TOK], w[:, c, (2 * i + b) * P:(2 * i + b + 1) * P],
                                     src[:, c], start=c == 0, stop=c == DC - 1)
                ins.then_inc(s_pj, 1)

            def step(g, u, par, proj, prep):
                if has(g, u, 0):
                    if u == 0:
                        for i in range(2):
                            pe.wait_ge(s_ev[i], at(g, NJ // 2, NJ // 2))
                    if has(g, u, 2):
                        pe.wait_ge(s_read, at(g, UG, u - 1))
                    tile = u // UT
                    for i in range(2):
                        pair = (u % UT) * 2 + i
                        ins = mm(psS[u % 2][:, 2 * i:2 * i + 2], qT[:, par, pair, tile * P:(tile + 1) * P],
                                 kz[:, par, pair, :, tile * P:(tile + 1) * P], start=True, stop=True)
                    ins.then_inc(s_sc, 1)
                if proj:
                    for j in OF_STEP[u]:
                        project(plus(g, 1), 1 - par, j)
                if has(g, u, 2):
                    pe.wait_ge(s_norm, at(g, UG, u - 1))
                    if has(g, u, 4):
                        pe.wait_ge(s_PT, at(g, UG, u - 3))
                    for h in range(HU):
                        ins = tp(psT[u % 2][:, h], S[:, (u - 2) % 4, h], t.ident[:])
                    ins.then_inc(s_tr, 1)
                if has(g, u, 3):
                    pe.wait_ge(s_PT, at(g, UG, u - 2))
                    un = (u - 3) % UG
                    vpar = par if u >= 3 else 1 - par
                    if un % 2 == 0 and has(g, u, 5):
                        pe.wait_ge(s_oT, at(g, UG // 2, (u - 3) // 2))
                    tile = un // UT
                    for h in range(HU):
                        head = (un % UT) * HU + h
                        row = (h % 2) * DH
                        ins = mm(psV[row:row + DH, (un % 2) * 2 + h // 2], v[:, vpar, tile, head * DH:(head + 1) * DH],
                                 PT[:, (u - 3) % 2, h], start=True, stop=True)
                    ins.then_inc(s_pv, 1)
                if u % UT == 3 and has(g, u, 7):
                    i = u // UT - 1
                    pe.wait_ge(s_oT, at(g, UG // 2, 4 * i // 2 + 2))
                    if begun(g, 1) or i > 0:
                        pe.wait_ge(s_x, at(g, GT, i))
                    if u == 7 and prep:
                        pe.wait_ge(s_cT, at(g, 1, 3))
                    elif u == 7:
                        pe.wait_ge(s_rxT, at(g, 1, 0))
                    if u == 3 and routed(g, 2):
                        pe.wait_ge(s_sel, at(g, 1, -1))
                    elif u == 3:
                        pe.wait_ge(s_xT, at(g, 1, 2))
                    if isinstance(g, int) and g == 0:
                        pe.wait_ge(s_late, 32)
                    for c in range(HP):
                        ins = mm(psM[:, 0], oT[:, c], wo[:, c], start=c == 0, stop=c == HP - 1)
                    ins.then_inc(s_wo, 1)
                if u == 0 and routed(g, 2):
                    logits(plus(g, -2))
                if u == 2 and routed(g, 2):
                    count(plus(g, -2))
                if u == 4 and routed(g, 1):
                    router_inputs(plus(g, -1), 1 - par)
                if proj and u == XT_STEP:
                    transpose_x(plus(g, 1))
                if prep and u == CT_STEP:
                    transpose_ctx(plus(g, 2))

            def router_inputs(g, par):
                pe.wait_ge(s_rxn, at(g, 1, 1))
                pe.wait_ge(s_x, at(g, GT, GT))
                transposes(rxn[:, par], s_rtx)

            def logits(g):
                pe.wait_ge(s_rxT, at(g, 1, 1))
                if isinstance(g, int) and g > NG - 3:
                    pe.wait_ge(s_x, min(NB, g * GT + 3))
                else:
                    pe.wait_ge(s_x, at(g, GT, 3))
                for i in range(GT):
                    for c in range(DC):
                        ins = mm(psM[:, i, 0:EW], rxT[:, c, i * P:(i + 1) * P], rw[:, c], start=c == 0, stop=c == DC - 1)
                ins.then_inc(s_lg, 1)

            def count(g):
                pe.wait_ge(s_cnt, at(g, 1, 1))
                pe.wait_ge(s_sh, at(g, 1, 1))
                if not isinstance(g, int) or g + 3 < NG:
                    pe.wait_ge(s_xT, at(g, 1, 4))
                for i in range(GT):
                    mm(psM[:, i, 0:CW], t.tri[:], t.cnt[:, i, 0:CW], start=True, stop=False)
                    if i:
                        mm(psM[:, i, 0:CW], t.ones_bf[:], t.cnt[:, 0, 0:CW], start=False, stop=False)
                    ins = mm(psM[:, i, 0:CW], t.ones_bf[:], t.acc[:, 0:CW], start=False, stop=True)
                ins.then_inc(s_pos, 1)

            def before():
                transpose_ctx(0)
                for j in range(8):
                    project(0, 0, j)
                transpose_ctx(1)
                transpose_x(0)
                for j in range(8, NJ):
                    project(0, 0, j)

            run(pe, step, before)


def experts(nc, t, d, layer):
    L = f"e{layer}_"
    first = layer == 0
    E, F, CAP = (E0, F0, CAP0) if first else (E1, F1, CAP1)
    FC = F // P
    NC = CAP // TOK
    EB = 4 if first else 2
    CB = EB * NC
    RB = 4 if first else 5
    UB = 2
    with ExitStack() as stack:
        m = Memory(nc, stack)
        w_in = m.sb(L + "w_in", [P, EB, DC, 2 * F])
        w_out = m.sb(L + "w_out", [P, EB, FC, D])
        rows = m.sb(L + "rows", [P, RB, GT, D])
        xT = m.sb(L + "xT", [P, UB, DC, TOK])
        act_ = m.sb(L + "act", [P, UB, FC, TOK])
        hT = m.sb(L + "hT", [P, UB, FC, TOK])
        y = m.sb(L + "y", [P, UB, GT, D])
        if not first:
            NT = CAP // P
            local = m.sb(L + "local", [P, E, NT])
            glob = m.sb(L + "glob", [P, E, NT])
            total = m.sb(L + "total", [P, K1, E])
            back = m.sb(L + "back", [P, E])
            second = m.sb(L + "second", [P, E, NT])
            source = m.sb(L + "source", [P, E, NT])
            source_row = m.sb(L + "source_row", [P, E * NT], I32)
            cur = m.sb(L + "cur", [P, RB, GT], I32)
            add1 = m.sb(L + "add1", [P, NB])
            gate_ = m.sb(L + "gates", [P, NB, K1])
            den = m.sb(L + "den", [P, NB])
            s_grid = m.sem(L + "slot_numbers_ready")
            s_tot = m.sem(L + "totals_ready")
            s_chain = m.sem(L + "vector_chain")
            s_src = m.sem(L + "sources_ready")
            s_cur = m.sem(L + "chunk_sources_copied")
        NHB = 1 if first else 2
        psX = [m.ps(L + f"psX{i}", [P, DC, TOK]) for i in range(2)]
        psH = [m.ps(L + f"psH{i}", [P, 2, TOK]) for i in range(UB if first else 4)]
        psY = [m.ps(L + f"psY{i}", [P, GT, D]) for i in range(2)]
        totals = psY[0][:, 0, 0:K1 * E]
        s_w = [m.sem(L + f"weights_loaded{i}") for i in range(EB)]
        s_r = [m.sem(L + f"rows_loaded{i}") for i in range(RB)]
        s_tx = m.sem(L + "transposed")
        s_xT = m.sem(L + "evacuated")
        s_h = m.sem(L + "hidden_ready")
        s_act = m.sem(L + "activated")
        s_hT = m.sem(L + "gated")
        s_y = m.sem(L + "output_ready")
        s_ye = m.sem(L + "output_evacuated")
        s_st = [m.sem(L + f"rows_stored{i}") for i in range(2)]
        block = stack.enter_context(nc.Block())
        buf, yd = d[f"buf{layer}"], d[f"y{layer}"]
        win, wout = (d["L0_ffn_w1"], d["L0_ffn_w2"]) if first else (d["L1_ffn_W_in"], d["L1_ffn_W_out"])
        NCH = E * NC
        NIT = E // EB

        def n_at(it, per, k):
            return it * per + k

        def each(eng, body):
            body(0, True)
            with eng.Fori(1, NIT) as it:
                body(it, False)

        @block.sync
        def _(sp):
            def weights(it, e):
                ex = it * EB + e
                w1 = win[ex] if isinstance(it, int) else win[bass.ds(ex, 1)].rearrange("o k n -> (o k) n")
                w2 = wout[ex] if isinstance(it, int) else wout[bass.ds(ex, 1)].rearrange("o k n -> (o k) n")
                sp.dma_start(w_in[:, e], w1.rearrange("(c p) n -> p c n", p=P)).then_inc(s_w[e], 16)
                sp.dma_start(w_out[:, e], w2.rearrange("(c p) n -> p c n", p=P)).then_inc(s_w[e], 16)

            def body(it, last):
                for c in range(CB):
                    r0 = it * (CB * TOK) + c * TOK
                    sp.wait_ge(s_ye, it * CB + c + 1)
                    sp.dma_start(yd[bass.ds(r0, TOK) if not last else slice(r0, r0 + TOK)]
                                 .rearrange("(i p) n -> p i n", p=P), y[:, c % 2]).then_inc(s_st[c % 2], 16)
                    if c % NC == NC - 1 and not last:
                        weights(it + 1, c // NC)

            for e in range(EB):
                weights(0, e)
            with sp.Fori(0, NIT - 1) as it:
                body(it, False)
            body(NIT - 1, True)
            for i in range(2):
                sp.wait_ge(s_st[i], NCH // 2 * 16)

        PER_LOAD = 16 if first else 16 * GT
        RPI = CB // RB

        @block.tensor
        def _(pe):
            mm = nc.tensor.matmul

            def val(it, n):
                return it * CB + n

            def transposes(it, c, skip):
                pe.wait_ge(s_r[c % RB], (it * RPI + c // RB + 1) * PER_LOAD)
                if not skip(2):
                    pe.wait_ge(s_xT, val(it, c - 1))
                for k in range(DC):
                    for i in range(GT):
                        ins = nc.tensor.transpose(psX[c % 2][:, k, i * P:(i + 1) * P], rows[:, c % RB, i, k * P:(k + 1) * P],
                                                  t.ident[:])
                ins.then_inc(s_tx, 1)

            def hidden(it, c, skip):
                e = c // NC
                if c % NC == 0:
                    pe.wait_ge(s_w[e], (it + 1) * 32)
                pe.wait_ge(s_xT, val(it, c + 1))
                for f in range(2 * FC):
                    if first:
                        if f == 0 and not skip(2):
                            pe.wait_ge(s_hT, val(it, c - 1))
                        dst = psH[c % 2][:, f]
                    else:
                        if f == 0 and not skip(1):
                            pe.wait_ge(s_act, val(it, c))
                        if f == FC and not skip(1):
                            pe.wait_ge(s_hT, val(it, c))
                        dst = psH[f // 2][:, f % 2]
                    for k in range(DC):
                        ins = mm(dst, w_in[:, e, k, f * P:(f + 1) * P], xT[:, c % 2, k], start=k == 0, stop=k == DC - 1)
                    if f in (FC - 1, 2 * FC - 1):
                        ins.then_inc(s_h, 1)

            def output(it, c, skip):
                e = c // NC
                pe.wait_ge(s_hT, val(it, c + 1))
                if not skip(2):
                    pe.wait_ge(s_ye, val(it, c - 1))
                for i in range(GT):
                    for f in range(FC):
                        ins = mm(psY[c % 2][:, i], hT[:, c % 2, f, i * P:(i + 1) * P], w_out[:, e, f], start=f == 0, stop=f == FC - 1)
                ins.then_inc(s_y, 1)

            def body(it, fresh):
                for c in range(CB):
                    n = lambda lag, c=c: (lambda back: fresh and c - lag < back)
                    transposes(it, c, n(0))
                    if not fresh or c >= 1:
                        hidden(*((it, c - 1) if c else (it - 1, CB - 1)), n(1))
                    if not fresh or c >= 2:
                        output(*((it, c - 2) if c >= 2 else (it - 1, CB + c - 2)), n(2))
            if not first:
                mm(totals, t.ones_bf[:], t.acc[:, 0:K1 * E], start=True, stop=False)
                for i in range(GT):
                    ins = mm(totals, t.ones_bf[:], t.cnt[:, i, 0:K1 * E], start=False, stop=i == GT - 1)
                ins.then_inc(s_tot, 1)
            each(pe, body)
            no = lambda back: False
            output(NIT - 1, CB - 2, no)
            hidden(NIT - 1, CB - 1, no)
            output(NIT - 1, CB - 1, no)

        @block.scalar
        def _(act):
            a = nc.scalar

            def body(it, fresh):
                for c in range(CB):
                    act.wait_ge(s_tx, it * CB + c + 1)
                    if not (fresh and c < 2):
                        act.wait_ge(s_h, it * (2 * CB) + 2 * (c - 1))
                    a.activation(xT[:, c % 2], psX[c % 2][:], ACT.Copy).then_inc(s_xT, 1)
                    if not fresh or c >= 1:
                        activate(it, c - 1, fresh and c <= 2)
            def activate(it, c, fresh2):
                p = c % 2
                act.wait_ge(s_h, it * (2 * CB) + 2 * c + (2 if first else 1))
                if not fresh2:
                    act.wait_ge(s_hT, it * CB + c - 1)
                if first:
                    a.activation(act_[:, p, 0], psH[p][:, 0], ACT.Silu).then_inc(s_act, 1)
                else:
                    for b in range(2):
                        ins = a.activation(act_[:, p, 2 * b:2 * b + 2], psH[b][:], ACT.Gelu)
                    ins.then_inc(s_act, 1)
            each(act, body)
            activate(NIT, -1, False)

        @block.vector
        def _(ve):
            v_ = nc.vector

            def gate(it, c, fresh2):
                p = c % 2
                ve.wait_ge(s_act, it * CB + c + 1)
                ve.wait_ge(s_h, it * (2 * CB) + 2 * c + 2)
                if not fresh2:
                    ve.wait_ge(s_y, it * CB + c - 1)
                if first:
                    v_.tensor_tensor(hT[:, p, 0], act_[:, p, 0], psH[p][:, 1], ALU.mult).then_inc(s_hT, 1)
                else:
                    for b in range(2):
                        ins = v_.tensor_tensor(hT[:, p, 2 * b:2 * b + 2], act_[:, p, 2 * b:2 * b + 2], psH[2 + b][:], ALU.mult)
                    ins.then_inc(s_hT, 1)

            def out(it, c, fresh2):
                ve.wait_ge(s_y, it * CB + c + 1)
                if not fresh2:
                    ve.wait_ge(s_st[c % 2], it * (CB * 8) + (c // 2) * 16)
                v_.tensor_copy(y[:, c % 2], psY[c % 2][:]).then_inc(s_ye, 1)

            def body(it, fresh):
                for c in range(CB):
                    gate(it, c, fresh and c < 2)
                    if not fresh or c >= 1:
                        out(it, c - 1, fresh and c <= 2)
            n = [0]

            def link(ins):
                n[0] += 1
                ins.then_inc(s_chain, 1)
                ve.wait_ge(s_chain, n[0])

            def sources():
                ve.wait_ge(s_tot, 1)
                ve.wait_ge(s_grid, 2)
                link(v_.tensor_copy(total[:].rearrange("p k e -> p (k e)"), totals))
                tot1 = total[:, 0].unsqueeze(2).broadcast_to([P, E, NT])
                tot = total[:, 1].unsqueeze(2).broadcast_to([P, E, NT])
                v_.tensor_scalar(back[:], total[:, 0], -1.0, float(E * CAP), ALU.mult, ALU.add)
                link(v_.tensor_tensor(total[:, 1], total[:, 0], total[:, 1], ALU.add))
                v_.tensor_tensor(second[:], local[:], tot1, ALU.is_ge)
                link(v_.tensor_tensor(source[:], local[:], tot, ALU.is_lt))
                link(v_.tensor_tensor(second[:], second[:], source[:], ALU.mult))
                link(v_.tensor_tensor(second[:], second[:], back[:].unsqueeze(2).broadcast_to([P, E, NT]), ALU.mult))
                link(v_.tensor_tensor(source[:], glob[:], second[:], ALU.add))
                v_.tensor_copy(source_row[:], source[:].rearrange("p e n -> p (e n)")).then_inc(s_src, 1)

            def gates():
                link(v_.tensor_tensor(t.oh1[:], t.oh1[:], total[:, 0].unsqueeze(1).broadcast_to([P, NB, E]), ALU.mult))
                link(v_.tensor_reduce(add1[:], t.oh1[:], AX, ALU.add))
                link(v_.tensor_tensor(t.pos1[:, :, 1], t.pos1[:, :, 1], add1[:], ALU.add))
                link(v_.tensor_scalar(gate_[:], t.pos1[:], float(CAP), None, ALU.is_lt))
                link(v_.tensor_tensor(gate_[:], gate_[:], t.p1[:], ALU.mult))
                link(v_.tensor_tensor(den[:], gate_[:, :, 0], gate_[:, :, 1], ALU.add))
                link(v_.tensor_scalar(den[:], den[:], 1e-9, None, ALU.max))
                link(v_.reciprocal(den[:], den[:]))
                link(v_.tensor_tensor(gate_[:], gate_[:], den[:].unsqueeze(2).broadcast_to([P, NB, K1]), ALU.mult))
                v_.tensor_scalar(t.prob1[:], gate_[:], t.gate[:, 3:4], None, ALU.mult)
                link(v_.tensor_scalar(t.pos1[:], t.pos1[:], float(CAP - 1), None, ALU.min))
                link(v_.scalar_tensor_tensor(out=gate_[:], in0=t.idf1[:], scalar=float(CAP), in1=t.pos1[:],
                                             op0=ALU.mult, op1=ALU.add))
                v_.tensor_copy(t.comb1[:], gate_[:])

            if not first:
                sources()
                gates()
            each(ve, body)
            out(NIT, -1, False)

        @block.gpsimd
        def _(pool):
            g_ = nc.gpsimd

            def body(it, fresh):
                for c in range(CB):
                    b, n0 = c % RB, c * GT
                    if not (fresh and c < RB):
                        pool.wait_ge(s_tx, (c if fresh else it * CB + c) - RB + 1)
                    if first:
                        r0 = c * TOK if fresh else it * (CB * TOK) + c * TOK
                        pool.sem_inc(t.s_passed, 1)
                        g_.dma_start(rows[:, b], buf[bass.ds(r0, TOK) if not fresh else slice(r0, r0 + TOK)]
                                     .rearrange("(i p) n -> p i n", p=P)).then_inc(s_r[b], 16)
                        continue
                    src = source_row[:, n0:n0 + GT] if fresh else source_row[:, bass.ds(it * (CB * GT) + n0, GT)]
                    pool.sem_inc(t.s_passed, 1)
                    g_.tensor_copy(cur[:, b], src).then_inc(s_cur, 1)
                    pool.wait_ge(s_cur, it * CB + c + 1)
                    pool.sem_inc(t.s_passed, 1)
                    for i in range(GT):
                        g_.indirect_dma_start(out=rows[:, b, i, :], out_offset=None, in_=buf,
                                              in_offset=bass.IndirectOffsetOnAxis(ap=cur[:, b, i:i + 1], axis=0)
                                              ).then_inc(s_r[b], 16)

            if not first:
                g_.iota(local[:], pattern=[[0, E], [P, NT]], base=0, channel_multiplier=1,
                        allow_small_or_imprecise_dtypes=True).then_inc(s_grid, 1)
                g_.iota(glob[:], pattern=[[CAP, E], [P, NT]], base=0, channel_multiplier=1,
                        allow_small_or_imprecise_dtypes=True).then_inc(s_grid, 1)
                pool.wait_ge(s_src, 1)
            each(pool, body)


def combine(nc, t, d):
    with ExitStack() as stack:
        m = Memory(nc, stack)
        RB = 4
        rows = m.sb("c_rows", [P, RB, K1, D])
        s_row = [m.sem(f"c_rows_gathered{i}") for i in range(RB)]
        s_acc = m.sem("c_row_added")
        s_out = m.sem("c_stored")
        block = stack.enter_context(nc.Block())

        @block.gpsimd
        def _(pool):
            for tile in range(NB):
                if tile >= RB:
                    pool.wait_ge(s_acc, K1 * (tile - RB + 1))
                for k in range(K1):
                    nc.gpsimd.indirect_dma_start(out=rows[:, tile % RB, k], out_offset=None, in_=d["y1"],
                                                 in_offset=bass.IndirectOffsetOnAxis(ap=t.comb1[:, tile, k:k + 1], axis=0)
                                                 ).then_inc(s_row[tile % RB], 16)

        @block.vector
        def _(ve):
            for tile in range(NB):
                ve.wait_ge(s_row[tile % RB], 16 * K1 * (tile // RB + 1))
                for k in range(K1):
                    if k:
                        ve.wait_ge(s_acc, K1 * tile + k)
                    nc.vector.scalar_tensor_tensor(out=t.x[:, tile], in0=rows[:, tile % RB, k], scalar=t.prob1[:, tile, k:k + 1],
                                                   in1=t.x[:, tile], op0=ALU.mult, op1=ALU.add).then_inc(s_acc, 1)

        @block.sync
        def _(sp):
            for tile in range(NB):
                sp.wait_ge(s_acc, K1 * (tile + 1))
                sp.dma_start(d["out"][tile], t.x[:, tile]).then_inc(s_out, 16)
            sp.wait_ge(s_out, 16 * NB)


class Resident:
    pass


def program(nc, d):
    with ExitStack() as stack:
        m = Memory(nc, stack)
        t = Resident()
        t.x = m.sb("x_all", [P, NB, D])
        t.ident = m.sb("ident", [P, P])
        t.tri = m.sb("tri", [P, P], BF16)
        t.ones_bf = m.sb("ones_bf", [P, P], BF16)
        t.iota = m.sb("iota", [P, E0])
        t.minus_half = m.sb("minus_half", [P, GT])
        t.gate = m.sb("gate", [P, 4])
        t.affine = m.sb("affine", [P, 4, DC])
        t.side = m.sb("side", [P, P])
        t.bo = m.sb("bo", [P, 2, D])
        t.acc = m.sb("acc", [P, E0], BF16)
        t.cnt = m.sb("cnt", [P, GT, E0], BF16)
        t.oh1 = m.sb("oh1", [P, NB, E1])
        t.idf1 = m.sb("idf1", [P, NB, K1])
        t.p1 = m.sb("p1", [P, NB, K1])
        t.pos1 = m.sb("pos1", [P, NB, K1])
        t.comb0 = m.sb("comb0", [P, NB, K0], I32)
        t.prob0 = m.sb("prob0", [P, NB, K0])
        t.comb1 = m.sb("comb1", [P, NB, K1], I32)
        t.prob1 = m.sb("prob1", [P, NB, K1])
        t.kz = m.sb("kz", [P, 2, HP, 2, TOK])
        t.s_xl = [m.sem(f"x_loaded{i}") for i in range(2)]
        t.s_vec = m.sem("side_and_affine_loaded")
        t.s_passed = m.sem("waits_passed")
        for layer, n, rows in ((0, E0 * CAP0, ROWS0), (1, E1 * CAP1, ROWS1)):
            d[f"buf{layer}"] = nc.dram_tensor(f"buf{layer}", [rows, D], F32).ap()
            d[f"y{layer}"] = nc.dram_tensor(f"y{layer}", [n, D], F32).ap()
        for phase in PHASES:
            if phase == "setup":
                setup(nc, t, d)
            elif phase == "combine":
                combine(nc, t, d)
            else:
                {"attention": attention, "experts": experts}[phase[:-1]](nc, t, d, int(phase[-1]))


PHASES = ("setup", "attention0", "experts0", "attention1", "experts1", "combine")

_INS = ["x", "ctx_1024", "fside_SxS2_0", "g_xattn", "g_ffn", "L0_xattn_W_q", "L0_xattn_W_k", "L0_xattn_W_v",
        "L0_xattn_W_out", "L0_xattn_b_out", "L0_ffn_router_w", "L0_ffn_w1", "L0_ffn_w2", "L1_xattn_ln_l_w",
        "L1_xattn_ln_l_b", "L1_xattn_ln_c_w", "L1_xattn_ln_c_b", "L1_xattn_Wq", "L1_xattn_Wkv", "L1_xattn_Wo",
        "L1_xattn_bo", "L1_ffn_Wg", "L1_ffn_W_in", "L1_ffn_W_out"]


def kernel(**inputs):
    import numpy as np
    import concourse.bacc as bacc
    from concourse.bass_utils import run_bass_kernel_spmd

    nc = bacc.Bacc("TRN2", target_bir_lowering=False, num_devices=1)
    arrays, d = {}, {}
    for name in _INS:
        a = np.ascontiguousarray(inputs[name])
        arrays[f"in_{name}"] = a
        d[name] = nc.dram_tensor(f"in_{name}", a.shape, mybir.dt.from_np(a.dtype), kind="ExternalInput").ap()
    d["out"] = nc.dram_tensor("out_x", (NB, P, D), F32, kind="ExternalOutput").ap()
    program(nc, d)
    result = run_bass_kernel_spmd(nc, [arrays], core_ids=[0])
    return result.results[0]["out_x"]
```

```python
from contextlib import ExitStack

import concourse.bass as bass
from concourse import mybir

F32 = mybir.dt.float32
F32R = mybir.dt.float32r
BF16 = mybir.dt.bfloat16
I32 = mybir.dt.int32
U32 = mybir.dt.uint32
ACT = mybir.ActivationFunctionType
ALU = mybir.AluOpType
AX = mybir.AxisListType.X

P = 128
NB = 32
D = 256
DC = D // P
H = 16
DH = 64
INNER = H * DH
HP = H // 2
GT = 2
NG = NB // GT
TOK = GT * P
HU = 4
UT = H // HU
UG = GT * UT
NU = NG * UG
EPS = 1e-5
SCALE = DH ** -0.5
CLIP = 11.0
BIG = 65536.0

E0, K0, F0, CAP0 = 64, 4, 128, 256
E1, K1, F1, CAP1 = 8, 2, 512, 1280
ROWS0, ROWS1 = E0 * CAP0, 2 * E1 * CAP1


def plus(g, n):
    return g + n if isinstance(g, int) else (g[0], g[1] + n)


def begun(g, n):
    return not isinstance(g, int) or g >= n


def at(g, per, k):
    if isinstance(g, int):
        return g * per + k
    reg, half = g
    return reg * (2 * per) + (half * per + k)




def split_product(pe, dst, a_hi, a_lo, b_hi, b_lo, start, stop):
    pe.matmul(dst, a_hi, b_hi, start=start, stop=False)
    pe.matmul(dst, a_hi, b_lo, start=False, stop=False)
    return pe.matmul(dst, a_lo, b_hi, start=False, stop=stop)


class Memory:

    def __init__(self, nc, stack):
        self.nc, self.stack = nc, stack

    def sb(self, name, shape, dt=F32):
        return self.stack.enter_context(self.nc.sbuf_tensor(name, shape, dt))

    def ps(self, name, shape, dt=F32):
        return self.stack.enter_context(self.nc.psum_tensor(name, shape, dt))

    def sem(self, name):
        return self.stack.enter_context(self.nc.semaphore(name))


def row_vector(ap, n):
    return ap.rearrange("(o n) -> o n", o=1).broadcast_to([P, n])


def setup(nc, t, d):
    with ExitStack() as stack:
        m = Memory(nc, stack)
        raw = m.sb("raw_gates", [P, 4])
        bo = m.sb("bo_raw", [P, 2, D])
        s_load = m.sem("setup_loaded")
        s_const = m.sem("setup_constants")
        s_tanh = m.sem("setup_tanh")
        s_v = m.sem("setup_vector")
        block = stack.enter_context(nc.Block())
        loads = 4

        @block.sync
        def _(sp):
            sp.dma_start(t.x[:, 0:2 * GT], d["x"][0:2 * GT].rearrange("b p d -> p b d")).then_inc(t.s_xl, 16)
            sp.dma_start(raw[:, 0:2], row_vector(d["g_xattn"], 2)).then_inc(s_load, 16)
            sp.dma_start(raw[:, 2:4], row_vector(d["g_ffn"], 2)).then_inc(s_load, 16)
            sp.dma_start(bo[:, 0, :], row_vector(d["L0_xattn_b_out"], D)).then_inc(s_load, 16)
            sp.dma_start(bo[:, 1, :], row_vector(d["L1_xattn_bo"], D)).then_inc(s_load, 16)
            sp.wait_ge(s_load, 16 * loads)

        @block.gpsimd
        def _(pool):
            g = nc.gpsimd
            g.memset(t.ident[:], 0.0).then_inc(s_const, 1)
            g.memset(t.tri[:], 1.0).then_inc(s_const, 1)
            g.memset(t.ones_bf[:], 1.0).then_inc(s_const, 1)
            g.memset(t.minus_half[:], -0.5).then_inc(s_const, 1)
            pool.wait_ge(s_const, 4)
            g.affine_select(out=t.ident[:], in_=t.ident[:], compare_op=ALU.not_equal, fill=1.0, base=0,
                            pattern=[[-1, P]], channel_multiplier=1).then_inc(s_const, 1)
            g.affine_select(out=t.tri[:], in_=t.tri[:], compare_op=ALU.is_gt, fill=0.0, base=0,
                            pattern=[[1, P]], channel_multiplier=-1).then_inc(s_const, 1)
            g.iota(t.iota[:], pattern=[[1, E0]], base=0, channel_multiplier=0,
                   allow_small_or_imprecise_dtypes=True).then_inc(s_const, 1)
            pool.wait_ge(s_const, 7)
            g.memset(t.kz[DH:P, :, :, 0], 0.0).then_inc(s_const, 1)
            pool.wait_ge(s_const, 8)

        @block.scalar
        def _(act):
            act.wait_ge(s_load, 16 * loads)
            nc.scalar.activation(t.gate[:], raw[:], ACT.Tanh).then_inc(s_tanh, 1)
            act.wait_ge(s_tanh, 1)

        @block.vector
        def _(v):
            nc.vector.memset(t.kz[0:DH, :, :, 1], 0.0).then_inc(s_v, 1)
            v.wait_ge(s_load, 16 * loads)
            v.wait_ge(s_tanh, 1)
            for i in range(2):
                nc.vector.tensor_scalar(t.bo[:, i, :], bo[:, i, :], t.gate[:, i:i + 1], None, ALU.mult).then_inc(s_v, 1)
            v.wait_ge(s_v, 3)


def attention(nc, t, d, layer):
    L = f"a{layer}_"
    first = layer == 0
    with ExitStack() as stack:
        m = Memory(nc, stack)
        w_hi = {w: m.sb(L + f"w{w}_hi", [P, DC, INNER], F32R) for w in "kvq"}
        w_lo = {w: m.sb(L + f"w{w}_lo", [P, DC, INNER], F32R) for w in "kvq"}
        wo = m.sb(L + "wo", [P, HP, D])
        ctx = m.sb(L + "ctx", [P, GT, D])
        xn = m.sb(L + "xn", [P, GT, D])
        plain = m.sb(L + "plain", [P, DC, TOK])
        x_hi = m.sb(L + "x_hi", [P, DC, TOK], F32R)
        x_lo = m.sb(L + "x_lo", [P, DC, TOK], F32R)
        c_hi = m.sb(L + "c_hi", [P, DC, TOK], F32R)
        c_lo = m.sb(L + "c_lo", [P, DC, TOK], F32R)
        qT = m.sb(L + "qT", [P, 2, HP, TOK])
        kz = t.kz
        v = m.sb(L + "v", [P, 2, GT, INNER])
        raw = {"k": qT[:, 0].rearrange("p h n -> p (h n)"), "v": qT[:, 1].rearrange("p h n -> p (h n)"),
               "q": v[:, 1].rearrange("p t n -> p (t n)")}
        raw = {w: ap.rearrange("p (c n) -> p c n", c=DC) for w, ap in raw.items()}
        S = m.sb(L + "S", [P, 4, HU, P])
        PT = m.sb(L + "PT", [P, 2, HU, P])
        oT = m.sb(L + "oT", [P, HP, P])
        stats = m.sb(L + "stats", [P, GT, 6])
        mv = m.sb(L + "mv", [P, GT, 2])
        var_eps = m.sb(L + "var_eps", [P, GT])
        rstd = m.sb(L + "rstd", [P, GT])
        mn = m.sb(L + "mn", [P, 2, HU])
        z = m.sb(L + "z", [P, 2, HU])
        rz = m.sb(L + "rz", [P, 2, HU])
        psP = [m.ps(L + f"psP{i}", [P, 512]) for i in range(2)]
        psS = [m.ps(L + f"psS{i}", [P, HU, P]) for i in range(2)]
        psT = [m.ps(L + f"psT{i}", [P, HU, P]) for i in range(2)]
        psV = m.ps(L + "psV", [P, 4, P])
        psM = m.ps(L + "psM", [P, 2, TOK])

        s_w = {w: m.sem(L + f"w_{w}_loaded_then_split") for w in "kvq"}
        s_ctx = m.sem(L + "context_loaded")
        s_mv = m.sem(L + "stats_then_moments_ready")
        s_ve = m.sem(L + "variance_shifted")
        s_rstd = m.sem(L + "rstd_ready")
        s_xn = m.sem(L + "normed")
        s_tx = m.sem(L + "x_transposed")
        s_tc = m.sem(L + "context_transposed")
        NS = 3
        s_xT = m.sem(L + "x_transposes_evacuated")
        s_cT = m.sem(L + "context_transposes_evacuated")
        s_pj = m.sem(L + "projected")
        s_ev = [m.sem(L + f"projection_evacuated{i}") for i in range(2)]
        s_sc = m.sem(L + "scores_ready")
        s_read = m.sem(L + "scores_read")
        s_exp = m.sem(L + "exp_ready")
        RZ = 1 if first else 2
        s_rz = m.sem(L + ("sums_inverted" if first else "sums_then_inverse_ready"))
        s_norm = m.sem(L + "probs_normed")
        s_tr = m.sem(L + "probs_transposed")
        s_PT = m.sem(L + "probs_evacuated")
        s_pv = m.sem(L + "values_weighted")
        s_oT = m.sem(L + "heads_evacuated")
        s_wo = m.sem(L + "output_projected")
        s_bo = m.sem(L + "output_bias_added")
        s_x = m.sem(L + "x_updated")
        if not first:
            idx = m.sb(L + "idx", [P, GT * K0], I32)
            rows = m.sb(L + "rows", [P, GT * K0, D])
            s_ix = m.sem(L + "indices_copied")
            s_row = [m.sem(L + f"rows_gathered{i}") for i in range(2)]
            s_acc = m.sem(L + "row_added")
            s_cn = m.sem(L + "context_normed")
            cstats = m.sb(L + "cstats", [P, GT, 6])
            cmv = m.sb(L + "cmv", [P, GT, 2])
            cve = m.sb(L + "cve", [P, GT])
            crs = m.sb(L + "crs", [P, GT])
            s_cmv = m.sem(L + "context_stats_then_moments_ready")
            s_cve = m.sem(L + "context_variance_shifted")
            s_crs = m.sem(L + "context_rstd_ready")
        else:
            zeros = m.sb(L + "zeros", [P, 512])
            s_min = m.sem(L + "min_ready")
            s_zero = [m.sem(L + f"buffer_{i}_cleared") for i in range(2)]
        NR = 1 if first else 2
        E, K, CAP = (E0, K0, CAP0) if first else (E1, K1, CAP1)
        CW = E if first else K * E
        EW = P
        rw = m.sb(L + "rw", [P, DC, EW])
        rxn = m.sb(L + "rxn", [P, 2, GT, D])
        rxT = m.sb(L + "rxT", [P, DC, TOK])
        rstats = m.sb(L + "rstats", [P, GT, 6])
        rmv = m.sb(L + "rmv", [P, GT, 2])
        rve = m.sb(L + "rve", [P, GT])
        rrs = m.sb(L + "rrs", [P, GT])
        rmx = m.sb(L + "rmx", [P, GT])
        pr = m.sb(L + "pr", [P, GT, E])
        rzs = m.sb(L + "rzs", [P, GT])
        rrz = m.sb(L + "rrz", [P, GT])
        top = m.sb(L + "top", [P, GT, 8])
        ids = m.sb(L + "ids", [P, GT, 8], U32)
        idf = m.sb(L + "idf", [P, GT, K])
        oh = m.sb(L + "oh", [P, GT, K, E])
        sel = m.sb(L + "sel", [P, GT, K, E])
        pos = m.sb(L + "pos", [P, GT, K])
        over = m.sb(L + "over", [P, GT, K])
        slot = m.sb(L + "slot", [P, GT, K])
        disp = m.sb(L + "disp", [P, 2, GT, K], I32)
        s_late = m.sem(L + "w_out_and_router_loaded")
        s_rwz = m.sem(L + "router_padded_then_zeros_made")
        s_v = m.sem(L + "routing_chain")
        s_rmv = m.sem(L + "routing_stats_then_moments_ready")
        s_rve = m.sem(L + "routing_variance_shifted")
        s_rrs = m.sem(L + "routing_rstd_ready")
        s_rxn = m.sem(L + "routing_normed")
        s_rtx = m.sem(L + "routing_transposed")
        s_rxT = m.sem(L + "routing_evacuated")
        s_lg = m.sem(L + "logits_ready")
        s_sh = m.sem(L + "logits_shifted")
        s_re = m.sem(L + "routing_exp_ready")
        s_cnt = m.sem(L + "choices_ready")
        s_pos = m.sem(L + "positions_ready")
        s_sel = m.sem(L + "positions_read")
        s_slot = m.sem(L + "slots_ready")
        s_out = [m.sem(L + f"rows_scattered{i}") for i in range(2)]
        buf = d[f"buf{layer}"]
        block = stack.enter_context(nc.Block())

        JOBS = [("k", i) for i in range(4)] + [("v", i) for i in range(4)] + [("q", i) for i in range(4)]
        NJ = len(JOBS)
        OF_STEP = [[0], [1, 2], [3], [4, 5], [6], [7, 8], [9, 10], [11]]
        XT_STEP, CT_STEP = 1, 6
        PEEL = 4

        OUT = GT * K * 16

        def outs(g):
            return g // 2 * OUT if isinstance(g, int) else g[0] * OUT + g[1] // 2 * OUT

        def tiles(ap, g):
            return ap[:, g * GT:(g + 1) * GT] if isinstance(g, int) else ap[:, bass.ds(at(g, GT, 0), GT)]

        def has(g, u, lag):
            return not isinstance(g, int) or 0 <= g * UG + u - lag < NU

        def routed(g, lag):
            return not isinstance(g, int) or 0 <= g - lag < NG

        def has_group(g, n):
            return not isinstance(g, int) or g + n < NG

        def settle(eng):
            eng.sem_inc(t.s_passed, 1)

        def run(eng, step, before):
            before()
            for g in range(PEEL):
                for u in range(UG):
                    step(g, u, g % 2, True, True)
            with eng.Fori(PEEL // 2, NG // 2 - 2) as j:
                for half in range(2):
                    for u in range(UG):
                        step((j, half), u, half, True, True)
            for g in (NG - 4, NG - 3):
                for u in range(UG):
                    step(g, u, g % 2, True, True)
            for u in range(UG):
                step(NG - 2, u, 0, True, False)
            for u in range(UG):
                step(NG - 1, u, 1, False, False)
            for g in (NG, NG + 1):
                for u in range(UG):
                    step(g, u, g % 2, False, False)

        def x_tile(g, i):
            if isinstance(g, int):
                return t.x[:, g * GT + i, :]
            return t.x[:, bass.ds(at(g, GT, i), 1), :].rearrange("p a d -> p (a d)")

        def wait_ctx(eng, g):
            eng.wait_ge(s_ctx, at(g, 16, 16))

        @block.sync
        def _(sp):
            W = {"q": ("L0_xattn_W_q" if first else "L1_xattn_Wq", 0),
                 "k": ("L0_xattn_W_k" if first else "L1_xattn_Wkv", 0),
                 "v": ("L0_xattn_W_v" if first else "L1_xattn_Wkv", 0 if first else INNER)}

            def load_w(kind):
                name, off = W[kind]
                sp.dma_start(raw[kind], d[name][:, off:off + INNER].rearrange("(c p) n -> p c n", p=P)).then_inc(s_w[kind], 16)

            def load_ctx(g):
                if begun(g, 1):
                    sp.wait_ge(s_tc, at(g, 1, 0))
                src = d["ctx_1024"][g * GT:(g + 1) * GT] if isinstance(g, int) else d["ctx_1024"][bass.ds(at(g, GT, 0), GT)]
                sp.dma_start(ctx[:], src.rearrange("b p d -> p b d")).then_inc(s_ctx, 16)

            load_ctx(0)
            load_w("k")
            load_w("v")
            load_w("q")
            load_ctx(1)
            if first:
                sp.dma_start(t.side[:], d["fside_SxS2_0"]).then_inc(t.s_rest, 16)
                for i, name in enumerate(("L1_xattn_ln_l_w", "L1_xattn_ln_l_b", "L1_xattn_ln_c_w", "L1_xattn_ln_c_b")):
                    with nc.allow_non_contiguous_dma("256 numbers, one column each"):
                        sp.dma_start(t.affine[:, i, :], d[name].rearrange("(c p) -> p c", p=P)).then_inc(t.s_rest, 16)
            sp.dma_start(wo[:], d["L0_xattn_W_out" if first else "L1_xattn_Wo"].rearrange("(c p) n -> p c n", p=P)
                         ).then_inc(s_late, 16)
            if first:
                sp.dma_start(t.x[:, 2 * GT:NB], d["x"][2 * GT:NB].rearrange("b p d -> p b d")).then_inc(t.s_rest, 16)
            sp.wait_ge(s_rwz, 1)
            sp.dma_start(rw[:, :, 0:E], d["L0_ffn_router_w" if first else "L1_ffn_Wg"].rearrange("(c p) e -> p c e", p=P)
                         ).then_inc(s_late, 16)
            def clear(n):
                layer, part = divmod(n, 2 * UG)
                dst = d[f"buf{layer}"].rearrange("(p r) d -> p (r d)", p=P).rearrange("p (n z) -> p n z", z=zeros.shape[1])
                per = dst.shape[1] // (2 * UG)
                sp.dma_start(dst[:, part * per:(part + 1) * per], zeros[:].unsqueeze(1).broadcast_to([P, per, zeros.shape[1]])
                             ).then_inc(s_zero[layer], 16)

            load_ctx(2)
            if first:
                sp.wait_ge(s_rwz, 2)
                for g in range(PEEL):
                    for u in range(UG):
                        sp.wait_ge(s_sc, at(g, UG, u + 1))
                        clear(g * UG + u)
                    load_ctx(g + 3)
                for i in range(2):
                    sp.wait_ge(s_zero[i], 16 * 2 * UG)
            for g in range(PEEL + 3 if first else 3, 2 * PEEL):
                load_ctx(g)
            with sp.Fori(PEEL, NG // 2) as j:
                for half in range(2):
                    load_ctx((j, half))

        @block.gpsimd
        def _(pool):
            g_ = nc.gpsimd

            def rstd_of(g, r):
                pool.wait_ge(s_mv, at(g, 2 * NR, 2 * r + 2))
                if r == 0 and begun(g, 1):
                    pool.wait_ge(s_xn, at(g, NR, 0))
                settle(pool)
                g_.tensor_scalar(var_eps[:], mv[:, :, 1], EPS, None, ALU.add).then_inc(s_ve, 1)
                pool.wait_ge(s_ve, at(g, NR, r + 1))
                g_.tensor_tensor(rstd[:], var_eps[:], t.minus_half[:], ALU.pow).then_inc(s_rstd, 1)

            def context_rstd(g):
                pool.wait_ge(s_cmv, at(g, 2, 2))
                if begun(g, 1):
                    pool.wait_ge(s_cn, at(g, GT, 0))
                settle(pool)
                g_.tensor_scalar(cve[:], cmv[:, :, 1], EPS, None, ALU.add).then_inc(s_cve, 1)
                pool.wait_ge(s_cve, at(g, 1, 1))
                g_.tensor_tensor(crs[:], cve[:], t.minus_half[:], ALU.pow).then_inc(s_crs, 1)

            def route_rstd(g):
                pool.wait_ge(s_rmv, at(g, 2, 2))
                if begun(g, 1):
                    pool.wait_ge(s_rxn, at(g, 1, 0))
                settle(pool)
                g_.tensor_scalar(rve[:], rmv[:, :, 1], EPS, None, ALU.add).then_inc(s_rve, 1)
                pool.wait_ge(s_rve, at(g, 1, 1))
                g_.tensor_tensor(rrs[:], rve[:], t.minus_half[:], ALU.pow).then_inc(s_rrs, 1)

            SC = 3 if first else 2

            def scatter(g, par, part):
                if part == 0:
                    pool.wait_ge(s_slot, at(g, 1, 1))
                    if isinstance(g, int) and g == 0 and first:
                        pool.wait_ge(s_zero[0], 16 * 2 * UG)
                    settle(pool)
                for n in range(part * SC, min(part * SC + SC, GT * K)):
                    i, k = n // K, n % K
                    g_.indirect_dma_start(out=buf, out_offset=bass.IndirectOffsetOnAxis(
                        ap=disp[:, par, i, k:k + 1], axis=0), in_=rxn[:, par, i], in_offset=None,
                        bounds_check=buf.shape[0] - 1, oob_is_err=False).then_inc(s_out[par], 16)

            def gather(g, part):
                if part == 0:
                    pool.wait_ge(s_ix, at(g, 1, 1))
                if begun(g, 1):
                    pool.wait_ge(s_acc, at(g, GT * K0, GT * (part + 1) - GT * K0))
                settle(pool)
                for i in range(GT):
                    n = part * GT + i
                    g_.indirect_dma_start(out=rows[:, n, :], out_offset=None, in_=d["y0"],
                                          in_offset=bass.IndirectOffsetOnAxis(ap=idx[:, n:n + 1], axis=0)
                                          ).then_inc(s_row[part // 2], 16)

            def step(g, u, par, proj, prep):
                if has(g, u, 1):
                    pool.wait_ge(s_rz, at(g, RZ * UG, RZ * u))
                    s = S[:, (u - 1) % 4]
                    g_.tensor_tensor(s, s, rz[:, (u - 1) % 2, :].unsqueeze(2).broadcast_to([P, HU, P]), ALU.mult
                                     ).then_inc(s_norm, 1)
                if u == 4 and routed(g, 1):
                    route_rstd(plus(g, -1))
                if u >= 5 and (u - 5) * SC < GT * K and routed(g, 2):
                    scatter(plus(g, -2), par, u - 5)
                if not first:
                    if u >= 6 and has_group(g, 3):
                        gather(plus(g, 3), u - 6)
                    if u < 2 and begun(g, 1) and has_group(g, 2):
                        gather(plus(g, 2), u + 2)
                    if u == 3 and prep:
                        context_rstd(plus(g, 2))
                    if u == 7 and prep:
                        rstd_of(plus(g, 2), 1)
                if u == 6 and prep:
                    rstd_of(plus(g, 2), 0)

            def before():
                g_.memset(rw[:], 0.0).then_inc(s_rwz, 1)
                if first:
                    g_.memset(zeros[:], 0.0).then_inc(s_rwz, 1)
                    rstd_of(0, 0)
                    rstd_of(1, 0)
                    return
                gather(0, 0)
                context_rstd(0)
                for part in range(1, 4):
                    gather(0, part)
                context_rstd(1)
                rstd_of(0, 0)
                rstd_of(0, 1)
                for part in range(4):
                    gather(1, part)
                rstd_of(1, 0)
                rstd_of(1, 1)
                for part in range(4):
                    gather(2, part)

            run(pool, step, before)
            for i in range(2):
                pool.wait_ge(s_out[i], NG // 2 * OUT)

        @block.scalar
        def _(act):
            a = nc.scalar

            def evac_in(g, hi, row, done):
                if first:
                    a.activation(plain[:], psM[:], ACT.Copy).then_inc(done, 1)
                else:
                    for c in range(DC):
                        ins = a.activation(plain[:, c], psM[:, c], ACT.Identity,
                                           bias=t.affine[:, row + 1, c:c + 1], scale=t.affine[:, row, c:c + 1])
                    ins.then_inc(done, 1)
                act.wait_ge(done, at(g, NS, 1))
                a.activation(hi[:], plain[:], ACT.Copy).then_inc(done, 1)

            def evac_x(g):
                act.wait_ge(s_tx, at(g, 1, 1))
                if begun(g, 1):
                    act.wait_ge(s_pj, at(g, NJ, 0))
                act.wait_ge(s_cT, at(g, NS, NS) if begun(g, 1) else 2 * NS)
                evac_in(g, x_hi, 0, s_xT)

            def evac_ctx(g):
                act.wait_ge(s_tc, at(g, 1, 1))
                if begun(g, 1):
                    act.wait_ge(s_pj, at(g, NJ, 8 - NJ))
                if begun(g, 2):
                    act.wait_ge(s_xT, at(g, NS, 0))
                elif g == 1:
                    act.wait_ge(s_cT, NS)
                evac_in(g, c_hi, 2, s_cT)

            def weights_hi(kind):
                act.wait_ge(s_w[kind], 16)
                a.activation(w_hi[kind][:], raw[kind], ACT.Copy).then_inc(s_w[kind], 1)

            def evac_job(g, par, j):
                kind, i = JOBS[j]
                act.wait_ge(s_pj, at(g, NJ, j + 1))
                if begun(g, 2) and j == 0:
                    act.wait_ge(s_sc, at(g, UG, -UG))
                if begun(g, 2) and j == 8:
                    act.wait_ge(s_sc, at(g, UG, -UG))
                if begun(g, 2) and j == 4:
                    act.wait_ge(s_pv, at(g, UG, -UG))
                if kind == "k":
                    src = psP[j % 2][:].rearrange("p (c n) -> p c n", c=2)
                    a.activation(kz[0:DH, par, 2 * i:2 * i + 2, 0], src[0:DH], ACT.Copy)
                    ins = a.activation(kz[DH:P, par, 2 * i:2 * i + 2, 1], src[DH:P], ACT.Copy)
                elif kind == "q":
                    ins = a.activation(qT[:, par, 2 * i:2 * i + 2], psP[j % 2][:].rearrange("p (c n) -> p c n", c=2),
                                       ACT.Copy, scale=-SCALE if first else SCALE)
                else:
                    ins = a.activation(v[:, par, i // 2, (i % 2) * 512:(i % 2) * 512 + 512], psP[j % 2][:], ACT.Copy)
                ins.then_inc(s_ev[j % 2], 1)

            def step(g, u, par, proj, prep):
                if proj:
                    for j in OF_STEP[u]:
                        evac_job(plus(g, 1), 1 - par, j)
                if has(g, u, 0):
                    s = S[:, u % 4]
                    if first:
                        act.wait_ge(s_min, at(g, UG, u + 1))
                        if has(g, u, 2):
                            act.wait_ge(s_rz, at(g, UG, u - 1))
                        for h in range(HU):
                            ins = a.activation(s[:, h], s[:, h], ACT.Exp, bias=mn[:, u % 2, h:h + 1], scale=-1.0,
                                               accum_out=z[:, u % 2, h:h + 1])
                        ins.then_inc(s_exp, 1)
                    else:
                        act.wait_ge(s_read, at(g, UG, u + 1))
                        a.activation(s, s, ACT.Exp).then_inc(s_exp, 1)
                if has(g, u, 2):
                    act.wait_ge(s_tr, at(g, UG, u - 1))
                    if has(g, u, 4):
                        act.wait_ge(s_pv, at(g, UG, u - 3))
                    a.activation(PT[:, u % 2], psT[u % 2][:], ACT.Copy).then_inc(s_PT, 1)
                if u % 2 == 0 and has(g, u, 3):
                    act.wait_ge(s_pv, at(g, UG, u - 2))
                    eight = ((u - 4) // 2) % 4
                    if not isinstance(g, int) or g * UG + u >= 8:
                        act.wait_ge(s_wo, at(g, GT, (u - 4) // 4))
                    a.activation(oT[:, (eight % 2) * 4:(eight % 2) * 4 + 4], psV[:], ACT.Copy).then_inc(s_oT, 1)
                if u == 0 and routed(g, 2):
                    act.wait_ge(s_sh, at(g, 1, -1))
                    a.activation(pr[:], pr[:], ACT.Exp).then_inc(s_re, 1)
                if u == 5 and routed(g, 1):
                    act.wait_ge(s_rtx, at(g, 1, 0))
                    if routed(g, 2):
                        act.wait_ge(s_lg, at(g, 1, -1))
                    a.activation(rxT[:], psM[:], ACT.Copy).then_inc(s_rxT, 1)
                if proj and u == XT_STEP:
                    evac_x(plus(g, 1))
                if prep and u == CT_STEP:
                    evac_ctx(plus(g, 2))

            def before():
                if not first:
                    act.wait_ge(t.s_rest, 16 * 6)
                weights_hi("k")
                evac_ctx(0)
                weights_hi("v")
                for j in range(4):
                    evac_job(0, 0, j)
                weights_hi("q")
                for j in range(4, 8):
                    evac_job(0, 0, j)
                evac_ctx(1)
                evac_x(0)
                for j in range(8, NJ):
                    evac_job(0, 0, j)

            run(act, step, before)

        @block.vector
        def _(ve):
            v_ = nc.vector

            def indices(g):
                if begun(g, 1):
                    for i in range(2):
                        ve.wait_ge(s_row[i], at(g, GT * K0 * 8, 0))
                src = t.comb0[:, g * GT:(g + 1) * GT] if isinstance(g, int) else t.comb0[:, bass.ds(at(g, GT, 0), GT)]
                v_.tensor_copy(idx[:].rearrange("p (k t) -> p t k", k=K0), src).then_inc(s_ix, 1)

            def add_rows(g, k):
                if k % 2 == 0:
                    ve.wait_ge(s_row[k // 2], at(g, GT * K0 * 8, GT * K0 * 8))
                for i in range(GT):
                    pr = (t.prob0[:, g * GT + i, k:k + 1] if isinstance(g, int)
                          else t.prob0[:, bass.ds(at(g, GT, i), 1), k:k + 1].rearrange("p a b -> p (a b)"))
                    if k:
                        ve.wait_ge(s_acc, at(g, GT * K0, (k - 1) * GT + i + 1))
                    v_.scalar_tensor_tensor(out=x_tile(g, i), in0=rows[:, k * GT + i, :], scalar=pr, in1=x_tile(g, i),
                                            op0=ALU.mult, op1=ALU.add).then_inc(s_acc, 1)

            def moments(g, r):
                if r == 0:
                    if begun(g, 1):
                        ve.wait_ge(s_xn, at(g, NR, 0))
                    if first and isinstance(g, int) and g == 0:
                        ve.wait_ge(t.s_xl, 16)
                    if not first:
                        ve.wait_ge(s_acc, at(g, GT * K0, GT * K0))
                else:
                    ve.wait_ge(s_xn, at(g, NR, 1))
                settle(ve)
                for i in range(GT):
                    ins = v_.bn_stats(stats[:, i], xn[:, i] if r else x_tile(g, i))
                ins.then_inc(s_mv, 1)
                ve.wait_ge(s_mv, at(g, 2 * NR, 2 * r + 1))
                settle(ve)
                for i in range(GT):
                    ins = v_.bn_aggr(mv[:, i], stats[:, i])
                ins.then_inc(s_mv, 1)

            def norm(g, r):
                ve.wait_ge(s_rstd, at(g, NR, r + 1))
                ve.wait_ge(s_mv, at(g, 2 * NR, 2 * r + 2))
                if r == 0 and begun(g, 1):
                    ve.wait_ge(s_tx, at(g, 1, 0))
                for i in range(GT):
                    ins = v_.tensor_scalar(xn[:, i], xn[:, i] if r else x_tile(g, i), mv[:, i, 0:1], rstd[:, i:i + 1],
                                           ALU.subtract, ALU.mult)
                ins.then_inc(s_xn, 1)

            def context_moments(g):
                wait_ctx(ve, g)
                if begun(g, 1):
                    ve.wait_ge(s_cn, at(g, GT, 0))
                settle(ve)
                for i in range(GT):
                    ins = v_.bn_stats(cstats[:, i], ctx[:, i])
                ins.then_inc(s_cmv, 1)
                ve.wait_ge(s_cmv, at(g, 2, 1))
                settle(ve)
                for i in range(GT):
                    ins = v_.bn_aggr(cmv[:, i], cstats[:, i])
                ins.then_inc(s_cmv, 1)

            def context_norm(g):
                ve.wait_ge(s_crs, at(g, 1, 1))
                ve.wait_ge(s_cmv, at(g, 2, 2))
                for i in range(GT):
                    v_.tensor_scalar(ctx[:, i], ctx[:, i], cmv[:, i, 0:1], crs[:, i:i + 1],
                                     ALU.subtract, ALU.mult).then_inc(s_cn, 1)

            def split_in(g, hi, lo, done):
                ve.wait_ge(done, at(g, NS, NS - 1))
                v_.tensor_tensor(lo[:], plain[:], hi[:].bitcast(F32), ALU.subtract).then_inc(done, 1)

            def weights_lo(kind):
                ve.wait_ge(s_w[kind], 17)
                v_.tensor_tensor(w_lo[kind][:], raw[kind], w_hi[kind][:].bitcast(F32), ALU.subtract
                                 ).then_inc(s_w[kind], 1)

            links = {"n": 0, "g": 0}
            PER = 13 if first else 12

            def link(ins):
                links["n"] += 1
                ins.then_inc(s_v, 1)
                ve.wait_ge(s_v, at(links["g"], PER, links["n"]))
                settle(ve)

            def route_moments(g):
                ve.wait_ge(s_x, at(g, GT, GT))
                settle(ve)
                for i in range(GT):
                    ins = v_.bn_stats(rstats[:, i], x_tile(g, i))
                ins.then_inc(s_rmv, 1)
                ve.wait_ge(s_rmv, at(g, 2, 1))
                settle(ve)
                for i in range(GT):
                    ins = v_.bn_aggr(rmv[:, i], rstats[:, i])
                ins.then_inc(s_rmv, 1)

            def route_norm(g, par):
                ve.wait_ge(s_rrs, at(g, 1, 1))
                if begun(g, 2):
                    ve.wait_ge(s_out[par], outs(g))
                for i in range(GT):
                    ins = v_.tensor_scalar(rxn[:, par, i], x_tile(g, i), rmv[:, i, 0:1], rrs[:, i:i + 1],
                                           ALU.subtract, ALU.mult)
                ins.then_inc(s_rxn, 1)

            def route_shift(g):
                links.update(n=0, g=g)
                ve.wait_ge(s_lg, at(g, 1, 1))
                link(v_.tensor_reduce(rmx[:], psM[:, :, 0:E], AX, ALU.max))
                v_.tensor_tensor(pr[:], psM[:, :, 0:E], rmx[:].unsqueeze(2).broadcast_to([P, GT, E]), ALU.subtract
                                 ).then_inc(s_sh, 1)

            def route_best(g):
                ve.wait_ge(s_re, at(g, 1, 1))
                settle(ve)
                for i in range(GT):
                    v_.max(top[:, i], pr[:, i])
                link(v_.tensor_reduce(rzs[:], pr[:], AX, ALU.add))
                for i in range(GT):
                    v_.max_index(ids[:, i], top[:, i], pr[:, i])
                link(v_.reciprocal(rrz[:], rzs[:]))

            def route_choose(g):
                if first:
                    v_.tensor_scalar(rrz[:], rrz[:], t.gate[:, 2:3], None, ALU.mult)
                link(v_.tensor_copy(idf[:], ids[:, :, 0:K]))
                v_.tensor_tensor(tiles(t.prob0 if first else t.p1, g), top[:, :, 0:K],
                                 rrz[:].unsqueeze(2).broadcast_to([P, GT, K]), ALU.mult)
                link(v_.tensor_tensor(oh[:].rearrange("p t k e -> p (t k) e"),
                                      t.iota[:, 0:E].unsqueeze(1).broadcast_to([P, GT * K, E]),
                                      idf[:].rearrange("p t k -> p (t k)").unsqueeze(2).broadcast_to([P, GT * K, E]),
                                      ALU.is_equal))
                for i in range(GT):
                    if begun(g, 1):
                        if i == 0:
                            ve.wait_ge(s_pos, at(g, 1, 0))
                        link(v_.tensor_tensor(t.acc[:, 0:CW], t.acc[:, 0:CW], t.cnt[:, i, 0:CW], ALU.add))
                    else:
                        link(v_.memset(t.acc[:, 0:CW], 0.0))
                if first:
                    with nc.allow_low_precision("sums of at most K zeros and ones"):
                        v_.tensor_reduce(t.cnt[:], oh[:].rearrange("p t k e -> p t e k"), AX, ALU.add).then_inc(s_cnt, 1)
                else:
                    v_.tensor_copy(t.cnt[:, :, 0:CW], oh[:].rearrange("p t k e -> p t (k e)")).then_inc(s_cnt, 1)
                    v_.tensor_copy(tiles(t.oh1, g), oh[:, :, 1])
                    v_.tensor_copy(tiles(t.idf1, g), idf[:])

            def route_read(g):
                ve.wait_ge(s_pos, at(g, 1, 1))
                for i in range(GT):
                    if first:
                        ins = v_.tensor_tensor(sel[:, i], oh[:, i], psM[:, i, 0:E].unsqueeze(1).broadcast_to([P, K, E]), ALU.mult)
                    else:
                        ins = v_.tensor_tensor(sel[:, i].rearrange("p k e -> p (k e)"), oh[:, i].rearrange("p k e -> p (k e)"),
                                               psM[:, i, 0:CW], ALU.mult)
                ins.then_inc(s_sel, 1)

            def route_slots(g, par):
                ve.wait_ge(s_sel, at(g, 1, 1))
                link(v_.tensor_reduce(pos[:], sel[:], AX, ALU.add))
                if not first:
                    v_.tensor_copy(tiles(t.pos1, g), pos[:])
                link(v_.tensor_scalar(over[:], pos[:], float(CAP), BIG, ALU.is_ge, ALU.mult))
                link(v_.scalar_tensor_tensor(out=slot[:], in0=idf[:], scalar=float(CAP), in1=pos[:], op0=ALU.mult, op1=ALU.add))
                link(v_.tensor_tensor(over[:], over[:], slot[:], ALU.add))
                if first:
                    v_.tensor_copy(disp[:, par], over[:])
                    link(v_.tensor_scalar(pos[:], pos[:], float(CAP - 1), None, ALU.min))
                    link(v_.scalar_tensor_tensor(out=slot[:], in0=idf[:], scalar=float(CAP), in1=pos[:], op0=ALU.mult, op1=ALU.add))
                    v_.tensor_copy(tiles(t.comb0, g), slot[:]).then_inc(s_slot, 1)
                else:
                    link(v_.tensor_scalar(over[:, :, 1], over[:, :, 1], float(E * CAP), None, ALU.add))
                    v_.tensor_copy(disp[:, par], over[:]).then_inc(s_slot, 1)
                assert links["n"] == PER, links

            def step(g, u, par, proj, prep):
                if u == 0 and proj:
                    norm(plus(g, 1), NR - 1)
                if u == 5 and routed(g, 1):
                    route_norm(plus(g, -1), 1 - par)
                if has(g, u, 1):
                    s = S[:, (u - 1) % 4]
                    ve.wait_ge(s_exp, at(g, UG, u))
                    if not first:
                        v_.tensor_reduce(z[:, (u - 1) % 2], s, AX, ALU.add).then_inc(s_rz, 1)
                        ve.wait_ge(s_rz, at(g, RZ * UG, RZ * u - 1))
                    if has(g, u, 3):
                        ve.wait_ge(s_norm, at(g, UG, u - 2))
                    v_.reciprocal(rz[:, (u - 1) % 2], z[:, (u - 1) % 2]).then_inc(s_rz, 1)
                if has(g, u, 0):
                    s = S[:, u % 4]
                    if has(g, u, 4):
                        ve.wait_ge(s_tr, at(g, UG, u - 3))
                    ve.wait_ge(s_sc, at(g, UG, u + 1))
                    if first:
                        for h in range(HU):
                            head = (u % UT) * HU + h
                            ins = v_.scalar_tensor_tensor(out=s[:, h], in0=t.side[:], scalar=-2.0 ** -(head + 1),
                                                          in1=psS[u % 2][:, h], op0=ALU.mult, op1=ALU.add)
                        ins.then_inc(s_read, 1)
                        if has(g, u, 2):
                            ve.wait_ge(s_exp, at(g, UG, u - 1))
                        ve.wait_ge(s_read, at(g, UG, u + 1))
                        v_.tensor_reduce(mn[:, u % 2], s, AX, ALU.min).then_inc(s_min, 1)
                    else:
                        v_.tensor_scalar(s, psS[u % 2][:], CLIP, -CLIP, ALU.min, ALU.max).then_inc(s_read, 1)
                if proj and u == XT_STEP + 1:
                    split_in(plus(g, 1), x_hi, x_lo, s_xT)
                if prep and u == CT_STEP + 1:
                    split_in(plus(g, 2), c_hi, c_lo, s_cT)
                if u % UT == 3 and has(g, u, 7):
                    i = u // UT - 1
                    x = x_tile(g, i)
                    v_.tensor_tensor(x, x, t.bo[:, layer], ALU.add).then_inc(s_bo, 1)
                    ve.wait_ge(s_bo, at(g, GT, i + 1))
                    ve.wait_ge(s_wo, at(g, GT, i + 1))
                    v_.scalar_tensor_tensor(out=x, in0=psM[:, 0], scalar=t.gate[:, layer:layer + 1], in1=x,
                                            op0=ALU.mult, op1=ALU.add).then_inc(s_x, 1)
                if routed(g, 2):
                    r = plus(g, -2)
                    if u == 0:
                        route_shift(r)
                    if u == 1:
                        route_best(r)
                    if u == 2:
                        route_choose(r)
                    if u == 4:
                        route_read(r)
                        route_slots(r, par)
                if u == 4 and routed(g, 1):
                    route_moments(plus(g, -1))
                if prep:
                    g2 = plus(g, 2)
                    if not first:
                        if u == 2:
                            add_rows(g2, 0)
                            context_moments(g2)
                        if u == 4:
                            add_rows(g2, 1)
                            context_norm(g2)
                        if u == 5:
                            add_rows(g2, 2)
                            add_rows(g2, 3)
                            if has_group(g, 3):
                                indices(plus(g, 3))
                        if u == 7:
                            norm(g2, 0)
                            moments(g2, 1)
                    if u == 6:
                        moments(g2, 0)

            def before():
                def inputs(g):
                    for k in range(K0):
                        add_rows(g, k)
                    indices(g + 1)
                    moments(g, 0)
                    norm(g, 0)
                    moments(g, 1)

                if first:
                    moments(0, 0)
                    weights_lo("k")
                    split_in(0, c_hi, c_lo, s_cT)
                    norm(0, 0)
                    weights_lo("v")
                    moments(1, 0)
                    weights_lo("q")
                    split_in(1, c_hi, c_lo, s_cT)
                    split_in(0, x_hi, x_lo, s_xT)
                    ve.wait_ge(t.s_rest, 16 * 6)
                    return
                indices(0)
                context_moments(0)
                weights_lo("k")
                context_norm(0)
                split_in(0, c_hi, c_lo, s_cT)
                weights_lo("v")
                context_moments(1)
                weights_lo("q")
                context_norm(1)
                inputs(0)
                norm(0, 1)
                split_in(1, c_hi, c_lo, s_cT)
                split_in(0, x_hi, x_lo, s_xT)
                inputs(1)

            run(ve, step, before)

        @block.tensor
        def _(pe):
            mm, tp = nc.tensor.matmul, nc.tensor.transpose

            def transposes(src, done):
                for c in range(DC):
                    for i in range(GT):
                        ins = tp(psM[:, c, i * P:(i + 1) * P], src[:, i, c * P:(c + 1) * P], t.ident[:])
                ins.then_inc(done, 1)

            def transpose_x(g):
                pe.wait_ge(s_xn, at(g, NR, NR))
                if begun(g, 3):
                    pe.wait_ge(s_sh, at(g, 1, -2))
                elif g == 2:
                    pe.wait_ge(s_x, 1)
                else:
                    pe.wait_ge(s_cT, NS + 1)
                if g == 1:
                    pe.wait_ge(s_xT, 1)
                transposes(xn, s_tx)

            def transpose_ctx(g):
                if first:
                    wait_ctx(pe, g)
                else:
                    pe.wait_ge(s_cn, at(g, GT, GT))
                if begun(g, 3):
                    pe.wait_ge(s_rxT, at(g, 1, -2))
                elif g == 2:
                    pe.wait_ge(s_xT, NS + 1)
                elif g == 1:
                    pe.wait_ge(s_cT, 1)
                transposes(ctx, s_tc)

            def project(g, par, j):
                kind, i = JOBS[j]
                if j == 0:
                    pe.wait_ge(s_cT, at(g, NS, NS))
                if j == 8:
                    pe.wait_ge(s_xT, at(g, NS, NS))
                if i == 0 and isinstance(g, int) and g == 0:
                    pe.wait_ge(s_w[kind], 18)
                if begun(g, 1) or j >= 2:
                    pe.wait_ge(s_ev[j % 2], at(g, NJ // 2, j // 2))
                bank = psP[j % 2]
                if kind == "v":
                    tile, half = i // 2, i % 2
                    for c in range(DC):
                        rows_, cols = slice(tile * P, (tile + 1) * P), slice(half * 512, half * 512 + 512)
                        ins = split_product(nc.tensor, bank[:], c_hi[:, c, rows_], c_lo[:, c, rows_],
                                            w_hi["v"][:, c, cols], w_lo["v"][:, c, cols], c == 0, c == DC - 1)
                else:
                    hi, lo = (x_hi, x_lo) if kind == "q" else (c_hi, c_lo)
                    for b in range(2):
                        for c in range(DC):
                            cols = slice((2 * i + b) * P, (2 * i + b + 1) * P)
                            ins = split_product(nc.tensor, bank[:, b * TOK:(b + 1) * TOK], w_hi[kind][:, c, cols],
                                                w_lo[kind][:, c, cols], hi[:, c], lo[:, c], c == 0, c == DC - 1)
                ins.then_inc(s_pj, 1)

            def step(g, u, par, proj, prep):
                if has(g, u, 0):
                    if u == 0:
                        for i in range(2):
                            pe.wait_ge(s_ev[i], at(g, NJ // 2, NJ // 2))
                    if has(g, u, 2):
                        pe.wait_ge(s_read, at(g, UG, u - 1))
                    tile = u // UT
                    for i in range(2):
                        pair = (u % UT) * 2 + i
                        ins = mm(psS[u % 2][:, 2 * i:2 * i + 2], qT[:, par, pair, tile * P:(tile + 1) * P],
                                 kz[:, par, pair, :, tile * P:(tile + 1) * P], start=True, stop=True)
                    ins.then_inc(s_sc, 1)
                if proj:
                    for j in OF_STEP[u]:
                        project(plus(g, 1), 1 - par, j)
                if u == 4 and routed(g, 2):
                    count(plus(g, -2))
                if has(g, u, 2):
                    pe.wait_ge(s_norm, at(g, UG, u - 1))
                    if has(g, u, 4):
                        pe.wait_ge(s_PT, at(g, UG, u - 3))
                    for h in range(HU):
                        ins = tp(psT[u % 2][:, h], S[:, (u - 2) % 4, h], t.ident[:])
                    ins.then_inc(s_tr, 1)
                if has(g, u, 3):
                    pe.wait_ge(s_PT, at(g, UG, u - 2))
                    un = (u - 3) % UG
                    vpar = par if u >= 3 else 1 - par
                    if un % 2 == 0 and has(g, u, 5):
                        pe.wait_ge(s_oT, at(g, UG // 2, (u - 3) // 2))
                    tile = un // UT
                    for h in range(HU):
                        head = (un % UT) * HU + h
                        row = (h % 2) * DH
                        ins = mm(psV[row:row + DH, (un % 2) * 2 + h // 2], v[:, vpar, tile, head * DH:(head + 1) * DH],
                                 PT[:, (u - 3) % 2, h], start=True, stop=True)
                    ins.then_inc(s_pv, 1)
                if u % UT == 3 and has(g, u, 7):
                    i = u // UT - 1
                    pe.wait_ge(s_oT, at(g, UG // 2, 4 * i // 2 + 2))
                    if begun(g, 1) or i > 0:
                        pe.wait_ge(s_x, at(g, GT, i))
                    if u == 7 and prep:
                        pe.wait_ge(s_cT, at(g, NS, 2 * NS + 1))
                    elif u == 7:
                        pe.wait_ge(s_rxT, at(g, 1, 0))
                    if u == 3 and proj:
                        pe.wait_ge(s_xT, at(g, NS, NS + 1))
                    elif u == 3:
                        pe.wait_ge(s_sh, at(g, 1, -1))
                    if isinstance(g, int) and g == 0:
                        pe.wait_ge(s_late, 32)
                    for c in range(HP):
                        ins = mm(psM[:, 0], oT[:, c], wo[:, c], start=c == 0, stop=c == HP - 1)
                    ins.then_inc(s_wo, 1)
                if u == 0 and routed(g, 2):
                    logits(plus(g, -2))
                if u == 5 and routed(g, 1):
                    router_inputs(plus(g, -1), 1 - par)
                if proj and u == XT_STEP:
                    transpose_x(plus(g, 1))
                if prep and u == CT_STEP:
                    transpose_ctx(plus(g, 2))

            def router_inputs(g, par):
                pe.wait_ge(s_rxn, at(g, 1, 1))
                pe.wait_ge(s_x, at(g, GT, GT))
                if begun(g, 1):
                    pe.wait_ge(s_sel, at(g, 1, 0))
                transposes(rxn[:, par], s_rtx)

            def logits(g):
                pe.wait_ge(s_rxT, at(g, 1, 1))
                if isinstance(g, int) and g > NG - 3:
                    pe.wait_ge(s_x, min(NB, g * GT + 3))
                else:
                    pe.wait_ge(s_x, at(g, GT, 3))
                for i in range(GT):
                    for c in range(DC):
                        ins = mm(psM[:, i, 0:EW], rxT[:, c, i * P:(i + 1) * P], rw[:, c], start=c == 0, stop=c == DC - 1)
                ins.then_inc(s_lg, 1)

            def count(g):
                pe.wait_ge(s_cnt, at(g, 1, 1))
                pe.wait_ge(s_x, min(NB, g * GT + 2 * GT) if isinstance(g, int) else at(g, GT, 2 * GT))
                for i in range(GT):
                    mm(psM[:, i, 0:CW], t.tri[:], t.cnt[:, i, 0:CW], start=True, stop=False)
                    if i:
                        mm(psM[:, i, 0:CW], t.ones_bf[:], t.cnt[:, 0, 0:CW], start=False, stop=False)
                    ins = mm(psM[:, i, 0:CW], t.ones_bf[:], t.acc[:, 0:CW], start=False, stop=True)
                ins.then_inc(s_pos, 1)

            def before():
                transpose_ctx(0)
                for j in range(8):
                    project(0, 0, j)
                transpose_ctx(1)
                transpose_x(0)
                for j in range(8, NJ):
                    project(0, 0, j)

            run(pe, step, before)


def experts0(nc, t, d):
    L = "e0_"
    E, F, CAP = E0, F0, CAP0
    FC = F // P
    NC = CAP // TOK
    EB = 4
    CB = EB * NC
    RB = 4
    UB = 2
    with ExitStack() as stack:
        m = Memory(nc, stack)
        w_in = m.sb(L + "w_in", [P, EB, DC, 2 * F])
        w_out = m.sb(L + "w_out", [P, EB, FC, D])
        rows = m.sb(L + "rows", [P, RB, GT, D])
        xT = m.sb(L + "xT", [P, UB, DC, TOK])
        act_ = m.sb(L + "act", [P, UB, FC, TOK])
        hT = m.sb(L + "hT", [P, UB, FC, TOK])
        y = m.sb(L + "y", [P, UB, GT, D])
        psX = [m.ps(L + f"psX{i}", [P, DC, TOK]) for i in range(2)]
        psH = [m.ps(L + f"psH{i}", [P, 2, TOK]) for i in range(UB)]
        psY = [m.ps(L + f"psY{i}", [P, GT, D]) for i in range(2)]
        s_w = [m.sem(L + f"weights_loaded{i}") for i in range(EB)]
        s_r = [m.sem(L + f"rows_loaded{i}") for i in range(RB)]
        s_tx = m.sem(L + "transposed")
        s_xT = m.sem(L + "evacuated")
        s_h = m.sem(L + "hidden_ready")
        s_act = m.sem(L + "activated")
        s_hT = m.sem(L + "gated")
        s_y = m.sem(L + "output_ready")
        s_ye = m.sem(L + "output_evacuated")
        s_st = [m.sem(L + f"rows_stored{i}") for i in range(2)]
        block = stack.enter_context(nc.Block())
        buf, yd = d["buf0"], d["y0"]
        win, wout = d["L0_ffn_w1"], d["L0_ffn_w2"]
        NCH = E * NC
        NIT = E // EB

        def each(eng, body):
            body(0, True)
            with eng.Fori(1, NIT) as it:
                body(it, False)

        @block.sync
        def _(sp):
            def weights(it, e):
                ex = it * EB + e
                w1 = win[ex] if isinstance(it, int) else win[bass.ds(ex, 1)].rearrange("o k n -> (o k) n")
                w2 = wout[ex] if isinstance(it, int) else wout[bass.ds(ex, 1)].rearrange("o k n -> (o k) n")
                sp.dma_start(w_in[:, e], w1.rearrange("(c p) n -> p c n", p=P)).then_inc(s_w[e], 16)
                sp.dma_start(w_out[:, e], w2.rearrange("(c p) n -> p c n", p=P)).then_inc(s_w[e], 16)

            def body(it, last):
                for c in range(CB):
                    r0 = it * (CB * TOK) + c * TOK
                    sp.wait_ge(s_ye, it * CB + c + 1)
                    sp.dma_start(yd[bass.ds(r0, TOK) if not last else slice(r0, r0 + TOK)]
                                 .rearrange("(i p) n -> p i n", p=P), y[:, c % 2]).then_inc(s_st[c % 2], 16)
                    if c % NC == NC - 1 and not last:
                        weights(it + 1, c // NC)

            weights(0, 0)
            sp.wait_ge(s_tx, 1)
            for e in range(1, EB):
                weights(0, e)
            with sp.Fori(0, NIT - 1) as it:
                body(it, False)
            body(NIT - 1, True)
            for i in range(2):
                sp.wait_ge(s_st[i], NCH // 2 * 16)

        RPI = CB // RB

        @block.tensor
        def _(pe):
            mm = nc.tensor.matmul

            def val(it, n):
                return it * CB + n

            def transposes(it, c, skip):
                pe.wait_ge(s_r[c % RB], (it * RPI + c // RB + 1) * 16)
                if not skip(2):
                    pe.wait_ge(s_xT, val(it, c - 1))
                for k in range(DC):
                    for i in range(GT):
                        ins = nc.tensor.transpose(psX[c % 2][:, k, i * P:(i + 1) * P], rows[:, c % RB, i, k * P:(k + 1) * P],
                                                  t.ident[:])
                ins.then_inc(s_tx, 1)

            def hidden(it, c, skip):
                e = c // NC
                if c % NC == 0:
                    pe.wait_ge(s_w[e], (it + 1) * 32)
                pe.wait_ge(s_xT, val(it, c + 1))
                for f in range(2 * FC):
                    if f == 0 and not skip(2):
                        pe.wait_ge(s_hT, val(it, c - 1))
                    dst = psH[c % 2][:, f]
                    for k in range(DC):
                        ins = mm(dst, w_in[:, e, k, f * P:(f + 1) * P], xT[:, c % 2, k], start=k == 0, stop=k == DC - 1)
                    if f in (FC - 1, 2 * FC - 1):
                        ins.then_inc(s_h, 1)

            def output(it, c, skip):
                e = c // NC
                pe.wait_ge(s_hT, val(it, c + 1))
                if not skip(2):
                    pe.wait_ge(s_ye, val(it, c - 1))
                for i in range(GT):
                    for f in range(FC):
                        ins = mm(psY[c % 2][:, i], hT[:, c % 2, f, i * P:(i + 1) * P], w_out[:, e, f], start=f == 0, stop=f == FC - 1)
                ins.then_inc(s_y, 1)

            def body(it, fresh):
                for c in range(CB):
                    n = lambda lag, c=c: (lambda back: fresh and c - lag < back)
                    transposes(it, c, n(0))
                    if not fresh or c >= 1:
                        hidden(*((it, c - 1) if c else (it - 1, CB - 1)), n(1))
                    if not fresh or c >= 2:
                        output(*((it, c - 2) if c >= 2 else (it - 1, CB + c - 2)), n(2))
            each(pe, body)
            no = lambda back: False
            output(NIT - 1, CB - 2, no)
            hidden(NIT - 1, CB - 1, no)
            output(NIT - 1, CB - 1, no)

        @block.scalar
        def _(act):
            a = nc.scalar

            def body(it, fresh):
                for c in range(CB):
                    act.wait_ge(s_tx, it * CB + c + 1)
                    if not (fresh and c < 2):
                        act.wait_ge(s_h, it * (2 * CB) + 2 * (c - 1))
                    a.activation(xT[:, c % 2], psX[c % 2][:], ACT.Copy).then_inc(s_xT, 1)
                    if not fresh or c >= 1:
                        activate(it, c - 1, fresh and c <= 2)
            def activate(it, c, fresh2):
                p = c % 2
                act.wait_ge(s_h, it * (2 * CB) + 2 * c + 2)
                if not fresh2:
                    act.wait_ge(s_hT, it * CB + c - 1)
                a.activation(act_[:, p, 0], psH[p][:, 0], ACT.Silu).then_inc(s_act, 1)
            each(act, body)
            activate(NIT, -1, False)

        @block.vector
        def _(ve):
            v_ = nc.vector

            def gate(it, c, fresh2):
                p = c % 2
                ve.wait_ge(s_act, it * CB + c + 1)
                ve.wait_ge(s_h, it * (2 * CB) + 2 * c + 2)
                if not fresh2:
                    ve.wait_ge(s_y, it * CB + c - 1)
                v_.tensor_tensor(hT[:, p, 0], act_[:, p, 0], psH[p][:, 1], ALU.mult).then_inc(s_hT, 1)

            def out(it, c, fresh2):
                ve.wait_ge(s_y, it * CB + c + 1)
                if not fresh2:
                    ve.wait_ge(s_st[c % 2], it * (CB * 8) + (c // 2) * 16)
                v_.tensor_copy(y[:, c % 2], psY[c % 2][:]).then_inc(s_ye, 1)

            def body(it, fresh):
                for c in range(CB):
                    gate(it, c, fresh and c < 2)
                    if not fresh or c >= 1:
                        out(it, c - 1, fresh and c <= 2)
            each(ve, body)
            out(NIT, -1, False)

        @block.gpsimd
        def _(pool):
            g_ = nc.gpsimd

            def body(it, fresh):
                for c in range(CB):
                    if not (fresh and c < RB):
                        pool.wait_ge(s_tx, (c if fresh else it * CB + c) - RB + 1)
                    r0 = c * TOK if fresh else it * (CB * TOK) + c * TOK
                    pool.sem_inc(t.s_passed, 1)
                    g_.dma_start(rows[:, c % RB], buf[bass.ds(r0, TOK) if not fresh else slice(r0, r0 + TOK)]
                                 .rearrange("(i p) n -> p i n", p=P)).then_inc(s_r[c % RB], 16)

            each(pool, body)


def experts1(nc, t, d):
    L = "e1_"
    E, F, CAP = E1, F1, CAP1
    FC = F // P
    NC = CAP // TOK
    NT = CAP // P
    EB = 2
    CB = EB * NC
    RB = 5
    WI, WO = 2 * F, FC * D
    with ExitStack() as stack:
        m = Memory(nc, stack)
        w = m.sb(L + "w", [P, EB, DC * WI + WO])
        w_hi = m.sb(L + "w_hi", [P, EB, DC * WI + WO], F32R)
        w_lo = m.sb(L + "w_lo", [P, EB, DC * WI + WO], F32R)
        rows = m.sb(L + "rows", [P, RB, GT, D])
        x_hi = m.sb(L + "x_hi", [P, 2, DC, TOK], F32R)
        x_lo = m.sb(L + "x_lo", [P, 2, DC, TOK], F32R)
        h = m.sb(L + "h", [P, 2, FC, TOK])
        h_hi = m.sb(L + "h_hi", [P, 2, FC, TOK], F32R)
        h_lo = m.sb(L + "h_lo", [P, 2, FC, TOK], F32R)
        y = m.sb(L + "y", [P, 2, GT, D])
        local = m.sb(L + "local", [P, E, NT])
        glob = m.sb(L + "glob", [P, E, NT])
        total = m.sb(L + "total", [P, K1, E])
        back = m.sb(L + "back", [P, E])
        second = m.sb(L + "second", [P, E, NT])
        source = m.sb(L + "source", [P, E, NT])
        source_row = m.sb(L + "source_row", [P, E * NT], I32)
        cur = m.sb(L + "cur", [P, RB, GT], I32)
        add1 = m.sb(L + "add1", [P, NB])
        gate_ = m.sb(L + "gates", [P, NB, K1])
        den = m.sb(L + "den", [P, NB])
        psX = [m.ps(L + f"psX{i}", [P, DC, TOK]) for i in range(2)]
        psH = [m.ps(L + f"psH{i}", [P, 2, TOK]) for i in range(4)]
        psY = [m.ps(L + f"psY{i}", [P, GT, D]) for i in range(2)]
        totals = psY[0][:, 0, 0:K1 * E]
        s_grid = m.sem(L + "slot_numbers_ready")
        s_tot = m.sem(L + "totals_ready")
        s_chain = m.sem(L + "vector_chain")
        s_src = m.sem(L + "sources_ready")
        s_cur = m.sem(L + "chunk_sources_copied")
        s_w = [m.sem(L + f"weights_loaded{i}") for i in range(EB)]
        s_whi = m.sem(L + "weights_hi_ready")
        s_wlo = m.sem(L + "weights_lo_ready")
        s_r = [m.sem(L + f"rows_loaded{i}") for i in range(RB)]
        s_tx = m.sem(L + "transposed")
        s_xhi = m.sem(L + "x_hi_ready")
        s_xlo = m.sem(L + "x_lo_ready")
        s_h = m.sem(L + "hidden_ready")
        s_act = m.sem(L + "activated")
        s_gated = m.sem(L + "gated")
        s_hhi = m.sem(L + "h_hi_ready")
        s_hlo = m.sem(L + "h_lo_ready")
        s_y = m.sem(L + "output_ready")
        s_ye = m.sem(L + "output_evacuated")
        s_st = [m.sem(L + f"rows_stored{i}") for i in range(2)]
        block = stack.enter_context(nc.Block())
        buf, yd = d["buf1"], d["y1"]
        win, wout = d["L1_ffn_W_in"], d["L1_ffn_W_out"]
        NCH = E * NC
        NIT = E // EB

        def each(eng, body):
            body(0, True)
            with eng.Fori(1, NIT - 1) as it:
                body(it, False)
            body(NIT - 1, False)

        THIRDS = [slice(0, WI), slice(WI, 2 * WI), slice(2 * WI, 2 * WI + WO)]
        assert DC == 2 and NC > 3

        def third_of(c):
            return ((c // NC + 1) % EB, c % NC - 1) if 1 <= c % NC <= 3 else None

        def made(it, c):
            return it * (3 * EB) + 3 * (c // NC + 1) + (c % NC - 1)

        @block.sync
        def _(sp):
            def weights(it, e):
                ex = it * EB + e
                w1 = win[ex] if isinstance(it, int) else win[bass.ds(ex, 1)].rearrange("o k n -> (o k) n")
                w2 = wout[ex] if isinstance(it, int) else wout[bass.ds(ex, 1)].rearrange("o k n -> (o k) n")
                sp.dma_start(w[:, e, 0:DC * WI].rearrange("p (c n) -> p c n", c=DC),
                             w1.rearrange("(c p) n -> p c n", p=P)).then_inc(s_w[e], 16)
                sp.dma_start(w[:, e, DC * WI:DC * WI + WO].rearrange("p (c n) -> p c n", c=FC),
                             w2.rearrange("(c p) n -> p c n", p=P)).then_inc(s_w[e], 16)

            def body(it, last):
                for c in range(CB):
                    if c % NC == 0 and not last:
                        sp.wait_ge(s_wlo, it * (3 * EB) + 3 * (c // NC + 1))
                        weights(it + 1, c // NC)
                    r0 = it * (CB * TOK) + c * TOK
                    sp.wait_ge(s_ye, it * CB + c + 1)
                    sp.dma_start(yd[bass.ds(r0, TOK) if not last else slice(r0, r0 + TOK)]
                                 .rearrange("(i p) n -> p i n", p=P), y[:, c % 2]).then_inc(s_st[c % 2], 16)

            weights(0, 0)
            sp.wait_ge(s_tx, 1)
            for e in range(1, EB):
                weights(0, e)
            with sp.Fori(0, NIT - 1) as it:
                body(it, False)
            body(NIT - 1, True)
            for i in range(2):
                sp.wait_ge(s_st[i], NCH // 2 * 16)

        RPI = CB // RB

        @block.tensor
        def _(pe):
            mm = nc.tensor.matmul

            def val(it, n):
                return it * CB + n

            def transposes(it, c, skip):
                pe.wait_ge(s_r[c % RB], (it * RPI + c // RB + 1) * (16 * GT))
                if not skip(2):
                    pe.wait_ge(s_xlo, val(it, c - 1))
                for k in range(DC):
                    for i in range(GT):
                        ins = nc.tensor.transpose(psX[c % 2][:, k, i * P:(i + 1) * P], rows[:, c % RB, i, k * P:(k + 1) * P],
                                                  t.ident[:])
                ins.then_inc(s_tx, 1)

            def hidden(it, c, skip):
                e = c // NC
                if c % NC == 0:
                    pe.wait_ge(s_wlo, it * (3 * EB) + 3 * (e + 1))
                pe.wait_ge(s_xlo, val(it, c + 1))
                for f in range(2 * FC):
                    if f == 0 and not skip(1):
                        pe.wait_ge(s_act, val(it, c))
                    if f == FC and not skip(1):
                        pe.wait_ge(s_gated, val(it, c))
                    for k in range(DC):
                        cols = slice(k * WI + f * P, k * WI + (f + 1) * P)
                        ins = split_product(nc.tensor, psH[f // 2][:, f % 2], w_hi[:, e, cols], w_lo[:, e, cols],
                                      x_hi[:, c % 2, k], x_lo[:, c % 2, k], k == 0, k == DC - 1)
                    if f in (FC - 1, 2 * FC - 1):
                        ins.then_inc(s_h, 1)

            def output(it, c, skip):
                e = c // NC
                pe.wait_ge(s_hlo, val(it, c + 1))
                if not skip(2):
                    pe.wait_ge(s_ye, val(it, c - 1))
                for i in range(GT):
                    for f in range(FC):
                        rows_ = slice(i * P, (i + 1) * P)
                        cols = slice(DC * WI + f * D, DC * WI + (f + 1) * D)
                        ins = split_product(nc.tensor, psY[c % 2][:, i], h_hi[:, c % 2, f, rows_], h_lo[:, c % 2, f, rows_],
                                      w_hi[:, e, cols], w_lo[:, e, cols], f == 0, f == FC - 1)
                ins.then_inc(s_y, 1)

            def body(it, fresh):
                for c in range(CB):
                    n = lambda lag, c=c: (lambda back: fresh and c - lag < back)
                    transposes(it, c, n(0))
                    if not fresh or c >= 1:
                        hidden(*((it, c - 1) if c else (it - 1, CB - 1)), n(1))
                    if not fresh or c >= 2:
                        output(*((it, c - 2) if c >= 2 else (it - 1, CB + c - 2)), n(2))

            mm(totals, t.ones_bf[:], t.acc[:, 0:K1 * E], start=True, stop=False)
            for i in range(GT):
                ins = mm(totals, t.ones_bf[:], t.cnt[:, i, 0:K1 * E], start=False, stop=i == GT - 1)
            ins.then_inc(s_tot, 1)
            each(pe, body)
            no = lambda back: False
            hidden(NIT - 1, CB - 1, no)
            output(NIT - 1, CB - 2, no)
            output(NIT - 1, CB - 1, no)

        @block.scalar
        def _(act):
            a = nc.scalar

            def activate(it, c, fresh2):
                p = c % 2
                act.wait_ge(s_h, it * (2 * CB) + 2 * c + 1)
                if not fresh2:
                    act.wait_ge(s_hlo, it * CB + c - 1)
                for b in range(2):
                    ins = a.activation(h[:, p, 2 * b:2 * b + 2], psH[b][:], ACT.Gelu)
                ins.then_inc(s_act, 1)
                act.wait_ge(s_gated, it * CB + c + 1)
                if not fresh2:
                    act.wait_ge(s_y, it * CB + c - 1)
                a.activation(h_hi[:, p], h[:, p], ACT.Copy).then_inc(s_hhi, 1)

            def weights_hi(e, part):
                a.activation(w_hi[:, e, THIRDS[part]], w[:, e, THIRDS[part]], ACT.Copy).then_inc(s_whi, 1)

            def body(it, fresh):
                for c in range(CB):
                    act.wait_ge(s_tx, it * CB + c + 1)
                    if not (fresh and c < 2):
                        act.wait_ge(s_h, it * (2 * CB) + 2 * (c - 1))
                    a.activation(x_hi[:, c % 2], psX[c % 2][:], ACT.Copy).then_inc(s_xhi, 1)
                    if not fresh or c >= 1:
                        activate(it, c - 1, fresh and c <= 2)
                    if third_of(c) and not (isinstance(it, int) and it == NIT - 1 and c >= NC):
                        e, part = third_of(c)
                        nxt = c // NC + 1
                        if part == 0:
                            act.wait_ge(s_w[e], (it + nxt // EB) * 32 + 32)
                        if not fresh or nxt == EB:
                            act.wait_ge(s_y, it * CB + (nxt - EB) * NC + NC)
                        weights_hi(e, part)

            act.wait_ge(s_w[0], 32)
            for part in range(3):
                weights_hi(0, part)
            each(act, body)
            activate(NIT, -1, False)

        @block.vector
        def _(ve):
            v_ = nc.vector

            def split_x(it, c):
                ve.wait_ge(s_xhi, it * CB + c + 1)
                v_.tensor_tensor(x_lo[:, c % 2], psX[c % 2][:], x_hi[:, c % 2].bitcast(F32), ALU.subtract
                                 ).then_inc(s_xlo, 1)

            def gate(it, c):
                p = c % 2
                ve.wait_ge(s_act, it * CB + c + 1)
                ve.wait_ge(s_h, it * (2 * CB) + 2 * c + 2)
                for b in range(2):
                    ins = v_.tensor_tensor(h[:, p, 2 * b:2 * b + 2], h[:, p, 2 * b:2 * b + 2], psH[2 + b][:], ALU.mult)
                ins.then_inc(s_gated, 1)
                ve.wait_ge(s_hhi, it * CB + c + 1)
                v_.tensor_tensor(h_lo[:, p], h[:, p], h_hi[:, p].bitcast(F32), ALU.subtract).then_inc(s_hlo, 1)

            def out(it, c, fresh2):
                ve.wait_ge(s_y, it * CB + c + 1)
                if not fresh2:
                    ve.wait_ge(s_st[c % 2], it * (CB * 8) + (c // 2) * 16)
                v_.tensor_copy(y[:, c % 2], psY[c % 2][:]).then_inc(s_ye, 1)

            def weights_lo(e, part):
                v_.tensor_tensor(w_lo[:, e, THIRDS[part]], w[:, e, THIRDS[part]], w_hi[:, e, THIRDS[part]].bitcast(F32),
                                 ALU.subtract).then_inc(s_wlo, 1)

            def body(it, fresh):
                for c in range(CB):
                    split_x(it, c)
                    if not fresh or c >= 1:
                        gate(it, c - 1)
                    if third_of(c) and not (isinstance(it, int) and it == NIT - 1 and c >= NC):
                        e, part = third_of(c)
                        ve.wait_ge(s_whi, made(it, c) + 1)
                        weights_lo(e, part)
                    if not fresh or c >= 2:
                        out(it, c - 2, fresh and c <= 3)

            n = [0]

            def link(ins):
                n[0] += 1
                ins.then_inc(s_chain, 1)
                ve.wait_ge(s_chain, n[0])

            def sources():
                ve.wait_ge(s_tot, 1)
                ve.wait_ge(s_grid, 2)
                link(v_.tensor_copy(total[:].rearrange("p k e -> p (k e)"), totals))
                tot1 = total[:, 0].unsqueeze(2).broadcast_to([P, E, NT])
                tot = total[:, 1].unsqueeze(2).broadcast_to([P, E, NT])
                v_.tensor_scalar(back[:], total[:, 0], -1.0, float(E * CAP), ALU.mult, ALU.add)
                link(v_.tensor_tensor(total[:, 1], total[:, 0], total[:, 1], ALU.add))
                v_.tensor_tensor(second[:], local[:], tot1, ALU.is_ge)
                link(v_.tensor_tensor(source[:], local[:], tot, ALU.is_lt))
                link(v_.tensor_tensor(second[:], second[:], source[:], ALU.mult))
                link(v_.tensor_tensor(second[:], second[:], back[:].unsqueeze(2).broadcast_to([P, E, NT]), ALU.mult))
                link(v_.tensor_tensor(source[:], glob[:], second[:], ALU.add))
                v_.tensor_copy(source_row[:], source[:].rearrange("p e n -> p (e n)")).then_inc(s_src, 1)

            def gates():
                link(v_.tensor_tensor(t.oh1[:], t.oh1[:], total[:, 0].unsqueeze(1).broadcast_to([P, NB, E]), ALU.mult))
                link(v_.tensor_reduce(add1[:], t.oh1[:], AX, ALU.add))
                link(v_.tensor_tensor(t.pos1[:, :, 1], t.pos1[:, :, 1], add1[:], ALU.add))
                link(v_.tensor_scalar(gate_[:], t.pos1[:], float(CAP), None, ALU.is_lt))
                link(v_.tensor_tensor(gate_[:], gate_[:], t.p1[:], ALU.mult))
                link(v_.tensor_tensor(den[:], gate_[:, :, 0], gate_[:, :, 1], ALU.add))
                link(v_.tensor_scalar(den[:], den[:], 1e-9, None, ALU.max))
                link(v_.reciprocal(den[:], den[:]))
                link(v_.tensor_tensor(gate_[:], gate_[:], den[:].unsqueeze(2).broadcast_to([P, NB, K1]), ALU.mult))
                v_.tensor_scalar(t.prob1[:], gate_[:], t.gate[:, 3:4], None, ALU.mult)
                link(v_.tensor_scalar(t.pos1[:], t.pos1[:], float(CAP - 1), None, ALU.min))
                link(v_.scalar_tensor_tensor(out=gate_[:], in0=t.idf1[:], scalar=float(CAP), in1=t.pos1[:],
                                             op0=ALU.mult, op1=ALU.add))
                v_.tensor_copy(t.comb1[:], gate_[:])

            sources()
            gates()
            for part in range(3):
                ve.wait_ge(s_whi, part + 1)
                weights_lo(0, part)
            each(ve, body)
            gate(NIT, -1)
            out(NIT, -2, False)
            out(NIT, -1, False)

        @block.gpsimd
        def _(pool):
            g_ = nc.gpsimd

            def body(it, fresh):
                for c in range(CB):
                    b, n0 = c % RB, c * GT
                    if not (fresh and c < RB):
                        pool.wait_ge(s_tx, (c if fresh else it * CB + c) - RB + 1)
                    src = source_row[:, n0:n0 + GT] if fresh else source_row[:, bass.ds(it * (CB * GT) + n0, GT)]
                    pool.sem_inc(t.s_passed, 1)
                    g_.tensor_copy(cur[:, b], src).then_inc(s_cur, 1)
                    pool.wait_ge(s_cur, it * CB + c + 1)
                    pool.sem_inc(t.s_passed, 1)
                    for i in range(GT):
                        g_.indirect_dma_start(out=rows[:, b, i, :], out_offset=None, in_=buf,
                                              in_offset=bass.IndirectOffsetOnAxis(ap=cur[:, b, i:i + 1], axis=0)
                                              ).then_inc(s_r[b], 16)

            g_.iota(local[:], pattern=[[0, E], [P, NT]], base=0, channel_multiplier=1,
                    allow_small_or_imprecise_dtypes=True).then_inc(s_grid, 1)
            g_.iota(glob[:], pattern=[[CAP, E], [P, NT]], base=0, channel_multiplier=1,
                    allow_small_or_imprecise_dtypes=True).then_inc(s_grid, 1)
            pool.wait_ge(s_src, 1)
            each(pool, body)


def combine(nc, t, d):
    with ExitStack() as stack:
        m = Memory(nc, stack)
        rows = m.sb("c_rows", [P, 2, GT * K1, D])
        s_row = [m.sem(f"c_rows_gathered{i}") for i in range(2)]
        s_acc = m.sem("c_row_added")
        s_out = m.sem("c_stored")
        block = stack.enter_context(nc.Block())

        @block.gpsimd
        def _(pool):
            for g in range(NG):
                if g >= 2:
                    pool.wait_ge(s_acc, GT * K1 * (g - 1))
                for n in range(GT * K1):
                    k, i = n // GT, n % GT
                    nc.gpsimd.indirect_dma_start(out=rows[:, g % 2, n], out_offset=None, in_=d["y1"],
                                                 in_offset=bass.IndirectOffsetOnAxis(
                                                     ap=t.comb1[:, g * GT + i, k:k + 1], axis=0)).then_inc(s_row[g % 2], 16)

        @block.vector
        def _(ve):
            for g in range(NG):
                ve.wait_ge(s_row[g % 2], 16 * GT * K1 * (g // 2 + 1))
                for n in range(GT * K1):
                    k, i = n // GT, n % GT
                    x = t.x[:, g * GT + i]
                    if k:
                        ve.wait_ge(s_acc, GT * K1 * g + i + 1)
                    nc.vector.scalar_tensor_tensor(out=x, in0=rows[:, g % 2, n], scalar=t.prob1[:, g * GT + i, k:k + 1],
                                                   in1=x, op0=ALU.mult, op1=ALU.add).then_inc(s_acc, 1)

        @block.sync
        def _(sp):
            for g in range(NG):
                sp.wait_ge(s_acc, GT * K1 * (g + 1))
                sp.dma_start(d["out"][g * GT:(g + 1) * GT].rearrange("b p d -> p b d"), t.x[:, g * GT:(g + 1) * GT]
                             ).then_inc(s_out, 16)
            sp.wait_ge(s_out, 16 * NG)


class Resident:
    pass


def program(nc, d):
    with ExitStack() as stack:
        m = Memory(nc, stack)
        t = Resident()
        t.x = m.sb("x_all", [P, NB, D])
        t.ident = m.sb("ident", [P, P])
        t.tri = m.sb("tri", [P, P], BF16)
        t.ones_bf = m.sb("ones_bf", [P, P], BF16)
        t.iota = m.sb("iota", [P, E0])
        t.minus_half = m.sb("minus_half", [P, GT])
        t.gate = m.sb("gate", [P, 4])
        t.affine = m.sb("affine", [P, 4, DC])
        t.side = m.sb("side", [P, P])
        t.bo = m.sb("bo", [P, 2, D])
        t.acc = m.sb("acc", [P, E0], BF16)
        t.cnt = m.sb("cnt", [P, GT, E0], BF16)
        t.oh1 = m.sb("oh1", [P, NB, E1])
        t.idf1 = m.sb("idf1", [P, NB, K1])
        t.p1 = m.sb("p1", [P, NB, K1])
        t.pos1 = m.sb("pos1", [P, NB, K1])
        t.comb0 = m.sb("comb0", [P, NB, K0], I32)
        t.prob0 = m.sb("prob0", [P, NB, K0])
        t.comb1 = m.sb("comb1", [P, NB, K1], I32)
        t.prob1 = m.sb("prob1", [P, NB, K1])
        t.kz = m.sb("kz", [P, 2, HP, 2, TOK])
        t.s_xl = m.sem("first_x_loaded")
        t.s_rest = m.sem("side_affine_and_x_loaded")
        t.s_passed = m.sem("waits_passed")
        for layer, n, rows in ((0, E0 * CAP0, ROWS0), (1, E1 * CAP1, ROWS1)):
            d[f"buf{layer}"] = nc.dram_tensor(f"buf{layer}", [rows, D], F32).ap()
            d[f"y{layer}"] = nc.dram_tensor(f"y{layer}", [n, D], F32).ap()
        for phase in PHASES:
            if phase == "setup":
                setup(nc, t, d)
            elif phase == "combine":
                combine(nc, t, d)
            else:
                {"attention0": lambda: attention(nc, t, d, 0), "attention1": lambda: attention(nc, t, d, 1),
                 "experts0": lambda: experts0(nc, t, d), "experts1": lambda: experts1(nc, t, d)}[phase]()


PHASES = ("setup", "attention0", "experts0", "attention1", "experts1", "combine")

_INS = ["x", "ctx_1024", "fside_SxS2_0", "g_xattn", "g_ffn", "L0_xattn_W_q", "L0_xattn_W_k", "L0_xattn_W_v",
        "L0_xattn_W_out", "L0_xattn_b_out", "L0_ffn_router_w", "L0_ffn_w1", "L0_ffn_w2", "L1_xattn_ln_l_w",
        "L1_xattn_ln_l_b", "L1_xattn_ln_c_w", "L1_xattn_ln_c_b", "L1_xattn_Wq", "L1_xattn_Wkv", "L1_xattn_Wo",
        "L1_xattn_bo", "L1_ffn_Wg", "L1_ffn_W_in", "L1_ffn_W_out"]


def kernel(**inputs):
    import numpy as np
    import concourse.bacc as bacc
    from concourse.bass_utils import run_bass_kernel_spmd

    nc = bacc.Bacc("TRN2", target_bir_lowering=False, num_devices=1)
    arrays, d = {}, {}
    for name in _INS:
        a = np.ascontiguousarray(inputs[name])
        arrays[f"in_{name}"] = a
        d[name] = nc.dram_tensor(f"in_{name}", a.shape, mybir.dt.from_np(a.dtype), kind="ExternalInput").ap()
    d["out"] = nc.dram_tensor("out_x", (NB, P, D), F32, kind="ExternalOutput").ap()
    program(nc, d)
    result = run_bass_kernel_spmd(nc, [arrays], core_ids=[0])
    return result.results[0]["out_x"]
```
